# Optimizing a Trainium2 kernel written in Bass

```python
import numpy as np
import jax
import jax.numpy as jnp

def _softmax(x, axis=-1):
    return jax.nn.softmax(x, axis=axis)

def _gelu(x):
    return jax.nn.gelu(x, approximate=True)

def _silu(x):
    return jax.nn.silu(x)

def _sigmoid(x):
    return jax.nn.sigmoid(x)

def _layernorm(x, axis=-1, eps=1e-05):
    m = jnp.mean(x, axis=axis, keepdims=True)
    v = jnp.var(x, axis=axis, keepdims=True)
    return (x - m) / jnp.sqrt(v + eps)

def _scatter_add(tgt, idx, src, axis=0):
    return tgt.at[idx].add(src)

def _segment_sum(src, seg, n):
    return jax.ops.segment_sum(src, seg, n)
kernel_name = 'mk_audio_tower_d2_tok_audfeat2048_r4_8ef179'

def setup_inputs(seed: int=0):
    np.random.seed(seed)
    _w = jnp.asarray

    def _rec_inputs():
        import jax
        import jax.numpy as jnp
        _rk = jax.random.key(seed)
        x = 0.000343403 + 1.00016 * jax.random.normal(jax.random.fold_in(_rk, 1), (128, 96, 512), jnp.float32)
        return x
    x = _rec_inputs()

    def _L0_tok_setup():
        import jax, jax.numpy as jnp
        import numpy as np
        N, C, T = (32, 128, 512)
        key = jax.random.key(seed)
        qkv = jax.random.normal(key, (N, 3 * C, T), dtype=jnp.float32)
        return {'qkv': qkv}
    _L0_tok_all = _L0_tok_setup()
    _L0_tok_in = {k: v for k, v in _L0_tok_all.items() if k in ()}
    del _L0_tok_all

    def _L0_attn_setup():
        import jax, jax.numpy as jnp
        import numpy as np
        D_MODEL = 512
        N_HEADS = 32
        N_KV_HEADS = 8
        HEAD_DIM = D_MODEL // N_HEADS
        N_REP = N_HEADS // N_KV_HEADS
        SCALE = HEAD_DIM ** (-0.5)

        def _rope_tables(seq_len):
            inv_freq = 1.0 / 10000.0 ** (jnp.arange(0, HEAD_DIM, 2, dtype=jnp.float32) / HEAD_DIM)
            t = jnp.arange(seq_len, dtype=jnp.float32)
            freqs = jnp.outer(t, inv_freq)
            return (jnp.cos(freqs), jnp.sin(freqs))

        def _apply_rope(x, cos, sin):
            x_r, x_i = (x[..., ::2], x[..., 1::2])
            out_r = x_r * cos - x_i * sin
            out_i = x_r * sin + x_i * cos
            out = jnp.stack([out_r, out_i], axis=-1)
            return out.reshape(x.shape)
        key = jax.random.key(seed)
        ks = jax.random.split(key, 5)
        bs, seq_len = (2, 512)
        std = D_MODEL ** (-0.5)
        x = jax.random.normal(ks[0], (bs, seq_len, D_MODEL), dtype=jnp.float32)
        wq = jax.random.normal(ks[1], (N_HEADS * HEAD_DIM, D_MODEL), dtype=jnp.float32) * std
        wk = jax.random.normal(ks[2], (N_KV_HEADS * HEAD_DIM, D_MODEL), dtype=jnp.float32) * std
        wv = jax.random.normal(ks[3], (N_KV_HEADS * HEAD_DIM, D_MODEL), dtype=jnp.float32) * std
        wo = jax.random.normal(ks[4], (D_MODEL, N_HEADS * HEAD_DIM), dtype=jnp.float32) * std
        return {'x': x, 'wq': wq, 'wk': wk, 'wv': wv, 'wo': wo}
    _L0_attn_all = _L0_attn_setup()
    _L0_attn_in = {k: v for k, v in _L0_attn_all.items() if k in ('wq', 'wk', 'wv', 'wo')}
    del _L0_attn_all

    def _L0_ffn_setup():
        import jax, jax.numpy as jnp
        import numpy as np
        D_MODEL = 512
        HIDDEN = int(2 * D_MODEL * 4 / 3)

        def ternary_quant(w):
            s = jnp.mean(jnp.abs(w))
            q = jnp.clip(jnp.round(w / s), -1.0, 1.0) * s
            return w + jax.lax.stop_gradient(q - w)
        key = jax.random.key(seed)
        k0, k1, k2, k3 = jax.random.split(key, 4)
        x = jax.random.normal(k0, (4, 1024, D_MODEL), dtype=jnp.float32)
        std_in = 1.0 / np.sqrt(D_MODEL)
        std_h = 1.0 / np.sqrt(HIDDEN)
        w1 = jax.random.uniform(k1, (HIDDEN, D_MODEL), jnp.float32, -std_in, std_in)
        w3 = jax.random.uniform(k2, (HIDDEN, D_MODEL), jnp.float32, -std_in, std_in)
        w2 = jax.random.uniform(k3, (D_MODEL, HIDDEN), jnp.float32, -std_h, std_h)
        return {'x': x, 'w1': w1, 'w3': w3, 'w2': w2}
    _L0_ffn_all = _L0_ffn_setup()
    _L0_ffn_in = {k: v for k, v in _L0_ffn_all.items() if k in ('w1', 'w3', 'w2')}
    del _L0_ffn_all

    def _L1_attn_setup():
        import jax, jax.numpy as jnp
        import numpy as np
        import math
        N_EMBD = 512
        N_HEAD = 16
        RATIO_KV = 4
        N_HEAD_KV = N_HEAD // RATIO_KV
        HEAD_DIM = N_EMBD // N_HEAD

        def alibi_slopes(n_heads):

            def pow2_slopes(n):
                start = 2 ** (-2 ** (-(math.log2(n) - 3)))
                return [start * start ** i for i in range(n)]
            if math.log2(n_heads).is_integer():
                return jnp.asarray(pow2_slopes(n_heads), dtype=jnp.float32)
            closest = 2 ** math.floor(math.log2(n_heads))
            base = pow2_slopes(closest)
            if n_heads <= 2 * closest:
                s = base + base[0::2]
            else:
                s = base + base[0::2] + base[1::2]
            return jnp.asarray(s[:n_heads], dtype=jnp.float32)
        key = jax.random.key(seed)
        k0, k1, k2, k3, k4 = jax.random.split(key, 5)
        B, T = (4, 512)
        x = jax.random.normal(k0, (B, T, N_EMBD), dtype=jnp.float32)
        s = 0.02
        Wq = jax.random.normal(k1, (N_EMBD, N_EMBD), dtype=jnp.float32) * s
        Wk = jax.random.normal(k2, (N_EMBD, N_HEAD_KV * HEAD_DIM), dtype=jnp.float32) * s
        Wv = jax.random.normal(k3, (N_EMBD, N_HEAD_KV * HEAD_DIM), dtype=jnp.float32) * s
        Wo = jax.random.normal(k4, (N_EMBD, N_EMBD), dtype=jnp.float32) * s
        return {'x': x, 'Wq': Wq, 'Wk': Wk, 'Wv': Wv, 'Wo': Wo}
    _L1_attn_all = _L1_attn_setup()
    _L1_attn_in = {k: v for k, v in _L1_attn_all.items() if k in ('Wq', 'Wk', 'Wv', 'Wo')}
    del _L1_attn_all

    def _L1_ffn_setup():
        import jax, jax.numpy as jnp
        import numpy as np
        _FP4_LUT = jnp.array([0.0, 0.5, 1.0, 1.5, 2.0, 3.0, 4.0, 6.0, -0.0, -0.5, -1.0, -1.5, -2.0, -3.0, -4.0, -6.0], dtype=jnp.float32)
        GROUP_SIZE = 128
        EPS = 1e-06

        def _dequant_fp4(packed_i32, scales_f16, group_size):
            out_f, in_p = packed_i32.shape
            w = packed_i32.astype(jnp.uint32)
            shifts = jnp.arange(8, dtype=jnp.uint32) * 4
            nib = w[:, :, None] >> shifts & jnp.uint32(15)
            vals = _FP4_LUT[nib.astype(jnp.int32)].reshape(out_f, in_p * 8)
            s = scales_f16.astype(jnp.float32).T
            s_full = jnp.repeat(s, group_size, axis=1)
            return vals * s_full
        key = jax.random.key(seed)
        k1, k2, k3, k4, k5 = jax.random.split(key, 5)
        B, S, H, I = (4, 512, 512, 1408)
        x = jax.random.normal(k1, (B, S, H), dtype=jnp.float32)
        gate_up_packed = jax.random.randint(k2, (2 * I, H // 8), 0, 2147483647, dtype=jnp.int32)
        gate_up_scales = jax.random.uniform(k3, (H // GROUP_SIZE, 2 * I), dtype=jnp.float32).astype(jnp.float16)
        down_packed = jax.random.randint(k4, (H, I // 8), 0, 2147483647, dtype=jnp.int32)
        down_scales = jax.random.uniform(k5, (I // GROUP_SIZE, H), dtype=jnp.float32).astype(jnp.float16)
        return {'x': x, 'gate_up_packed': gate_up_packed, 'gate_up_scales': gate_up_scales, 'down_packed': down_packed, 'down_scales': down_scales}
    _L1_ffn_all = _L1_ffn_setup()
    _L1_ffn_in = {k: v for k, v in _L1_ffn_all.items() if k in ('gate_up_packed', 'gate_up_scales', 'down_packed', 'down_scales')}
    del _L1_ffn_all
    return {'x': x, 'L0_attn_wq': _L0_attn_in['wq'], 'L0_attn_wk': _L0_attn_in['wk'], 'L0_attn_wv': _L0_attn_in['wv'], 'L0_attn_wo': _L0_attn_in['wo'], 'L0_ffn_w1': _L0_ffn_in['w1'], 'L0_ffn_w3': _L0_ffn_in['w3'], 'L0_ffn_w2': _L0_ffn_in['w2'], 'L1_attn_Wq': _L1_attn_in['Wq'], 'L1_attn_Wk': _L1_attn_in['Wk'], 'L1_attn_Wv': _L1_attn_in['Wv'], 'L1_attn_Wo': _L1_attn_in['Wo'], 'L1_ffn_gate_up_packed': _L1_ffn_in['gate_up_packed'], 'L1_ffn_gate_up_scales': _L1_ffn_in['gate_up_scales'], 'L1_ffn_down_packed': _L1_ffn_in['down_packed'], 'L1_ffn_down_scales': _L1_ffn_in['down_scales']}

def reference(x, L0_attn_wq, L0_attn_wk, L0_attn_wv, L0_attn_wo, L0_ffn_w1, L0_ffn_w3, L0_ffn_w2, L1_attn_Wq, L1_attn_Wk, L1_attn_Wv, L1_attn_Wo, L1_ffn_gate_up_packed, L1_ffn_gate_up_scales, L1_ffn_down_packed, L1_ffn_down_scales):
    import jax
    import jax.numpy as jnp

    def _L0_tok_ref(qkv):
        import jax, jax.numpy as jnp
        import numpy as np
        N, C, T = (32, 128, 512)
        ch = qkv.shape[1] // 3
        q, k, v = jnp.split(qkv, 3, axis=1)
        scale = 1.0 / np.sqrt(np.sqrt(ch))
        weight = jnp.einsum('bct,bcs->bts', q * scale, k * scale)
        weight = jax.nn.softmax(weight.astype(jnp.float32), axis=-1).astype(weight.dtype)
        return jnp.einsum('bts,bcs->bct', weight, v)

    def _L0_attn_ref(x, wq, wk, wv, wo):
        import jax, jax.numpy as jnp
        import numpy as np
        D_MODEL = 512
        N_HEADS = 32
        N_KV_HEADS = 8
        HEAD_DIM = D_MODEL // N_HEADS
        N_REP = N_HEADS // N_KV_HEADS
        SCALE = HEAD_DIM ** (-0.5)

        def _rope_tables(seq_len):
            inv_freq = 1.0 / 10000.0 ** (jnp.arange(0, HEAD_DIM, 2, dtype=jnp.float32) / HEAD_DIM)
            t = jnp.arange(seq_len, dtype=jnp.float32)
            freqs = jnp.outer(t, inv_freq)
            return (jnp.cos(freqs), jnp.sin(freqs))

        def _apply_rope(x, cos, sin):
            x_r, x_i = (x[..., ::2], x[..., 1::2])
            out_r = x_r * cos - x_i * sin
            out_i = x_r * sin + x_i * cos
            out = jnp.stack([out_r, out_i], axis=-1)
            return out.reshape(x.shape)
        bs, seq_len, _ = x.shape
        q = (x @ wq.T).reshape(bs, seq_len, N_HEADS, HEAD_DIM).transpose(0, 2, 1, 3)
        k = (x @ wk.T).reshape(bs, seq_len, N_KV_HEADS, HEAD_DIM).transpose(0, 2, 1, 3)
        v = (x @ wv.T).reshape(bs, seq_len, N_KV_HEADS, HEAD_DIM).transpose(0, 2, 1, 3)
        cos, sin = _rope_tables(seq_len)
        q = _apply_rope(q, cos, sin)
        k = _apply_rope(k, cos, sin)
        k = jnp.repeat(k, N_REP, axis=1)
        v = jnp.repeat(v, N_REP, axis=1)
        attn = jnp.einsum('bhqd,bhkd->bhqk', q, k) * SCALE
        causal = jnp.triu(jnp.ones((seq_len, seq_len), dtype=bool), k=1)
        attn = jnp.where(causal, -jnp.inf, attn)
        attn = jax.nn.softmax(attn, axis=-1)
        out = jnp.einsum('bhqk,bhkd->bhqd', attn, v)
        out = out.transpose(0, 2, 1, 3).reshape(bs, seq_len, D_MODEL)
        return out @ wo.T

    def _L0_ffn_ref(x, w1, w3, w2):
        import jax, jax.numpy as jnp
        import numpy as np
        D_MODEL = 512
        HIDDEN = int(2 * D_MODEL * 4 / 3)

        def ternary_quant(w):
            s = jnp.mean(jnp.abs(w))
            q = jnp.clip(jnp.round(w / s), -1.0, 1.0) * s
            return w + jax.lax.stop_gradient(q - w)
        w1q = ternary_quant(w1)
        w3q = ternary_quant(w3)
        w2q = ternary_quant(w2)
        h1 = jnp.einsum('bsd,hd->bsh', x, w1q)
        h3 = jnp.einsum('bsd,hd->bsh', x, w3q)
        g = jax.nn.silu(h1) * h3
        return jnp.einsum('bsh,dh->bsd', g, w2q)

    def _L1_attn_ref(x, Wq, Wk, Wv, Wo):
        import jax, jax.numpy as jnp
        import numpy as np
        import math
        N_EMBD = 512
        N_HEAD = 16
        RATIO_KV = 4
        N_HEAD_KV = N_HEAD // RATIO_KV
        HEAD_DIM = N_EMBD // N_HEAD

        def alibi_slopes(n_heads):

            def pow2_slopes(n):
                start = 2 ** (-2 ** (-(math.log2(n) - 3)))
                return [start * start ** i for i in range(n)]
            if math.log2(n_heads).is_integer():
                return jnp.asarray(pow2_slopes(n_heads), dtype=jnp.float32)
            closest = 2 ** math.floor(math.log2(n_heads))
            base = pow2_slopes(closest)
            if n_heads <= 2 * closest:
                s = base + base[0::2]
            else:
                s = base + base[0::2] + base[1::2]
            return jnp.asarray(s[:n_heads], dtype=jnp.float32)
        B, T, C = x.shape
        group = N_HEAD // N_HEAD_KV
        q = (x @ Wq).reshape(B, T, N_HEAD, HEAD_DIM).transpose(0, 2, 1, 3)
        k = (x @ Wk).reshape(B, T, N_HEAD_KV, HEAD_DIM).transpose(0, 2, 1, 3)
        v = (x @ Wv).reshape(B, T, N_HEAD_KV, HEAD_DIM).transpose(0, 2, 1, 3)
        k = jnp.repeat(k, group, axis=1)
        v = jnp.repeat(v, group, axis=1)
        scale = 1.0 / math.sqrt(HEAD_DIM)
        att = jnp.einsum('bhqd,bhkd->bhqk', q, k) * scale
        slopes = alibi_slopes(N_HEAD)
        slopes = jnp.repeat(slopes, group)[:N_HEAD]
        pos = jnp.arange(T)
        rel = pos[None, :] - pos[:, None]
        bias = slopes[:, None, None] * rel.astype(jnp.float32)[None, :, :]
        causal = jnp.triu(jnp.full((T, T), -jnp.inf, dtype=jnp.float32), k=1)
        att = att + bias[None] + causal[None, None]
        att = jax.nn.softmax(att.astype(jnp.float32), axis=-1).astype(q.dtype)
        y = jnp.einsum('bhqk,bhkd->bhqd', att, v)
        y = y.transpose(0, 2, 1, 3).reshape(B, T, C)
        return y @ Wo

    def _L1_ffn_ref(x, gate_up_packed, gate_up_scales, down_packed, down_scales):
        import jax, jax.numpy as jnp
        import numpy as np
        _FP4_LUT = jnp.array([0.0, 0.5, 1.0, 1.5, 2.0, 3.0, 4.0, 6.0, -0.0, -0.5, -1.0, -1.5, -2.0, -3.0, -4.0, -6.0], dtype=jnp.float32)
        GROUP_SIZE = 128
        EPS = 1e-06

        def _dequant_fp4(packed_i32, scales_f16, group_size):
            out_f, in_p = packed_i32.shape
            w = packed_i32.astype(jnp.uint32)
            shifts = jnp.arange(8, dtype=jnp.uint32) * 4
            nib = w[:, :, None] >> shifts & jnp.uint32(15)
            vals = _FP4_LUT[nib.astype(jnp.int32)].reshape(out_f, in_p * 8)
            s = scales_f16.astype(jnp.float32).T
            s_full = jnp.repeat(s, group_size, axis=1)
            return vals * s_full
        I = gate_up_packed.shape[0] // 2
        w_gu = _dequant_fp4(gate_up_packed, gate_up_scales, GROUP_SIZE)
        w_down = _dequant_fp4(down_packed, down_scales, GROUP_SIZE)
        gate_up = jnp.einsum('bsh,oh->bso', x, w_gu)
        gate, up = (gate_up[..., :I], gate_up[..., I:])
        h = jax.nn.silu(gate) * up
        y = jnp.einsum('bsi,hi->bsh', h, w_down)
        rms = jnp.sqrt(jnp.mean(y * y, axis=-1, keepdims=True) + EPS)
        return y / rms
    h = _L0_tok_ref(x)
    h = h + _L0_attn_ref(_layernorm(h, axis=-1), L0_attn_wq, L0_attn_wk, L0_attn_wv, L0_attn_wo)
    h = h + _L0_ffn_ref(_layernorm(h, axis=-1), L0_ffn_w1, L0_ffn_w3, L0_ffn_w2)
    h = h + _L1_attn_ref(_layernorm(h, axis=-1), L1_attn_Wq, L1_attn_Wk, L1_attn_Wv, L1_attn_Wo)
    h = h + _L1_ffn_ref(_layernorm(h, axis=-1), L1_ffn_gate_up_packed, L1_ffn_gate_up_scales, L1_ffn_down_packed, L1_ffn_down_scales)
    return h

_drawn_inputs = setup_inputs


def setup_inputs(seed=0):
    import zlib

    import numpy as np

    out = dict(_drawn_inputs(seed))
    spreads = {}
    factors = {}
    for name, (base, spread) in spreads.items():
        noise = np.random.default_rng([zlib.crc32(name.encode()), seed]).standard_normal(out[name].shape)
        drawn = base * np.exp(spread * noise) if base else spread * noise
        out[name] = jnp.asarray(drawn.astype(out[name].dtype))
    for name, factor in factors.items():
        out[name] = (out[name] * factor).astype(out[name].dtype)
    return out
```

```python
import numpy as np
import concourse.bass as bass
from concourse import mybir
from contextlib import ExitStack

F32 = mybir.dt.float32
F16 = mybir.dt.float16
BF16 = mybir.dt.bfloat16
I32 = mybir.dt.int32
ALU = mybir.AluOpType
ACT = mybir.ActivationFunctionType
AX = mybir.AxisListType


def loop_pairs(eng, step, first, loop_from, loop_to, last):
    for n in range(first, loop_from):
        step(n // 2, n % 2)
    with eng.Fori(loop_from // 2, loop_to // 2) as k:
        step(k, 0)
        step(k, 1)
    for n in range(loop_to, last):
        step(n // 2, n % 2)


def wait(eng, sem, count):
    if not isinstance(count, int) or count > 0:
        eng.wait_ge(sem, count)


def wait_alone(eng, passed, sem, count):
    if not isinstance(count, int) or count > 0:
        eng.wait_ge(sem, count)
        if not isinstance(count, int):
            eng.sem_inc(passed, 1)


def semaphores(nc, ctx, prefix):
    made = []

    def make(name):
        made.append(nc.alloc_semaphore(prefix + name))
        return made[-1]

    def end():
        nc.clear_and_free_semaphores(made)
        nc.all_engine_barrier()
    ctx.callback(end)
    return make


def inside(t, tiles):
    return not isinstance(t, int) or 0 <= t < tiles


def token_mixer(nc, x, ident_dram, h_dram, SEQS=128):
    C, T = x.shape[1] // 3, x.shape[2]
    P = 128
    B = P // C
    NT = T // P
    TILES = SEQS // B
    SCALE = float(C) ** -0.5
    PARTS = 3
    KS = PARTS * C
    KM = KS + 2
    W = C + 1
    with ExitStack() as ctx:
        sb = lambda name, shape, dt: ctx.enter_context(nc.sbuf_tensor(name, shape, dt))
        sem = semaphores(nc, ctx, "")
        ident = sb("tm_ident", [P, P], F32)
        xin = [sb(f"tm_xin{i}", [P, 3, T], F32) for i in range(2)]
        xs = [sb(f"tm_xs{i}", [P, 4, T], F16) for i in range(2)]
        qk = [sb(f"tm_qk{i}", [P, 2, B, T], F16) for i in range(2)]
        vhi = [sb(f"tm_vhi{i}", [P, NT, B, W], F16) for i in range(2)]
        vlo = [sb(f"tm_vlo{i}", [P, NT, B, C], F16) for i in range(2)]
        negmax = [sb(f"tm_negmax{i}", [P, B * NT], F32) for i in range(2)]
        mrow = sb("tm_mrow", [B * NT, 2, P], F16)
        prob = [sb(f"tm_prob{i}", [P, NT, T], F32) for i in range(2)]
        phi = [sb(f"tm_phi{i}", [P, NT, T], F16) for i in range(2)]
        plo = [sb(f"tm_plo{i}", [P, NT, T], F16) for i in range(2)]
        rden = sb("tm_rden", [P, 2, 2, NT], F32)
        hT = [sb(f"tm_hT{i}", [P, NT, B, C], F32) for i in range(2)]
        htok = [sb(f"tm_htok{i}", [P, T], F32) for i in range(2)]
        s1 = ctx.enter_context(nc.psum_tensor("tm_s1", [P, 2, T], F32))
        s2 = ctx.enter_context(nc.psum_tensor("tm_s2", [P, 2, 2, T], F32))
        po = ctx.enter_context(nc.psum_tensor("tm_po", [P, 512], F32))
        pm = ctx.enter_context(nc.psum_tensor("tm_pm", [P, 512], F32))
        po_v = po[:, 0:2 * NT * W].rearrange("p (b i w) -> p b i w", b=2, i=NT)
        pm_v = pm[:, :].rearrange("p (j n) -> p j n", j=NT)

        ident_in = sem("tm_ident_in")
        ones_set = sem("tm_ones_set")
        loaded = [sem(f"tm_loaded{i}") for i in range(2)]
        split = sem("tm_split")
        sp_passed, pool_passed = sem("tm_sp_passed"), sem("tm_pool_passed")
        stacked = [[sem(f"tm_stacked{u}{b}") for b in range(B)] for u in range(2)]
        vt_ready = sem("tm_vt_ready")
        vhi_ready = sem("tm_vhi_ready")
        vlo_ready = sem("tm_vlo_ready")
        s1_ready = sem("tm_s1_ready")
        max_done = sem("tm_max_done")
        mt_ready = sem("tm_mt_ready")
        mhi_done = sem("tm_mhi_done")
        mrow_done = sem("tm_mrow_done")
        mrow_in = sem("tm_mrow_in")
        s2_ready = sem("tm_s2_ready")
        exp_done = sem("tm_exp_done")
        phi_ready = sem("tm_phi_ready")
        plo_ready = sem("tm_plo_ready")
        pv_done = sem("tm_pv_done")
        rden_done = sem("tm_rden_done")
        norm_done = sem("tm_norm_done")
        htr_done = sem("tm_htr_done")
        htok_ready = sem("tm_htok_ready")
        stored = [sem(f"tm_stored{i}") for i in range(2)]

        FIRST, FROM, TO, LAST = -3, 4, (TILES - 3) // 2 * 2, TILES + 1
        block = ctx.enter_context(nc.Block())

        @block.sync
        def _(sp):
            sp.dma_start(ident[:, :], ident_dram).then_inc(ident_in, 16)

            def load(t, u, k):
                if inside(t, TILES):
                    wait_alone(sp, sp_passed, split, 2 * (t - 1))
                    wait_alone(sp, sp_passed, vt_ready, t - 1)
                    for b in range(B):
                        sp.dma_start(xin[u][b * C:(b + 1) * C, :, :],
                                     x[t * B + b].rearrange("(s c) t -> c s t", c=C)).then_inc(loaded[u], 16)

            def store(t, u, k):
                if inside(t, TILES):
                    wait_alone(sp, sp_passed, htok_ready, t + 1)
                    sp.dma_start(h_dram[bass.ds(t * P, P), :], htok[u][:, :]).then_inc(stored[u], 16)

            def stack(t, u, b):
                if inside(t, TILES):
                    wait_alone(sp, sp_passed, split, 2 * (t + 1))
                    wait_alone(sp, sp_passed, s2_ready, 8 * (t - 2) + 2 * b + 2)
                    c = slice(b * C, (b + 1) * C)
                    for g, (lo, hi) in enumerate(((0, 2), (0, 3), (1, 2))):
                        sp.dma_start(qk[u][g * C:(g + 1) * C, :, b, :],
                                     xs[u][c, lo:hi + 1:hi - lo, :]).then_inc(stacked[u][b], 16)

            def maxima(t, u):
                if inside(t, TILES):
                    wait_alone(sp, sp_passed, mrow_done, t + 1)
                    for part in range(2):
                        sp.dma_start(qk[u][KS + part:KS + part + 1, 0, :, :]
                                     .rearrange("o b (i t) -> o (b i) t", i=NT),
                                     mrow[:, part, :]).then_inc(mrow_in, 16)

            def step(k, u):
                n = 2 * k + u
                load(n + 3, 1 - u, k + (u + 3) // 2)
                store(n - 1, 1 - u, 0)
                stack(n + 2, u, 0)
                stack(n + 2, u, 1)
                maxima(n + 1, 1 - u)
                stack(n + 2, u, 2)
                stack(n + 2, u, 3)
            loop_pairs(sp, step, FIRST, FROM, TO, LAST)
            for u in range(2):
                sp.wait_ge(stored[u], 16 * (TILES // 2))

        @block.gpsimd
        def _(pool):
            def parts(t, u, half):
                if inside(t, TILES):
                    wait_alone(pool, pool_passed, loaded[u], 64 * (half + 1))
                    for b in range(B):
                        wait_alone(pool, pool_passed, stacked[u][b], 48 * half)
                    pool.tensor_copy(xs[u][:, 0:4:2, :], xin[u][:, 0:2, :]).then_inc(split, 1)
                    wait(pool, split, 2 * t + 1)
                    pool.tensor_tensor(xs[u][:, 1:4:2, :], xin[u][:, 0:2, :], xs[u][:, 0:4:2, :],
                                       ALU.subtract).then_inc(split, 1)

            def step(k, u):
                n = 2 * k + u
                parts(n + 2, u, k + 1)
            loop_pairs(pool, step, FIRST, FROM, TO, LAST)

        @block.scalar
        def _(act):
            def values_hi(t, u):
                if inside(t, TILES):
                    wait(act, vt_ready, t + 1)
                    wait(act, pv_done, 4 * (t - 1))
                    if isinstance(t, int) and t < 2:
                        wait(act, ones_set, 4)
                    nc.scalar.copy(vhi[u][:, :, :, 0:C], pm_v.rearrange("p j (b c) -> p j b c", b=B))\
                        .then_inc(vhi_ready, 1)

            def exps(t, b):
                if inside(t, TILES):
                    for h in range(2):
                        wait(act, s2_ready, 8 * t + 2 * b + h + 1)
                        if h == 0:
                            wait(act, plo_ready, 4 * t + b - 1)
                        nc.scalar.activation(prob[b % 2][:, 2 * h:2 * h + 2, :], s2[:, h, :, :], ACT.Exp,
                                             scale=SCALE).then_inc(exp_done, 1)

            def probs_hi(t, b):
                if inside(t, TILES):
                    wait(act, exp_done, 8 * t + 2 * b + 2)
                    wait(act, pv_done, 4 * t + b - 1)
                    nc.scalar.copy(phi[b % 2][:, :, :], prob[b % 2][:, :, :]).then_inc(phi_ready, 1)

            def tokens_out(t, u, half):
                if inside(t, TILES):
                    wait(act, htr_done, t + 1)
                    wait(act, stored[u], 16 * half)
                    nc.scalar.copy(htok[u][:, :], pm[:, :]).then_inc(htok_ready, 1)

            def step(k, u):
                n = 2 * k + u
                probs_hi(n - 1, 3)
                exps(n, 0)
                tokens_out(n - 1, 1 - u, k + (u - 1) // 2)
                values_hi(n + 1, 1 - u)
                for b in range(3):
                    probs_hi(n, b)
                    exps(n, b + 1)
            loop_pairs(act, step, FIRST, FROM, TO, LAST)

        @block.vector
        def _(dve):
            for u in range(2):
                dve.memset(qk[u][KS:KM, 1, :, :], 1.0).then_inc(ones_set, 1)
                dve.memset(vhi[u][:, :, :, C:W], 1.0).then_inc(ones_set, 1)

            def values_lo(t, u):
                if inside(t, TILES):
                    wait(dve, vhi_ready, t + 1)
                    nc.vector.tensor_tensor(vlo[u][:, :, :, :], pm_v.rearrange("p j (b c) -> p j b c", b=B),
                                            vhi[u][:, :, :, 0:C], ALU.subtract).then_inc(vlo_ready, 1)

            def maxes(t, u, b):
                if inside(t, TILES):
                    for i in range(NT):
                        m = b * NT + i
                        wait(dve, s1_ready, 16 * t + m + 1)
                        if m == 0:
                            wait(dve, mt_ready, t - 1)
                        nc.vector.tensor_reduce(negmax[u][:, m:m + 1], s1[:, m % 2, :], AX.X, ALU.max,
                                                negate=True).then_inc(max_done, 1)

            def probs_lo(t, b):
                if inside(t, TILES):
                    wait(dve, phi_ready, 4 * t + b + 1)
                    nc.vector.tensor_tensor(plo[b % 2][:, :, :], prob[b % 2][:, :, :], phi[b % 2][:, :, :],
                                            ALU.subtract).then_inc(plo_ready, 1)

            def maxima_parts(t):
                if inside(t, TILES):
                    wait(dve, mt_ready, t + 1)
                    wait(dve, mrow_in, 32 * t)
                    nc.vector.tensor_copy(mrow[:, 0, :], pm[0:B * NT, 0:P]).then_inc(mhi_done, 1)
                    wait(dve, mhi_done, t + 1)
                    nc.vector.tensor_tensor(mrow[:, 1, :], pm[0:B * NT, 0:P], mrow[:, 0, :],
                                            ALU.subtract).then_inc(mrow_done, 1)

            def normalise(t, u, pair):
                if inside(t, TILES):
                    wait(dve, pv_done, 4 * t + 2 * pair + 2)
                    if pair == 0:
                        wait(dve, htr_done, t - 1)
                    nc.vector.reciprocal(rden[:, pair, :, :], po_v[:, :, :, C]).then_inc(rden_done, 1)
                    wait(dve, rden_done, 2 * t + pair + 1)
                    nc.vector.tensor_tensor(
                        hT[u][:, :, 2 * pair:2 * pair + 2, :].rearrange("p i b c -> p b i c"),
                        po_v[:, :, :, 0:C],
                        rden[:, pair, :, :].unsqueeze(3).broadcast_to([P, 2, NT, C]),
                        ALU.mult).then_inc(norm_done, 1)

            def step(k, u):
                n = 2 * k + u
                maxes(n + 1, 1 - u, 0)
                probs_lo(n - 1, 3)
                maxes(n + 1, 1 - u, 1)
                normalise(n - 1, 1 - u, 1)
                values_lo(n + 1, 1 - u)
                maxes(n + 1, 1 - u, 2)
                probs_lo(n, 0)
                maxes(n + 1, 1 - u, 3)
                maxima_parts(n + 1)
                probs_lo(n, 1)
                normalise(n, u, 0)
                probs_lo(n, 2)
            loop_pairs(dve, step, FIRST, FROM, TO, LAST)

        @block.tensor
        def _(pe):
            pe.wait_ge(ident_in, 16)
            pe.wait_ge(ones_set, 4)

            def values_transposed(t, u, half):
                if inside(t, TILES):
                    wait(pe, loaded[u], 64 * (half + 1))
                    wait(pe, mrow_done, t)
                    wait(pe, htok_ready, t - 1)
                    for j in range(NT):
                        last = nc.tensor.transpose(pm_v[:, j, :], xin[u][:, 2, j * P:(j + 1) * P], ident[:, :])
                    last.then_inc(vt_ready, 1)

            def scores_for_max(t, u, b, half):
                if inside(t, TILES):
                    wait(pe, stacked[u][b], 48 * (half + 1))
                    for i in range(NT):
                        m = b * NT + i
                        wait(pe, max_done, 16 * t + m - 1)
                        nc.tensor.matmul(s1[:, m % 2, :], qk[u][0:KS, 0, b, i * P:(i + 1) * P],
                                         qk[u][0:KS, 1, b, :], start=True, stop=True).then_inc(s1_ready, 1)

            def scores(t, u, b):
                if inside(t, TILES):
                    if b == 0:
                        wait(pe, mrow_in, 32 * (t + 1))
                    for h in range(2):
                        wait(pe, exp_done, 8 * t + 2 * b + h - 1)
                        for j in (2 * h, 2 * h + 1):
                            last = nc.tensor.matmul(s2[:, h, j % 2, :], qk[u][0:KM, 1, b, j * P:(j + 1) * P],
                                                    qk[u][0:KM, 0, b, :], start=True, stop=True)
                        last.then_inc(s2_ready, 1)

            def values(t, u, b):
                if inside(t, TILES):
                    wait(pe, plo_ready, 4 * t + b + 1)
                    if b == 0:
                        wait(pe, vlo_ready, t + 1)
                    if b % 2 == 0:
                        wait(pe, norm_done, 2 * t + b // 2)
                    for i in range(NT):
                        at = slice(i * P, (i + 1) * P)
                        for j in range(NT):
                            ph, pl = phi[b % 2][:, j, at], plo[b % 2][:, j, at]
                            nc.tensor.matmul(po_v[:, b % 2, i, :], ph, vhi[u][:, j, b, :], start=j == 0, stop=False)
                            nc.tensor.matmul(po_v[:, b % 2, i, 0:C], ph, vlo[u][:, j, b, :], start=False, stop=False)
                            last = nc.tensor.matmul(po_v[:, b % 2, i, :], pl, vhi[u][:, j, b, :],
                                                    start=False, stop=j == NT - 1)
                    last.then_inc(pv_done, 1)

            def tokens(t, u):
                if inside(t, TILES):
                    wait(pe, norm_done, 2 * t + 2)
                    wait(pe, mrow_done, min(t + 2, TILES) if isinstance(t, int) else t + 2)
                    for i in range(NT):
                        last = nc.tensor.transpose(pm_v[:, i, :], hT[u][:, i, :, :].rearrange("p b c -> p (b c)"),
                                                   ident[:, :])
                    last.then_inc(htr_done, 1)

            def maxima(t, u):
                if inside(t, TILES):
                    wait(pe, max_done, 16 * (t + 1))
                    wait(pe, vlo_ready, t + 1)
                    nc.tensor.transpose(pm[0:B * NT, 0:P], negmax[u][:, :], ident[:, :]).then_inc(mt_ready, 1)

            def step(k, u):
                n = 2 * k + u
                scores_for_max(n + 1, 1 - u, 0, k + (u + 1) // 2)
                scores(n, u, 0)
                scores_for_max(n + 1, 1 - u, 1, k + (u + 1) // 2)
                values(n - 1, 1 - u, 3)
                tokens(n - 1, 1 - u)
                values_transposed(n + 1, 1 - u, k + (u + 1) // 2)
                scores_for_max(n + 1, 1 - u, 2, k + (u + 1) // 2)
                scores(n, u, 1)
                scores_for_max(n + 1, 1 - u, 3, k + (u + 1) // 2)
                values(n, u, 0)
                maxima(n + 1, 1 - u)
                scores(n, u, 2)
                values(n, u, 1)
                scores(n, u, 3)
                values(n, u, 2)
            loop_pairs(pe, step, FIRST, FROM, TO, LAST)
def attention(nc, pre, h_dram, out_dram, wqkv_dram, wo_dram, const, HKV, D, rope, TILES=32):
    P, L, DM = 128, 32, 512
    R = 4
    B = P // L
    KT = DM // P
    G = HKV // 2
    DQ, DKV = R * HKV * D, HKV * D
    DALL = DQ + 2 * DKV
    NB = HKV * B * L
    SB = max(1, NB // 512)
    W = D + 1
    SCALE, EPS = float(D) ** -0.5, 1e-5
    with ExitStack() as ctx:
        sb = lambda name, shape, dt: ctx.enter_context(nc.sbuf_tensor(pre + name, shape, dt))
        sem = semaphores(nc, ctx, pre)
        ps = lambda name, shape, dt: ctx.enter_context(nc.psum_tensor(pre + name, shape, dt))
        pair = lambda name, shape, dt: [sb(f"{name}{i}", shape, dt) for i in range(2)]
        ident = sb("ident", [P, P], F32)
        ident16 = sb("ident16", [P, P], F16)
        select = sb("select", [96, P], BF16)
        bias = sb("bias", [96, NB], BF16)
        own = sb("own", [P, B], F32)
        minus_half = sb("minus_half", [P, 1], F32)
        wstage = sb("wstage", [P, KT * DALL], F32)
        wqkv = [sb(f"wqkv{i}", [P, KT, DALL], F16) for i in range(2)]
        wo = [sb(f"wo{i}", [P, R, DM], F16) for i in range(2)]
        if rope:
            cos = sb("cos", [P, 16], F32)
            sin = sb("sin", [P, 2, 8], F32)
            turned = sb("turned", [P, DQ + DKV], F32)
            crossed = sb("crossed", [P, DQ + DKV], F32)
            rot = sb("rot", [P, DQ + DKV], F32)
        hin, hres, hout = pair("hin", [P, DM], F32), pair("hres", [P, DM], F32), pair("hout", [P, DM], F32)
        stats, mv, rstd = pair("stats", [P, 6], F32), pair("mv", [P, 2], F32), pair("rstd", [P, 1], F32)
        veps = pair("veps", [P, 1], F32)
        xn = sb("xn", [P, DM], F32)
        xhi, xlo = pair("xhi", [P, KT, P], F16), pair("xlo", [P, KT, P], F16)
        qkv = sb("qkv", [P, DALL], F32)
        qs = sb("qs", [P, R, HKV, 2, D], F16)
        kp = sb("kp", [P, 2, HKV, 2, D], F16)
        v16, vrest = sb("v16", [P, DKV], F16), sb("vrest", [P, DKV], F32)
        vhi, vlo = pair("vhi", [P, HKV, B, W], F16), pair("vlo", [P, HKV, B, W], F16)
        qT = sb("qT", [P, 2, B, R, L], F16)
        kT = sb("kT", [P, 2, 2, B, G, L], F16)
        mx = sb("mx", [P, HKV * B], F32)
        shifted = sb("shifted", [P, NB], F32)
        prob = sb("prob", [P, HKV, B, L], F32)
        pThi, pTlo = sb("pThi", [P, HKV, P], F16), sb("pTlo", [P, HKV, P], F16)
        rden = sb("rden", [P, 2, G, B], F32)
        y = sb("y", [P, B, HKV, D], F32)
        yThi, yTlo = sb("yThi", [P, R, B, L], F16), sb("yTlo", [P, R, B, L], F16)

        bankA = ps("bankA", [P, 512], F32)
        bankB = ps("bankB", [P, 512], F32)
        bankC = ps("bankC", [P, 512], F32)
        bankD = ps("bankD", [P, 1024], F16)
        bankS = ps("bankS", [P, 1024], F32)
        bankO = ps("bankO", [P, 2, 512], F32)
        S = bankS[:, 0:NB]
        kTp = bankC[:, :].bitcast(F16)[:, 0:4 * P]
        O = bankO[:, :, 0:G * B * W].rearrange("p f (g b w) -> p f g b w", g=G, b=B)

        c_in, w_in, w_hi, w_ready = sem("c_in"), sem("w_in"), sem("w_hi"), sem("w_ready")
        set_up = sem("set_up")
        h_in = [sem(f"h_in{i}") for i in range(2)]
        res_in = [sem(f"res_in{i}") for i in range(2)]
        stored = [sem(f"stored{i}") for i in range(2)]
        names = ("stats_done mv_done veps_done rstd_done xn_done xT_ready xhi_done xlo_done q_ready kv_ready "
                 "q_copied kv_copied turned_done crossed_done rot_done qhi_done qlo_done khi_done klo_done "
                 "v16_done vrest_done v_done qT_ready kT_ready qT_copied kT_act kT_dve s_ready max_done "
                 "shift_done exp_done pT_ready pThi_done pTlo_done o_ready rden_done y_done yT_ready "
                 "yThi_done yTlo_done z_ready out_done sp_passed pool_passed dve_passed").split()
        s = {n: sem(n) for n in names}

        FIRST, FROM, TO, LAST = -4, 2, (TILES - 4) // 2 * 2, TILES + 1
        block = ctx.enter_context(nc.Block())

        @block.sync
        def _(sp):
            consts = [(ident, "ident"), (ident16, "ident16"), (select, "select"), (bias, pre + "bias"),
                      (own, "own")]
            if rope:
                consts += [(cos, "cos"), (sin, "sin")]
            for dst, name in consts:
                sp.dma_start(dst[:], const[name]).then_inc(c_in, 16)
            sp.dma_start(wstage[:, :].rearrange("p (j n) -> p j n", j=KT),
                         wqkv_dram.rearrange("(j p) n -> p j n", p=P)).then_inc(w_in, 16)
            sp.wait_ge(w_ready, 1)
            sp.dma_start(wstage[:, 0:R * DM].rearrange("p (r n) -> p r n", r=R),
                         wo_dram.rearrange("(r p) n -> p r n", p=P)).then_inc(w_in, 16)

            def load(t, u):
                if inside(t, TILES):
                    wait_alone(sp, s["sp_passed"], s["xn_done"], t - 1)
                    sp.dma_start(hin[u][:, :], h_dram[bass.ds(t * P, P), :]).then_inc(h_in[u], 16)

            def load_residual(t, u):
                if inside(t, TILES):
                    wait_alone(sp, s["sp_passed"], s["out_done"], t - 1)
                    sp.dma_start(hres[u][:, :], h_dram[bass.ds(t * P, P), :]).then_inc(res_in[u], 16)

            def store(t, u):
                if inside(t, TILES):
                    wait_alone(sp, s["sp_passed"], s["out_done"], t + 1)
                    sp.dma_start(out_dram[bass.ds(t * P, P), :], hout[u][:, :]).then_inc(stored[u], 16)

            def step(k, u):
                n = 2 * k + u
                load(n + 4, u)
                load_residual(n, u)
                store(n - 1, 1 - u)
            loop_pairs(sp, step, FIRST, FROM, TO, LAST)
            for u in range(2):
                sp.wait_ge(stored[u], 16 * (TILES // 2))

        @block.gpsimd
        def _(pool):
            pool.wait_ge(c_in, 16 * (7 if rope else 5))
            pool.wait_ge(set_up, 8)

            def inverse_deviation(t, u):
                if inside(t, TILES):
                    wait(pool, s["veps_done"], t + 1)
                    pool.tensor_tensor(rstd[u][:, :], veps[u][:, :], minus_half[:, :], ALU.pow)\
                        .then_inc(s["rstd_done"], 1)

            def cross(t):
                if inside(t, TILES) and rope:
                    wait_alone(pool, s["pool_passed"], s["q_copied"], t + 1)
                    wait_alone(pool, s["pool_passed"], s["kv_copied"], t + 1)
                    wait_alone(pool, s["pool_passed"], s["rot_done"], t)
                    src = qkv[:, 0:DQ + DKV].rearrange("p (h i e) -> p h i e", e=2, i=8)
                    dst = crossed[:, :].rearrange("p (h i e) -> p h i e", e=2, i=8)
                    for e in range(2):
                        pool.tensor_tensor(dst[:, :, :, e], src[:, :, :, 1 - e],
                                           sin[:, e, :].unsqueeze(1).broadcast_to([P, (DQ + DKV) // 16, 8]),
                                           ALU.mult).then_inc(s["crossed_done"], 1)

            def values(t, u):
                if inside(t, TILES):
                    wait_alone(pool, s["pool_passed"], s["kv_copied"], t + 1)
                    wait_alone(pool, s["pool_passed"], s["o_ready"], t - 1)
                    v = qkv[:, DQ + DKV:DALL]
                    spread = lambda a: a.rearrange("p (h d) -> p h d", h=HKV).unsqueeze(2)\
                        .broadcast_to([P, HKV, B, D])
                    mask = own[:, :].unsqueeze(1).unsqueeze(3).broadcast_to([P, HKV, B, D])
                    pool.tensor_copy(v16[:, :], v).then_inc(s["v16_done"], 1)
                    pool.tensor_tensor(vhi[u][:, :, :, 0:D], spread(v), mask, ALU.mult).then_inc(s["v_done"], 1)
                    wait_alone(pool, s["pool_passed"], s["v16_done"], t + 1)
                    pool.tensor_tensor(vrest[:, :], v, v16[:, :], ALU.subtract).then_inc(s["vrest_done"], 1)
                    wait_alone(pool, s["pool_passed"], s["vrest_done"], t + 1)
                    pool.tensor_tensor(vlo[u][:, :, :, 0:D], spread(vrest[:, :]), mask, ALU.mult)\
                        .then_inc(s["v_done"], 1)

            def step(k, u):
                n = 2 * k + u
                inverse_deviation(n + 3, 1 - u)
                cross(n + 1)
                values(n + 1, 1 - u)
            loop_pairs(pool, step, FIRST, FROM, TO, LAST)

        @block.scalar
        def _(act):
            act.wait_ge(w_in, 16)
            nc.scalar.copy(wqkv[0][:, :, :], wstage[:, :].rearrange("p (j n) -> p j n", j=KT)).then_inc(w_hi, 1)
            act.wait_ge(w_in, 32)
            nc.scalar.copy(wo[0][:, :, :], wstage[:, 0:R * DM].rearrange("p (r n) -> p r n", r=R)).then_inc(w_hi, 1)
            act.wait_ge(set_up, 8)

            def copy_qT(t):
                if inside(t, TILES):
                    wait(act, s["qT_ready"], t + 1)
                    wait(act, s["s_ready"], t)
                    for f in range(2):
                        last = nc.scalar.copy(qT[:, f, :, :, :].rearrange("p b r q -> p r b q"),
                                              bankD[:, f * R * P:(f + 1) * R * P]
                                              .rearrange("p (r b q) -> p r b q", r=R, b=B))
                    last.then_inc(s["qT_copied"], 1)

            def copy_kT(t):
                if inside(t, TILES):
                    wait(act, s["kT_dve"], t + 1)
                    for j in range(G // 2, G):
                        rows = slice(j * P // G, (j + 1) * P // G)
                        last = nc.scalar.copy(kT[rows, :, :, :, j, :].rearrange("p a f b k -> p (a f b) k"),
                                              kTp[rows, :].rearrange("p (n k) -> p n k", k=L))
                    last.then_inc(s["kT_act"], 1)

            def x_hi(t, u):
                if inside(t, TILES):
                    wait(act, s["xT_ready"], t + 1)
                    wait(act, s["kv_ready"], t - 1)
                    nc.scalar.copy(xhi[u][:, :, :], bankA[:, :].rearrange("p (j n) -> p j n", j=KT))\
                        .then_inc(s["xhi_done"], 1)

            def exps(t):
                if inside(t, TILES):
                    wait(act, s["shift_done"], t + 1)
                    wait(act, s["pT_ready"], t)
                    for f in range(2):
                        half = slice(f * NB // 2, (f + 1) * NB // 2)
                        last = nc.scalar.activation(
                            prob[:, f * G:(f + 1) * G, :, :].rearrange("p g b k -> p b g k"),
                            shifted[:, half].rearrange("p (b g k) -> p b g k", b=B, g=G), ACT.Exp, scale=SCALE)
                    last.then_inc(s["exp_done"], 1)

            def copy_q(t):
                if inside(t, TILES):
                    wait(act, s["q_ready"], t + 1)
                    wait(act, s["qlo_done"], t)
                    wait(act, s["klo_done"], t)
                    wait(act, s["v_done"], 2 * t)
                    if rope:
                        wait(act, s["turned_done"], t)
                        wait(act, s["crossed_done"], 2 * t)
                    nc.scalar.copy(qkv[:, 0:DQ], bankB[:, 0:DQ]).then_inc(s["q_copied"], 1)

            def copy_kv(t):
                if inside(t, TILES):
                    wait(act, s["kv_ready"], t + 1)
                    nc.scalar.copy(qkv[:, DQ:DALL], bankC[:, 0:2 * DKV]).then_inc(s["kv_copied"], 1)

            def probs_hi(t):
                if inside(t, TILES):
                    wait(act, s["pT_ready"], t + 1)
                    wait(act, s["o_ready"], t)
                    nc.scalar.copy(pThi[:, :, :], bankS[:, 0:HKV * P].rearrange("p (h n) -> p h n", h=HKV))\
                        .then_inc(s["pThi_done"], 1)

            def y_hi(t):
                if inside(t, TILES):
                    wait(act, s["yT_ready"], t + 1)
                    wait(act, s["z_ready"], t)
                    nc.scalar.copy(yThi[:, :, :, :].rearrange("p r b q -> p b r q"),
                                   bankA[:, :].rearrange("p (b r q) -> p b r q", b=B, r=R))\
                        .then_inc(s["yThi_done"], 1)

            def qk_hi(t):
                if inside(t, TILES):
                    if rope:
                        wait(act, s["rot_done"], t + 1)
                    else:
                        wait(act, s["q_copied"], t + 1)
                        wait(act, s["kv_copied"], t + 1)
                    wait(act, s["kT_ready"], t)
                    src = rot if rope else qkv
                    nc.scalar.copy(qs[:, :, :, 0, :], src[:, 0:DQ].rearrange("p (h r d) -> p r h d", h=HKV, r=R))\
                        .then_inc(s["qhi_done"], 1)
                    nc.scalar.copy(kp[:, 0, :, :, :], src[:, DQ:DQ + DKV].rearrange("p (h d) -> p h d", h=HKV)
                                   .unsqueeze(2).broadcast_to([P, HKV, 2, D])).then_inc(s["khi_done"], 1)

            def step(k, u):
                n = 2 * k + u
                copy_qT(n)
                copy_kT(n)
                x_hi(n + 2, u)
                exps(n)
                copy_q(n + 1)
                probs_hi(n)
                copy_kv(n + 1)
                y_hi(n)
                qk_hi(n + 1)
            loop_pairs(act, step, FIRST, FROM, TO, LAST)

        @block.vector
        def _(dve):
            dve.memset(minus_half[:, :], -0.5).then_inc(set_up, 1)
            for i in range(4):
                dve.memset(kT[:, i // 2, i % 2, :, :, :], 0.0).then_inc(set_up, 1)
            dve.wait_ge(c_in, 16 * (7 if rope else 5))
            for u in range(2):
                nc.vector.tensor_copy(vhi[u][:, :, :, D], own[:, :].unsqueeze(1).broadcast_to([P, HKV, B]))\
                    .then_inc(set_up, 1)
            dve.memset(vlo[0][:, :, :, D], 0.0)
            dve.memset(vlo[1][:, :, :, D], 0.0).then_inc(set_up, 1)
            dve.wait_ge(w_hi, 1)
            nc.vector.tensor_tensor(wqkv[1][:, :, :], wstage[:, :].rearrange("p (j n) -> p j n", j=KT),
                                    wqkv[0][:, :, :], ALU.subtract).then_inc(w_ready, 1)
            dve.wait_ge(w_hi, 2)
            nc.vector.tensor_tensor(wo[1][:, :, :], wstage[:, 0:R * DM].rearrange("p (r n) -> p r n", r=R),
                                    wo[0][:, :, :], ALU.subtract).then_inc(w_ready, 1)

            def row_stats(t, u):
                if inside(t, TILES):
                    nc.vector.bn_stats(stats[u][:, :], hin[u][:, :]).then_inc(s["stats_done"], 1)

            def mean_variance(t, u):
                if inside(t, TILES):
                    wait_alone(dve, s["dve_passed"], s["stats_done"], t + 1)
                    nc.vector.bn_aggr(mv[u][:, :], stats[u][:, :]).then_inc(s["mv_done"], 1)

            def variance_eps(t, u):
                if inside(t, TILES):
                    wait(dve, s["mv_done"], t + 1)
                    nc.vector.tensor_scalar(veps[u][:, :], mv[u][:, 1:2], EPS, None, ALU.add)\
                        .then_inc(s["veps_done"], 1)

            def x_normalised(t, u):
                if inside(t, TILES):
                    wait(dve, s["rstd_done"], t + 1)
                    wait(dve, s["xT_ready"], t)
                    nc.vector.tensor_scalar(xn[:, :], hin[u][:, :], mv[u][:, 0:1], rstd[u][:, :],
                                            ALU.subtract, ALU.mult).then_inc(s["xn_done"], 1)

            def copy_kT(t):
                if inside(t, TILES):
                    wait(dve, s["kT_ready"], t + 1)
                    wait(dve, s["s_ready"], t)
                    for j in range(G // 2):
                        rows = slice(j * P // G, (j + 1) * P // G)
                        last = nc.vector.tensor_copy(kT[rows, :, :, :, j, :].rearrange("p a f b k -> p (a f b) k"),
                                                     kTp[rows, :].rearrange("p (n k) -> p n k", k=L))
                    last.then_inc(s["kT_dve"], 1)

            def residual(t, u, half):
                if inside(t, TILES):
                    wait(dve, s["z_ready"], t + 1)
                    wait(dve, res_in[u], 16 * (half + 1))
                    wait(dve, stored[u], 16 * half)
                    nc.vector.tensor_tensor(hout[u][:, :], bankB[:, :], hres[u][:, :], ALU.add)\
                        .then_inc(s["out_done"], 1)

            def maxes(t):
                if inside(t, TILES):
                    wait(dve, s["s_ready"], t + 1)
                    nc.vector.tensor_reduce(mx[:, :], S.rearrange("p (n k) -> p n k", k=L), AX.X, ALU.max)\
                        .then_inc(s["max_done"], 1)

            def shift(t):
                if inside(t, TILES):
                    wait(dve, s["max_done"], t + 1)
                    wait(dve, s["exp_done"], t)
                    nc.vector.tensor_tensor(shifted[:, :].rearrange("p (n k) -> p n k", k=L),
                                            S.rearrange("p (n k) -> p n k", k=L),
                                            mx[:, :].unsqueeze(2).broadcast_to([P, HKV * B, L]), ALU.subtract)\
                        .then_inc(s["shift_done"], 1)

            def x_lo(t, u):
                if inside(t, TILES):
                    wait(dve, s["xhi_done"], t + 1)
                    nc.vector.tensor_tensor(xlo[u][:, :, :], bankA[:, :].rearrange("p (j n) -> p j n", j=KT),
                                            xhi[u][:, :, :], ALU.subtract).then_inc(s["xlo_done"], 1)

            def probs_lo(t):
                if inside(t, TILES):
                    wait(dve, s["pThi_done"], t + 1)
                    nc.vector.tensor_tensor(pTlo[:, :, :], bankS[:, 0:HKV * P].rearrange("p (h n) -> p h n", h=HKV),
                                            pThi[:, :, :], ALU.subtract).then_inc(s["pTlo_done"], 1)

            def turn(t):
                if inside(t, TILES) and rope:
                    wait(dve, s["kv_copied"], t + 1)
                    wait(dve, s["q_copied"], t + 1)
                    n = (DQ + DKV) // 16
                    nc.vector.tensor_tensor(turned[:, :].rearrange("p (n d) -> p n d", d=16),
                                            qkv[:, 0:DQ + DKV].rearrange("p (n d) -> p n d", d=16),
                                            cos[:, :].unsqueeze(1).broadcast_to([P, n, 16]), ALU.mult)\
                        .then_inc(s["turned_done"], 1)

            def rotate(t):
                if inside(t, TILES) and rope:
                    wait(dve, s["turned_done"], t + 1)
                    wait(dve, s["crossed_done"], 2 * t + 2)
                    wait(dve, s["khi_done"], t)
                    nc.vector.tensor_tensor(rot[:, :], turned[:, :], crossed[:, :], ALU.add)\
                        .then_inc(s["rot_done"], 1)

            def inverse_sums(t):
                if inside(t, TILES):
                    wait(dve, s["o_ready"], t + 1)
                    nc.vector.reciprocal(rden[:, :, :, :].rearrange("p f g b -> p f (g b)"),
                                         bankO[:, :, 0:G * B * W].rearrange("p f (n w) -> p f n w", w=W)[:, :, :, D])\
                        .then_inc(s["rden_done"], 1)

            def normalise(t):
                if inside(t, TILES):
                    wait(dve, s["rden_done"], t + 1)
                    wait(dve, s["yT_ready"], t)
                    for f in range(2):
                        last = nc.vector.tensor_tensor(
                            y[:, :, f * G:(f + 1) * G, :].rearrange("p b g d -> p g b d"), O[:, f, :, :, 0:D],
                            rden[:, f, :, :].unsqueeze(3).broadcast_to([P, G, B, D]), ALU.mult)
                    last.then_inc(s["y_done"], 1)

            def y_lo(t):
                if inside(t, TILES):
                    wait(dve, s["yThi_done"], t + 1)
                    nc.vector.tensor_tensor(yTlo[:, :, :, :].rearrange("p r b q -> p b r q"),
                                            bankA[:, :].rearrange("p (b r q) -> p b r q", b=B, r=R),
                                            yThi[:, :, :, :].rearrange("p r b q -> p b r q"), ALU.subtract)\
                        .then_inc(s["yTlo_done"], 1)

            def qk_lo(t):
                if inside(t, TILES):
                    wait(dve, s["qhi_done"], t + 1)
                    src = rot if rope else qkv
                    nc.vector.tensor_tensor(qs[:, :, :, 1, :], src[:, 0:DQ].rearrange("p (h r d) -> p r h d", h=HKV, r=R),
                                            qs[:, :, :, 0, :], ALU.subtract).then_inc(s["qlo_done"], 1)
                    wait(dve, s["khi_done"], t + 1)
                    nc.vector.tensor_tensor(kp[:, 1, :, :, :], src[:, DQ:DQ + DKV].rearrange("p (h d) -> p h d", h=HKV)
                                            .unsqueeze(2).broadcast_to([P, HKV, 2, D]),
                                            kp[:, 0, :, :, :], ALU.subtract).then_inc(s["klo_done"], 1)

            def step(k, u):
                n = 2 * k + u
                copy_kT(n)
                if inside(n + 3, TILES):
                    wait(dve, h_in[1 - u], 16 * (k + (u + 3) // 2 + 1))
                row_stats(n + 3, 1 - u)
                residual(n - 1, 1 - u, k + (u - 1) // 2)
                mean_variance(n + 3, 1 - u)
                maxes(n)
                variance_eps(n + 3, 1 - u)
                shift(n)
                x_lo(n + 2, u)
                x_normalised(n + 3, 1 - u)
                probs_lo(n)
                turn(n + 1)
                inverse_sums(n)
                rotate(n + 1)
                normalise(n)
                y_lo(n)
                qk_lo(n + 1)
            loop_pairs(dve, step, FIRST, FROM, TO, LAST)

        @block.tensor
        def _(pe):
            pe.wait_ge(c_in, 16 * (7 if rope else 5))
            pe.wait_ge(set_up, 8)
            pe.wait_ge(w_ready, 2)

            def transpose_qk(t):
                if inside(t, TILES):
                    wait(pe, s["qlo_done"], t + 1)
                    wait(pe, s["qT_copied"], t)
                    for f in range(2):
                        for r in range(R):
                            at = (f * R + r) * P
                            last = nc.tensor.transpose(bankD[:, at:at + P],
                                                       qs[:, r, f * G:(f + 1) * G, :, :]
                                                       .rearrange("p g a d -> p (g a d)"), ident16[:, :])
                    last.then_inc(s["qT_ready"], 1)
                    wait(pe, s["klo_done"], t + 1)
                    wait(pe, s["kv_copied"], t + 1)
                    for a in range(2):
                        for f in range(2):
                            at = (a * 2 + f) * P
                            last = nc.tensor.transpose(kTp[:, at:at + P],
                                                       kp[:, a, f * G:(f + 1) * G, :, :]
                                                       .rearrange("p g e d -> p (g e d)"), ident16[:, :])
                    last.then_inc(s["kT_ready"], 1)

            def project_out(t):
                if inside(t, TILES):
                    wait(pe, s["yTlo_done"], t + 1)
                    wait(pe, s["q_copied"], t + 2 if not isinstance(t, int) else min(t + 2, TILES))
                    n = 0
                    for r in range(R):
                        hi, lo = (a[:, r, :, :].rearrange("p b q -> p (b q)") for a in (yThi, yTlo))
                        for a, w in ((hi, wo[0]), (hi, wo[1]), (lo, wo[0])):
                            last = nc.tensor.matmul(bankB[:, :], a, w[:, r, :], start=n == 0, stop=n == 3 * R - 1)
                            n += 1
                    last.then_inc(s["z_ready"], 1)

            def scores(t):
                if inside(t, TILES):
                    wait(pe, s["qT_copied"], t + 1)
                    wait(pe, s["kT_act"], t + 1)
                    wait(pe, s["pTlo_done"], t)
                    cols = NB // 2 // B
                    for i in range(SB):
                        span = slice(i * NB // SB, (i + 1) * NB // SB)
                        nc.tensor.matmul(S[:, span], select[:, :], bias[:, span], start=True, stop=False)
                        blocks = [(f, b) for f in range(2) for b in range(B)]
                        mine = blocks[i * len(blocks) // SB:(i + 1) * len(blocks) // SB]
                        for f, b in mine:
                            at = (f * B + b) * cols
                            for a in range(2):
                                last = nc.tensor.matmul(S[:, at:at + cols], qT[:, f, b, :, :].rearrange("p r q -> p (r q)"),
                                                        kT[:, a, f, b, :, :].rearrange("p g k -> p (g k)"),
                                                        start=False, stop=(f, b) == mine[-1] and a == 1)
                    last.then_inc(s["s_ready"], 1)

            def transpose_x(t):
                if inside(t, TILES):
                    wait(pe, s["xn_done"], t + 1)
                    wait(pe, s["yTlo_done"], t - 2)
                    for j in range(KT):
                        last = nc.tensor.transpose(bankA[:, j * P:(j + 1) * P], xn[:, j * P:(j + 1) * P], ident[:, :])
                    last.then_inc(s["xT_ready"], 1)

            def project(t, u, out, cols, done, free, used):
                if inside(t, TILES):
                    wait(pe, s["xlo_done"], t + 1)
                    wait(pe, s[free], used)
                    n = 0
                    for j in range(KT):
                        for a, w in ((xhi, wqkv[0]), (xhi, wqkv[1]), (xlo, wqkv[0])):
                            last = nc.tensor.matmul(out, a[u][:, j, :], w[:, j, cols], start=n == 0,
                                                    stop=n == 3 * KT - 1)
                            n += 1
                    last.then_inc(s[done], 1)

            def transpose_probs(t):
                if inside(t, TILES):
                    wait(pe, s["exp_done"], t + 1)
                    for h in range(HKV):
                        last = nc.tensor.transpose(bankS[:, h * P:(h + 1) * P],
                                                   prob[:, h, :, :].rearrange("p b k -> p (b k)"), ident[:, :])
                    last.then_inc(s["pT_ready"], 1)

            def weigh_values(t, u):
                if inside(t, TILES):
                    wait(pe, s["pTlo_done"], t + 1)
                    wait(pe, s["v_done"], 2 * t + 2)
                    wait(pe, s["y_done"], t)
                    for h in range(HKV):
                        out = bankO[:, h // G, (h % G) * B * W:(h % G + 1) * B * W]
                        for n, (p, v) in enumerate(((pThi, vhi), (pThi, vlo), (pTlo, vhi))):
                            last = nc.tensor.matmul(out, p[:, h, :], v[u][:, h, :, :].rearrange("p b w -> p (b w)"),
                                                    start=n == 0, stop=n == 2)
                    last.then_inc(s["o_ready"], 1)

            def transpose_y(t):
                if inside(t, TILES):
                    wait(pe, s["y_done"], t + 1)
                    wait(pe, s["xlo_done"], t + 3 if not isinstance(t, int) else min(t + 3, TILES))
                    for b in range(B):
                        last = nc.tensor.transpose(bankA[:, b * P:(b + 1) * P],
                                                   y[:, b, :, :].rearrange("p h d -> p (h d)"), ident[:, :])
                    last.then_inc(s["yT_ready"], 1)

            def step(k, u):
                n = 2 * k + u
                transpose_qk(n)
                project_out(n - 1)
                scores(n)
                transpose_x(n + 2)
                project(n + 1, 1 - u, bankB[:, 0:DQ], slice(0, DQ), "q_ready", "out_done", n)
                transpose_probs(n)
                project(n + 1, 1 - u, bankC[:, 0:2 * DKV], slice(DQ, DALL), "kv_ready", "kT_act", n + 1)
                weigh_values(n, u)
                transpose_y(n)
            loop_pairs(pe, step, FIRST, FROM, TO, LAST)
def ternary_weights(nc, sources, targets, scales, counts):
    P = 128
    with ExitStack() as ctx:
        sb = lambda name, shape, dt: ctx.enter_context(nc.sbuf_tensor("tw_" + name, shape, dt))
        sem = semaphores(nc, ctx, "tw_")
        N = max(t.shape[1] * t.shape[2] for t in targets)
        w = [sb(f"w{i}", [P, N], F32) for i in range(3)]
        below = sb("below", [P, N], F16)
        ones = sb("ones", [P, P], F32)
        rows = sb("rows", [P, 3], F32)
        bounds = sb("bounds", [P, 2, 3], F32)
        total = ctx.enter_context(nc.psum_tensor("tw_total", [P, 512], F32))
        cleared, arrived = sem("cleared"), [sem(f"arrived{i}") for i in range(3)]
        summed, totalled, bounded, below_done, done = (sem(n) for n in
                                                       ("summed", "totalled", "bounded", "below_done", "done"))
        block = ctx.enter_context(nc.Block())
        sizes = [t.shape[1] * t.shape[2] for t in targets]
        counts_in = []

        @block.sync
        def _(sp):
            for i, (src, target) in enumerate(zip(sources, targets)):
                K, M = src.shape
                full = K // P
                v = w[i][:, 0:sizes[i]].rearrange("p (j n) -> p j n", n=M)
                if K % P:
                    sp.wait_ge(cleared, 1)
                    sp.dma_start(v[0:K % P, full, :], src[full * P:K, :]).then_inc(arrived[i], 16)
                sp.dma_start(v[:, 0:full, :], src[0:full * P, :].rearrange("(j p) n -> p j n", p=P))\
                    .then_inc(arrived[i], 16)

        @block.tensor
        def _(pe):
            pe.wait_ge(summed, 3)
            pe.wait_ge(cleared, 2)
            nc.tensor.matmul(total[:, 0:3], ones[:, :], rows[:, :], start=True, stop=True).then_inc(totalled, 1)

        @block.vector
        def _(dve):
            K, M = sources[2].shape
            dve.memset(w[2][:, (K // P) * M:sizes[2]], 0.0).then_inc(cleared, 1)
            dve.memset(ones[:, :], 1.0).then_inc(cleared, 1)
            for i in range(3):
                dve.wait_ge(arrived[i], 32 if sources[i].shape[0] % P else 16)
                nc.vector.tensor_reduce(rows[:, i:i + 1], w[i][:, 0:sizes[i]], AX.X, ALU.add,
                                        apply_absolute_value=True).then_inc(summed, 1)
            dve.wait_ge(totalled, 1)
            for i in range(3):
                for sign, to in ((0.5, bounds[:, 0, i:i + 1]), (-0.5, bounds[:, 1, i:i + 1]),
                                 (1.0, scales[:, i:i + 1])):
                    nc.vector.tensor_scalar(to, total[:, i:i + 1], 1.0 / counts[i], sign, ALU.mult, ALU.mult)\
                        .then_inc(bounded, 1)
            dve.wait_ge(bounded, 9)
            for i in range(3):
                if i:
                    dve.wait_ge(done, i)
                nc.vector.tensor_scalar(below[:, 0:sizes[i]], w[i][:, 0:sizes[i]], bounds[:, 1, i:i + 1], None,
                                        ALU.is_lt).then_inc(below_done, 1)
                dve.wait_ge(below_done, i + 1)
                nc.vector.scalar_tensor_tensor(targets[i][:, :, :].rearrange("p j n -> p (j n)"),
                                               w[i][:, 0:sizes[i]], bounds[:, 0, i:i + 1], below[:, 0:sizes[i]],
                                               ALU.is_gt, ALU.subtract).then_inc(done, 1)


def fp4_weights(nc, packed, scales, targets, const):
    P, WORDS = 128, 16
    CH = 1408
    chunks = []
    for which, (words, _) in enumerate(zip(packed, scales)):
        K, M = words.shape[0] // WORDS, words.shape[1]
        if M > CH:
            chunks += [(which, j, 1, c) for j in range(K) for c in range(0, M, CH)]
        else:
            chunks += [(which, j, min(2, K - j), 0) for j in range(0, K, 2)]
    with ExitStack() as ctx:
        sb = lambda name, shape, dt: ctx.enter_context(nc.sbuf_tensor("fw_" + name, shape, dt))
        sem = semaphores(nc, ctx, "fw_")
        pair = lambda name, dt: [sb(f"{name}{i}", [P, CH], dt) for i in range(2)]
        shifts = sb("shifts", [P, 1], I32)
        words, scale = pair("words", I32), pair("scale", F16)
        nibble, code, sign = pair("nibble", I32), pair("code", I32), pair("sign", I32)
        half, double, signed, value = pair("half", F32), pair("double", F32), pair("signed", F32), pair("value", F32)
        c_in, in0, in1 = sem("c_in"), sem("in0"), sem("in1")
        arrived = (in0, in1)
        nib, codes, halves, doubles, signs, sscale, v1, v2, v3, hi, lo = (
            sem(n) for n in "nib codes halves doubles signs sscale v1 v2 v3 hi lo".split())
        block = ctx.enter_context(nc.Block())

        def views(n):
            which, j, rows, c = chunks[n]
            M = packed[which].shape[1]
            cols = min(CH, M)
            t = [x[:, j:j + rows, c:c + cols] for x in targets[which]]
            v = lambda x: x[n % 2][:, 0:rows * cols]
            return t, v, lambda a: a.rearrange("p (j n) -> p j n", j=rows)

        @block.sync
        def _(sp):
            sp.dma_start(shifts[:, :], const["shifts"]).then_inc(c_in, 16)
            for n, (which, j, rows, c) in enumerate(chunks):
                M = packed[which].shape[1]
                cols = min(CH, M)
                if n >= 2:
                    sp.wait_ge(nib, n - 1)
                    sp.wait_ge(sscale, n - 1)
                for r in range(rows):
                    at = (j + r) * WORDS
                    src = packed[which][at:at + WORDS, c:c + cols]
                    for w in range(WORDS):
                        sp.dma_start(words[n % 2][8 * w:8 * w + 8, r * cols:(r + 1) * cols],
                                     src[w:w + 1, :].broadcast_to([8, cols])).then_inc(arrived[n % 2], 16)
                    sp.dma_start(scale[n % 2][:, r * cols:(r + 1) * cols],
                                 scales[which][j + r:j + r + 1, c:c + cols].broadcast_to([P, cols]))\
                        .then_inc(arrived[n % 2], 16)

        arrivals = []
        total = [0, 0]
        for n, (_, _, rows, _) in enumerate(chunks):
            total[n % 2] += 16 * (WORDS + 1) * rows
            arrivals.append(total[n % 2])

        @block.vector
        def _(dve):
            dve.wait_ge(c_in, 16)

            def unpack(n):
                _, v, _ = views(n)
                dve.wait_ge(arrived[n % 2], arrivals[n])
                size = v(words).shape[1]
                nc.vector.tensor_tensor(v(nibble), v(words), shifts[:, :].broadcast_to([P, size]),
                                        ALU.logical_shift_right).then_inc(nib, 1)
                dve.wait_ge(nib, n + 1)
                if n >= 2:
                    dve.wait_ge(doubles, n - 1)
                    dve.wait_ge(halves, n - 1)
                    dve.wait_ge(signs, n - 1)
                nc.vector.tensor_scalar(v(code), v(nibble), 7, None, ALU.bitwise_and).then_inc(codes, 1)
                nc.vector.tensor_scalar(v(sign), v(nibble), 8, None, ALU.bitwise_and).then_inc(codes, 1)

            def combine(n):
                t, v, r = views(n)
                dve.wait_ge(halves, n + 1)
                nc.vector.scalar_tensor_tensor(v(value), v(code), -2.0, v(half), ALU.add, ALU.max).then_inc(v1, 1)
                dve.wait_ge(v1, n + 1)
                dve.wait_ge(doubles, n + 1)
                nc.vector.tensor_tensor(v(value), v(value), v(double), ALU.max).then_inc(v2, 1)
                dve.wait_ge(v2, n + 1)
                dve.wait_ge(sscale, n + 1)
                nc.vector.tensor_tensor(v(value), v(value), v(signed), ALU.mult).then_inc(v3, 1)
                dve.wait_ge(hi, n + 1)
                nc.vector.tensor_tensor(t[1], r(v(value)), t[0], ALU.subtract).then_inc(lo, 1)

            for n in range(len(chunks) + 1):
                if n < len(chunks):
                    unpack(n)
                if n:
                    combine(n - 1)

        @block.scalar
        def _(act):
            def prepare(n):
                _, v, _ = views(n)
                act.wait_ge(codes, 2 * n + 2)
                if n >= 2:
                    act.wait_ge(v2, n - 1)
                    act.wait_ge(v3, n - 1)
                nc.scalar.activation(v(half), v(code), ACT.Copy, scale=0.5).then_inc(halves, 1)
                nc.scalar.activation(v(double), v(code), ACT.Copy, scale=2.0, bias=-8.0).then_inc(doubles, 1)
                nc.scalar.activation(v(signed), v(sign), ACT.Copy, scale=-0.25, bias=1.0).then_inc(signs, 1)

            def high(n):
                t, v, r = views(n)
                act.wait_ge(v3, n + 1)
                nc.scalar.copy(t[0], r(v(value))).then_inc(hi, 1)

            for n in range(len(chunks) + 1):
                if n < len(chunks):
                    prepare(n)
                if n:
                    high(n - 1)

        @block.gpsimd
        def _(pool):
            for n in range(len(chunks)):
                _, v, _ = views(n)
                pool.wait_ge(signs, n + 1)
                pool.wait_ge(arrived[n % 2], arrivals[n])
                pool.tensor_tensor(v(signed), v(signed), v(scale), ALU.mult).then_inc(sscale, 1)


def feed_forward(nc, pre, h_dram, out_dram, gate, up, down, scales, const, HID, rms_out, GROUPS=8):
    P, DM, GT = 128, 512, 512
    KT, NT = DM // P, GT // P
    MT = (HID + P - 1) // P
    rows = [min(P, HID - m * P) for m in range(MT)]
    EPS, RMS_EPS = 1e-5, 1e-6
    TILES = GROUPS * NT
    assert MT % 2
    with ExitStack() as ctx:
        sb = lambda name, shape, dt: ctx.enter_context(nc.sbuf_tensor(pre + name, shape, dt))
        sem = semaphores(nc, ctx, pre)
        pair = lambda name, shape, dt: [sb(f"{name}{i}", shape, dt) for i in range(2)]
        ident, minus_half = sb("ident", [P, P], F32), sb("minus_half", [P, 1], F32)
        hin, hres, hout = pair("hin", [P, DM], F32), pair("hres", [P, DM], F32), pair("hout", [P, DM], F32)
        stats, mv, veps, rstd = (pair(n, [P, w], F32) for n, w in (("stats", 6), ("mv", 2), ("veps", 1), ("rstd", 1)))
        xn = sb("xn", [P, DM], F32)
        xhi, xlo = pair("xhi", [P, KT, GT], F16), pair("xlo", [P, KT, GT], F16)
        act_out, prod = pair("act_out", [P, GT], F32), pair("prod", [P, GT], F32)
        ghi, glo = pair("ghi", [P, MT, GT], F16), pair("glo", [P, MT, GT], F16)
        if rms_out:
            square, ssum, ms, rinv = pair("square", [P, DM], F32), pair("ssum", [P, 1], F32), pair("ms", [P, 1], F32), pair("rinv", [P, 1], F32)
        gu = [[ctx.enter_context(nc.psum_tensor(f"{pre}gu{i}{w}", [P, GT], F32)) for w in "gu"] for i in range(2)]
        px = ctx.enter_context(nc.psum_tensor(pre + "px", [P, KT * P], F32))
        pz = [ctx.enter_context(nc.psum_tensor(f"{pre}pz{i}", [P, DM], F32)) for i in range(2)]

        c_in, set_up = sem("c_in"), sem("set_up")
        h_in, res_in, stored = ([sem(f"{n}{i}") for i in range(2)] for n in ("h_in", "res_in", "stored"))
        names = ("stats_done mv_done veps_done rstd_done xn_done xT_ready xhi_done xlo_done gu_ready act_done "
                 "prod_done ghi_done glo_done z_ready out_done sp_passed dve_passed sq_done ms_done "
                 "rinv_done").split()
        s = {n: sem(n) for n in names}
        FIRST, FROM, TO, LAST = -1, 2, (GROUPS - 1) // 2 * 2, GROUPS + 1
        parts_x = [(x, w) for x in (0, 1) for w in range(len(gate)) if x + w < 2]
        xparts, gparts = (xhi, xlo), (ghi, glo)
        block = ctx.enter_context(nc.Block())

        norm_at = [2, 4, 6, 8]
        down_at = [0, 1, 2, 3]

        @block.sync
        def _(sp):
            sp.dma_start(ident[:, :], const["ident"]).then_inc(c_in, 16)

            def load(g, i):
                if inside(g, GROUPS):
                    t = NT * g + i
                    wait_alone(sp, s["sp_passed"], s["xn_done"], t - 1)
                    sp.dma_start(hin[i % 2][:, :], h_dram[bass.ds(t * P, P), :]).then_inc(h_in[i % 2], 16)

            def residual(g, i):
                if inside(g, GROUPS):
                    t = NT * g + i
                    wait_alone(sp, s["sp_passed"], s["out_done"], t - 1)
                    sp.dma_start(hres[i % 2][:, :], h_dram[bass.ds(t * P, P), :]).then_inc(res_in[i % 2], 16)

            def store(g, i):
                if inside(g, GROUPS):
                    t = NT * g + i
                    wait_alone(sp, s["sp_passed"], s["out_done"], t + 1)
                    sp.dma_start(out_dram[bass.ds(t * P, P), :], hout[i % 2][:, :]).then_inc(stored[i % 2], 16)

            def step(k, u):
                n = 2 * k + u
                residual(n - 1, 0)
                residual(n - 1, 1)
                load(n + 1, 0)
                load(n + 1, 1)
                store(n - 1, 0)
                residual(n - 1, 2)
                store(n - 1, 1)
                residual(n - 1, 3)
                store(n - 1, 2)
                store(n - 1, 3)
                load(n + 1, 2)
                load(n + 1, 3)
            loop_pairs(sp, step, FIRST, FROM, TO, LAST)
            for u in range(2):
                sp.wait_ge(stored[u], 16 * (TILES // 2))

        @block.gpsimd
        def _(pool):
            pool.wait_ge(set_up, 1)

            def inverse_deviation(g, i):
                if inside(g, GROUPS):
                    wait(pool, s["veps_done"], NT * g + i + 1)
                    pool.tensor_tensor(rstd[i % 2][:, :], veps[i % 2][:, :], minus_half[:, :], ALU.pow)\
                        .then_inc(s["rstd_done"], 1)

            def inverse_rms(g, i):
                if inside(g, GROUPS) and rms_out:
                    wait(pool, s["ms_done"], NT * g + i + 1)
                    pool.tensor_tensor(rinv[i % 2][:, :], ms[i % 2][:, :], minus_half[:, :], ALU.pow)\
                        .then_inc(s["rinv_done"], 1)

            def step(k, u):
                n = 2 * k + u
                for m in range(MT):
                    if m in norm_at:
                        inverse_deviation(n + 1, norm_at.index(m))
                    if m in down_at:
                        inverse_rms(n - 1, down_at.index(m))
            loop_pairs(pool, step, FIRST, FROM, TO, LAST)

        @block.scalar
        def _(act):
            def gate_act(g, m, u):
                if inside(g, GROUPS):
                    n = MT * g + m
                    wait(act, s["gu_ready"], n + 1)
                    wait(act, s["prod_done"], n - 1)
                    nc.scalar.activation(act_out[(m + u) % 2][0:rows[m], :], gu[(m + u) % 2][0][0:rows[m], :], ACT.Silu,
                                         scale=scales[0:rows[m], 0:1] if scales is not None else 1.0)\
                        .then_inc(s["act_done"], 1)

            def hidden_hi(g, m, u):
                if inside(g, GROUPS):
                    wait(act, s["prod_done"], MT * g + m + 1)
                    if m == 0:
                        wait(act, s["z_ready"], NT * (g - 1))
                    nc.scalar.copy(ghi[u][0:rows[m], m, :], prod[(m + u) % 2][0:rows[m], :])\
                        .then_inc(s["ghi_done"], 1)

            def x_hi(g, i, u):
                if inside(g, GROUPS):
                    wait(act, s["xT_ready"], NT * g + i + 1)
                    if i == 0:
                        wait(act, s["gu_ready"], MT * (g - 1))
                    nc.scalar.copy(xhi[u][:, :, i * P:(i + 1) * P], px[:, :].rearrange("p (j n) -> p j n", j=KT))\
                        .then_inc(s["xhi_done"], 1)

            def squares(g, i):
                if inside(g, GROUPS) and rms_out:
                    t = NT * g + i
                    wait(act, s["z_ready"], t + 1)
                    wait(act, s["sq_done"], t - 1)
                    nc.scalar.activation(square[i % 2][:, :], pz[i % 2][:, :], ACT.Square, accum_out=ssum[i % 2][:, :])\
                        .then_inc(s["sq_done"], 1)

            def step(k, u):
                n = 2 * k + u
                for m in range(MT):
                    gate_act(n, m, u)
                    if m:
                        hidden_hi(n, m - 1, u)
                    if m in down_at:
                        squares(n - 1, down_at.index(m))
                    if m in norm_at:
                        x_hi(n + 1, norm_at.index(m), 1 - u)
                hidden_hi(n, MT - 1, u)
            loop_pairs(act, step, FIRST, FROM, TO, LAST)

        @block.vector
        def _(dve):
            dve.memset(minus_half[:, :], -0.5).then_inc(set_up, 1)

            def hidden(g, m, u):
                if inside(g, GROUPS):
                    n = MT * g + m
                    r = slice(0, rows[m])
                    wait(dve, s["act_done"], n + 1)
                    wait(dve, s["glo_done"], n - 1)
                    if scales is not None:
                        nc.vector.scalar_tensor_tensor(prod[(m + u) % 2][r, :], gu[(m + u) % 2][1][r, :], scales[r, 1:2],
                                                       act_out[(m + u) % 2][r, :], ALU.mult, ALU.mult)\
                            .then_inc(s["prod_done"], 1)
                    else:
                        nc.vector.tensor_tensor(prod[(m + u) % 2][r, :], gu[(m + u) % 2][1][r, :], act_out[(m + u) % 2][r, :],
                                                ALU.mult).then_inc(s["prod_done"], 1)

            def hidden_lo(g, m, u):
                if inside(g, GROUPS):
                    wait(dve, s["ghi_done"], MT * g + m + 1)
                    r = slice(0, rows[m])
                    nc.vector.tensor_tensor(glo[u][r, m, :], prod[(m + u) % 2][r, :], ghi[u][r, m, :], ALU.subtract)\
                        .then_inc(s["glo_done"], 1)

            def row_stats(g, i, half):
                if inside(g, GROUPS):
                    t, u = NT * g + i, i % 2
                    wait_alone(dve, s["dve_passed"], h_in[u], 16 * (half + 1))
                    nc.vector.bn_stats(stats[u][:, :], hin[u][:, :]).then_inc(s["stats_done"], 1)
                    wait_alone(dve, s["dve_passed"], s["stats_done"], t + 1)
                    nc.vector.bn_aggr(mv[u][:, :], stats[u][:, :]).then_inc(s["mv_done"], 1)
                    wait(dve, s["mv_done"], t + 1)
                    nc.vector.tensor_scalar(veps[u][:, :], mv[u][:, 1:2], EPS, None, ALU.add)\
                        .then_inc(s["veps_done"], 1)

            def x_normalised(g, i):
                if inside(g, GROUPS):
                    t, u = NT * g + i, i % 2
                    wait(dve, s["rstd_done"], t + 1)
                    wait(dve, s["xT_ready"], t)
                    nc.vector.tensor_scalar(xn[:, :], hin[u][:, :], mv[u][:, 0:1], rstd[u][:, :],
                                            ALU.subtract, ALU.mult).then_inc(s["xn_done"], 1)

            def x_lo(g, i, u):
                if inside(g, GROUPS):
                    wait(dve, s["xhi_done"], NT * g + i + 1)
                    nc.vector.tensor_tensor(xlo[u][:, :, i * P:(i + 1) * P], px[:, :].rearrange("p (j n) -> p j n", j=KT),
                                            xhi[u][:, :, i * P:(i + 1) * P], ALU.subtract).then_inc(s["xlo_done"], 1)

            def mean_square(g, i):
                if inside(g, GROUPS) and rms_out:
                    wait(dve, s["sq_done"], NT * g + i + 1)
                    nc.vector.tensor_scalar(ms[i % 2][:, :], ssum[i % 2][:, :], 1.0 / DM, RMS_EPS, ALU.mult, ALU.add)\
                        .then_inc(s["ms_done"], 1)

            def output(g, i, half):
                if inside(g, GROUPS):
                    t, u = NT * g + i, i % 2
                    wait(dve, s["rinv_done" if rms_out else "z_ready"], t + 1)
                    wait(dve, res_in[u], 16 * (half + 1))
                    wait(dve, stored[u], 16 * half)
                    nc.vector.scalar_tensor_tensor(hout[u][:, :], pz[u][:, :],
                                                   rinv[u][:, :] if rms_out else scales[:, 2:3], hres[u][:, :],
                                                   ALU.mult, ALU.add).then_inc(s["out_done"], 1)

            def step(k, u):
                n = 2 * k + u
                for m in range(MT):
                    hidden(n, m, u)
                    if m in norm_at:
                        i = norm_at.index(m)
                        x_normalised(n + 1, i)
                    if m in down_at:
                        mean_square(n - 1, down_at.index(m))
                    if m:
                        hidden_lo(n, m - 1, u)
                    if m - 1 in down_at:
                        i = down_at.index(m - 1)
                        output(n - 1, i, 2 * (n - 1) + i // 2)
                    if m in norm_at:
                        x_lo(n + 1, norm_at.index(m), 1 - u)
                    if m + 1 in norm_at:
                        i = norm_at.index(m + 1)
                        row_stats(n + 1, i, 2 * (n + 1) + i // 2)
                hidden_lo(n, MT - 1, u)
            loop_pairs(dve, step, FIRST, FROM, TO, LAST)

        @block.tensor
        def _(pe):
            pe.wait_ge(c_in, 16)

            def gate_up(g, m, u):
                if inside(g, GROUPS):
                    n = MT * g + m
                    if m == 0:
                        wait(pe, s["xlo_done"], NT * (g + 1))
                    wait(pe, s["prod_done"], n - 1)
                    for which, weights in enumerate((gate, up)):
                        c = 0
                        for j in range(KT):
                            for x, w in parts_x:
                                last = nc.tensor.matmul(gu[(m + u) % 2][which][0:rows[m], :],
                                                        weights[w][:, j, m * P:m * P + rows[m]],
                                                        xparts[x][u][:, j, :], start=c == 0,
                                                        stop=c == KT * len(parts_x) - 1)
                                c += 1
                    last.then_inc(s["gu_ready"], 1)

            def transpose_x(g, i):
                if inside(g, GROUPS):
                    t = NT * g + i
                    wait(pe, s["xn_done"], t + 1)
                    wait(pe, s["xlo_done"], t)
                    for j in range(KT):
                        last = nc.tensor.transpose(px[:, j * P:(j + 1) * P], xn[:, j * P:(j + 1) * P], ident[:, :])
                    last.then_inc(s["xT_ready"], 1)

            def project(g, i, u):
                if inside(g, GROUPS):
                    t = NT * g + i
                    if i == 0:
                        wait(pe, s["glo_done"], MT * (g + 1))
                    wait(pe, s["out_done"], t - 1)
                    c = 0
                    for m in range(MT):
                        for x, w in parts_x:
                            last = nc.tensor.matmul(pz[i % 2][:, :], gparts[x][u][0:rows[m], m, i * P:(i + 1) * P],
                                                    down[w][0:rows[m], m, :], start=c == 0,
                                                    stop=c == MT * len(parts_x) - 1)
                            c += 1
                    last.then_inc(s["z_ready"], 1)

            def step(k, u):
                n = 2 * k + u
                for m in range(MT):
                    gate_up(n, m, u)
                    if m in down_at:
                        project(n - 1, down_at.index(m), 1 - u)
                    if m in norm_at:
                        transpose_x(n + 1, norm_at.index(m))
            loop_pairs(pe, step, FIRST, FROM, TO, LAST)
def three_bf16(a):
    parts, rest = [], np.asarray(a, np.float64)
    for _ in range(3):
        part = rest.astype(np.float32).astype(np.dtype("bfloat16"))
        parts.append(part)
        rest = rest - part.astype(np.float64)
    return parts


def constants():
    P, L, B = 128, 32, 4
    q, k = np.arange(L)[:, None], np.arange(L)[None, :]
    out = {"ident": np.eye(P, dtype=np.float32), "ident16": np.eye(P, dtype=np.float16)}
    row = np.arange(96)[:, None] % L
    out["select"] = (row == np.arange(P)[None, :] % L).astype(np.dtype("bfloat16"))
    out["own"] = (np.arange(P)[:, None] // L == np.arange(B)[None, :]).astype(np.float32)
    for pre, kv, d, slope in (("a0_", 8, 16, lambda h: 0.0), ("a1_", 4, 32, lambda h: np.float32(2 ** -0.5 * (2 ** -0.5) ** h))):
        table = np.zeros((96, 2, B, kv // 2, L), np.dtype("bfloat16"))
        for h in range(kv):
            full = np.where(k <= q, float(slope(h)) * (k - q) * float(d) ** 0.5, 0.0)
            for n, part in enumerate(three_bf16(full)):
                part = part.copy()
                if n == 0:
                    part[k + 0 * q > q] = -1e30
                table[n * L:(n + 1) * L, h // (kv // 2), :, h % (kv // 2), :] = part[:, None, :]
        out[pre + "bias"] = table.reshape(96, -1)
    out["shifts"] = np.ascontiguousarray((np.arange(P, dtype=np.int32)[:, None] % 8) * 4).astype(np.int32)
    inv = (np.float32(1.0) / np.power(np.float32(10000.0), np.arange(0, 16, 2, dtype=np.float32) / np.float32(16))).astype(np.float32)
    angle = np.outer(np.arange(L, dtype=np.float32), inv).astype(np.float32)
    angle = np.tile(angle, (B, 1))
    out["cos"] = np.repeat(np.cos(angle), 2, axis=1).astype(np.float32)
    out["sin"] = np.stack([-np.sin(angle), np.sin(angle)], axis=1).astype(np.float32)
    return out


_X = "x"
_OUT = (128, 32, 512)


def audio_tower(nc, x, weights, const, out):
    P, TOKENS, DM = 128, 4096, 512
    h = [nc.dram_tensor(f"h{i}", (TOKENS, DM), F32, kind="Internal").ap() for i in range(4)]
    y = out.rearrange("b s d -> (b s) d")
    token_mixer(nc, x, const["ident"], h[0])
    attention(nc, "a0_", h[0], h[1], weights["qkv0"], weights["o0"], const, 8, 16, True)
    with ExitStack() as ctx:
        sources = [weights[n] for n in ("w1", "w3", "w2")]
        tern = [ctx.enter_context(nc.sbuf_tensor(f"tern{i}", [P, (w.shape[0] + P - 1) // P, w.shape[1]], F16))
                for i, w in enumerate(sources)]
        scales = ctx.enter_context(nc.sbuf_tensor("tern_scales", [P, 3], F32))
        ternary_weights(nc, sources, tern, scales, [w.shape[0] * w.shape[1] for w in sources])
        feed_forward(nc, "f0_", h[1], h[2], [tern[0]], [tern[1]], [tern[2]], scales, const, sources[0].shape[1], False)
    attention(nc, "a1_", h[2], h[3], weights["qkv1"], weights["o1"], const, 4, 32, False)
    with ExitStack() as ctx:
        HID = weights["gu"].shape[1] // 2
        gu = [ctx.enter_context(nc.sbuf_tensor(f"gu{i}", [P, DM // P, 2 * HID], F16)) for i in range(2)]
        dn = [ctx.enter_context(nc.sbuf_tensor(f"dn{i}", [P, HID // P, DM], F16)) for i in range(2)]
        fp4_weights(nc, (weights["gu"], weights["dn"]), (weights["gu_scales"], weights["dn_scales"]), (gu, dn), const)
        feed_forward(nc, "f1_", h[3], y, [w[:, :, 0:HID] for w in gu], [w[:, :, HID:] for w in gu], dn, None,
                     const, HID, True)


def kernel(**inputs):
    import concourse.bacc as bacc
    from concourse.bass_utils import run_bass_kernel_spmd

    a = {k: np.asarray(v) for k, v in inputs.items()}

    def rows_by_repeat(w, heads, d):
        return w.reshape(heads, 4, d, 512).transpose(1, 0, 2, 3).reshape(512, 512)

    layouts = {
        "qkv0": np.concatenate([a["L0_attn_wq"], a["L0_attn_wk"], a["L0_attn_wv"]], axis=0).T,
        "o0": rows_by_repeat(a["L0_attn_wo"].T, 8, 16),
        "w1": a["L0_ffn_w1"].T, "w3": a["L0_ffn_w3"].T, "w2": a["L0_ffn_w2"].T,
        "qkv1": np.concatenate([a["L1_attn_Wq"], a["L1_attn_Wk"], a["L1_attn_Wv"]], axis=1),
        "o1": rows_by_repeat(a["L1_attn_Wo"], 4, 32),
        "gu": a["L1_ffn_gate_up_packed"].T, "gu_scales": a["L1_ffn_gate_up_scales"],
        "dn": a["L1_ffn_down_packed"].T, "dn_scales": a["L1_ffn_down_scales"],
    }
    tables = constants()
    nc = bacc.Bacc("TRN2", target_bir_lowering=False, num_devices=1)
    arrays = {"in_x": np.ascontiguousarray(a["x"])}
    arrays.update({f"in_{k}": np.ascontiguousarray(v) for k, v in layouts.items()})
    arrays.update({f"const_{k}": np.ascontiguousarray(v) for k, v in tables.items()})
    aps = {k: nc.dram_tensor(k, v.shape, mybir.dt.from_np(v.dtype), kind="ExternalInput").ap()
           for k, v in arrays.items()}
    out = nc.dram_tensor("out", _OUT, F32, kind="ExternalOutput").ap()
    audio_tower(nc, aps["in_x"], {k: aps[f"in_{k}"] for k in layouts}, {k: aps[f"const_{k}"] for k in tables}, out)
    r = run_bass_kernel_spmd(nc, [arrays], core_ids=[0])
    return r.results[0]["out"]
```

```python
import numpy as np
import concourse.bass as bass
from concourse import mybir
from contextlib import ExitStack

F32 = mybir.dt.float32
F16 = mybir.dt.float16
BF16 = mybir.dt.bfloat16
I32 = mybir.dt.int32
ALU = mybir.AluOpType
ACT = mybir.ActivationFunctionType
AX = mybir.AxisListType


def loop_pairs(eng, step, first, loop_from, loop_to, last):
    for n in range(first, loop_from):
        step(n // 2, n % 2)
    with eng.Fori(loop_from // 2, loop_to // 2) as k:
        step(k, 0)
        step(k, 1)
    for n in range(loop_to, last):
        step(n // 2, n % 2)


def wait(eng, sem, count):
    if not isinstance(count, int) or count > 0:
        eng.wait_ge(sem, count)


def wait_alone(eng, passed, sem, count):
    if not isinstance(count, int) or count > 0:
        eng.wait_ge(sem, count)
        if not isinstance(count, int):
            eng.sem_inc(passed, 1)


def semaphores(nc, ctx, prefix):
    made = []

    def make(name):
        made.append(nc.alloc_semaphore(prefix + name))
        return made[-1]

    def end():
        nc.clear_and_free_semaphores(made)
        nc.all_engine_barrier()
    ctx.callback(end)
    return make


def inside(t, tiles):
    return not isinstance(t, int) or 0 <= t < tiles


def token_mixer(nc, x, ident_dram, h_dram, SEQS=128):
    C, T = x.shape[1] // 3, x.shape[2]
    P = 128
    B = P // C
    NT = T // P
    TILES = SEQS // B
    SCALE = float(C) ** -0.5
    PARTS = 3
    KS = PARTS * C
    KM = KS + 2
    W = C + 1
    SLOTS = B * NT
    LEAD, LAG = 8, 12
    with ExitStack() as ctx:
        sb = lambda name, shape, dt: ctx.enter_context(nc.sbuf_tensor(name, shape, dt))
        sem = semaphores(nc, ctx, "")
        ident = sb("tm_ident", [P, P], F32)
        xqk = [sb(f"tm_xqk{i}", [P, 2, T], F32) for i in range(2)]
        xv = [sb(f"tm_xv{i}", [P, T], F32) for i in range(2)]
        xs = [sb(f"tm_xs{i}", [P, 4, T], F16) for i in range(2)]
        qk = [sb(f"tm_qk{i}", [P, 2, B, T], F16) for i in range(2)]
        v = [sb(f"tm_v{i}", [P, B, W], F32) for i in range(2)]
        vhi = [sb(f"tm_vhi{i}", [P, NT, B, W], F16) for i in range(2)]
        vlo = [sb(f"tm_vlo{i}", [P, NT, B, C], F16) for i in range(2)]
        negmax = [sb(f"tm_negmax{i}", [P, SLOTS], F32) for i in range(2)]
        mrow = sb("tm_mrow", [SLOTS, 2, P], F16)
        prob = [sb(f"tm_prob{i}", [P, NT, T], F32) for i in range(B)]
        phi = [sb(f"tm_phi{i}", [P, NT, T], F16) for i in range(B)]
        plo = [sb(f"tm_plo{i}", [P, NT, T], F16) for i in range(B)]
        rden = sb("tm_rden", [P, 2, 2, NT], F32)
        hT = [sb(f"tm_hT{i}", [P, NT, B, C], F32) for i in range(2)]
        htok = [sb(f"tm_htok{i}", [P, T], F32) for i in range(2)]
        s1 = ctx.enter_context(nc.psum_tensor("tm_s1", [P, 2, T], F32))
        s2 = ctx.enter_context(nc.psum_tensor("tm_s2", [P, 2, 2, T], F32))
        bankA = ctx.enter_context(nc.psum_tensor("tm_bankA", [P, 512], F32))
        bankB = ctx.enter_context(nc.psum_tensor("tm_bankB", [P, 512], F32))
        sums = [bank[:, 0:2 * NT * W].rearrange("p (b i w) -> p b i w", b=2, i=NT) for bank in (bankA, bankB)]
        vT = bankA[:, :].rearrange("p (j n) -> p j n", j=NT)
        tokT = bankB[:, :].rearrange("p (j n) -> p j n", j=NT)

        ident_in = sem("tm_ident_in")
        ones_set = sem("tm_ones_set")
        qk_in = [sem(f"tm_qk_in{i}") for i in range(2)]
        v_in = [sem(f"tm_v_in{i}") for i in range(2)]
        xhi_done, xlo_done = sem("tm_xhi_done"), sem("tm_xlo_done")
        phi_done = sem("tm_phi_done")
        plo_done, plo_pool = sem("tm_plo_done"), sem("tm_plo_pool")
        vlo_done = sem("tm_vlo_done")
        sp_passed, pool_passed = sem("tm_sp_passed"), sem("tm_pool_passed")
        stacked = [[sem(f"tm_stacked{u}{b}") for b in range(B)] for u in range(2)]
        vt_ready = sem("tm_vt_ready")
        v_ready = sem("tm_v_ready")
        s1_ready = sem("tm_s1_ready")
        max_done = sem("tm_max_done")
        mt_ready = sem("tm_mt_ready")
        mhi_done = sem("tm_mhi_done")
        mrow_done = sem("tm_mrow_done")
        mrow_in = sem("tm_mrow_in")
        s2_ready = sem("tm_s2_ready")
        exp_done = sem("tm_exp_done")
        pv_done = sem("tm_pv_done")
        rden_done = sem("tm_rden_done")
        norm_done = sem("tm_norm_done")
        htr_done = sem("tm_htr_done")
        htok_ready = sem("tm_htok_ready")
        stored = [sem(f"tm_stored{i}") for i in range(2)]

        FIRST, FROM, TO, LAST = -4, 4, (TILES - 3) // 2 * 2, TILES + 2
        VALUES_AT, TOKENS_AT, MAXIMA_AT = 6, 14, 10
        block = ctx.enter_context(nc.Block())

        @block.sync
        def _(sp):
            sp.dma_start(ident[:, :], ident_dram).then_inc(ident_in, 16)

            def load(t, u):
                if inside(t, TILES):
                    wait_alone(sp, sp_passed, xlo_done, t - 1)
                    for part in range(2):
                        sp.dma_start(xqk[u][:, part, :], x[bass.ds(t * B, B)][:, part * C:(part + 1) * C, :])\
                            .then_inc(qk_in[u], 16)

            def load_values(t, u):
                if inside(t, TILES):
                    wait_alone(sp, sp_passed, vt_ready, t - 1)
                    sp.dma_start(xv[u][:, :], x[bass.ds(t * B, B)][:, 2 * C:3 * C, :]).then_inc(v_in[u], 16)

            def store(t, u):
                if inside(t, TILES):
                    wait_alone(sp, sp_passed, htok_ready, t + 1)
                    sp.dma_start(h_dram[bass.ds(t * P, P), :], htok[u][:, :]).then_inc(stored[u], 16)

            def stack(t, u, b):
                if inside(t, TILES):
                    wait_alone(sp, sp_passed, xlo_done, t + 1)
                    wait_alone(sp, sp_passed, s2_ready, 8 * (t - 2) + 2 * b + 2)
                    c = slice(b * C, (b + 1) * C)
                    for g, (lo, hi) in enumerate(((0, 2), (0, 3), (1, 2))):
                        sp.dma_start(qk[u][g * C:(g + 1) * C, :, b, :],
                                     xs[u][c, lo:hi + 1:hi - lo, :]).then_inc(stacked[u][b], 16)

            def maxima(t, u):
                if inside(t, TILES):
                    wait_alone(sp, sp_passed, mrow_done, t + 1)
                    for part in range(2):
                        sp.dma_start(qk[u][KS + part:KS + part + 1, 0, :, :]
                                     .rearrange("o b (i t) -> o (b i) t", i=NT),
                                     mrow[:, part, :]).then_inc(mrow_in, 16)

            def step(k, u):
                n = 2 * k + u
                load(n + 4, u)
                load_values(n + 1, 1 - u)
                store(n - 2, u)
                stack(n + 2, u, 0)
                stack(n + 2, u, 1)
                maxima(n + 1, 1 - u)
                stack(n + 2, u, 2)
                stack(n + 2, u, 3)
            loop_pairs(sp, step, FIRST, FROM, TO, LAST)
            for u in range(2):
                sp.wait_ge(stored[u], 16 * (TILES // 2))

        @block.gpsimd
        def _(pool):
            def x_lo(t, u):
                if inside(t, TILES):
                    wait(pool, xhi_done, t + 1)
                    pool.tensor_tensor(xs[u][:, 1:4:2, :], xqk[u][:, :, :], xs[u][:, 0:4:2, :],
                                       ALU.subtract).then_inc(xlo_done, 1)

            def probs_lo(t, b):
                if inside(t, TILES):
                    wait(pool, phi_done, 8 * t + 2 * b + 1)
                    pool.tensor_tensor(plo[b][:, 1, :], prob[b][:, 1, :], phi[b][:, 1, :],
                                       ALU.subtract).then_inc(plo_pool, 1)

            def step(k, u):
                n = 2 * k + u
                for b in range(B):
                    if b == 1:
                        x_lo(n + 3, 1 - u)
                    probs_lo(n, b)
            loop_pairs(pool, step, FIRST, FROM, TO, LAST)

        @block.scalar
        def _(act):
            def x_hi(t, u, half):
                if inside(t, TILES):
                    wait(act, qk_in[u], 32 * (half + 1))
                    for b in range(B):
                        wait(act, stacked[u][b], 48 * half)
                    nc.scalar.copy(xs[u][:, 0:4:2, :], xqk[u][:, :, :]).then_inc(xhi_done, 1)

            def values_in(t, u):
                if inside(t, TILES):
                    wait(act, vt_ready, t + 1)
                    wait(act, pv_done, 4 * (t - 1))
                    if isinstance(t, int) and t < 2:
                        wait(act, ones_set, 6)
                    nc.scalar.copy(vhi[u][:, 1:NT, :, 0:C], vT[:, 1:NT, :].rearrange("p j (b c) -> p j b c", b=B))\
                        .then_inc(v_ready, 1)
                    nc.scalar.copy(v[u][:, :, 0:C], vT[:, 0, :].rearrange("p (b c) -> p b c", b=B))\
                        .then_inc(v_ready, 1)

            def exps(t, b, h):
                if inside(t, TILES):
                    wait(act, s2_ready, 8 * t + 2 * b + h + 1)
                    if h == 0:
                        wait(act, pv_done, 4 * (t - 1) + b + 1)
                    nc.scalar.activation(prob[b][:, 2 * h:2 * h + 2, :], s2[:, h, :, :], ACT.Exp,
                                         scale=SCALE).then_inc(exp_done, 1)

            def probs_hi(t, b, h):
                if inside(t, TILES):
                    tiles = slice(2, 4) if h else slice(1, 2)
                    wait(act, exp_done, 8 * t + 2 * b + h + 1)
                    nc.scalar.copy(phi[b][:, tiles, :], prob[b][:, tiles, :]).then_inc(phi_done, 1)

            def tokens_out(t, u, half):
                if inside(t, TILES):
                    wait(act, htr_done, t + 1)
                    wait(act, stored[u], 16 * half)
                    nc.scalar.copy(htok[u][:, :], bankB[:, :]).then_inc(htok_ready, 1)

            def step(k, u):
                n = 2 * k + u
                for b in range(B):
                    for h in range(2):
                        exps(n, b, h)
                        probs_hi(n, b, h)
                        if b == 1 and h == 0:
                            values_in(n, u)
                    if b == 0:
                        x_hi(n + 3, 1 - u, k + 1 + u)
                tokens_out(n - 1, 1 - u, k + (u - 1) // 2)
            loop_pairs(act, step, FIRST, FROM, TO, LAST)

        @block.vector
        def _(dve):
            for u in range(2):
                dve.memset(qk[u][KS:KM, 1, :, :], 1.0).then_inc(ones_set, 1)
                dve.memset(v[u][:, :, C:W], 1.0).then_inc(ones_set, 1)
                dve.memset(vhi[u][:, :, :, C:W], 1.0).then_inc(ones_set, 1)

            def maxes(t, u, m):
                if inside(t, TILES):
                    wait(dve, s1_ready, SLOTS * t + m + 1)
                    if m == 0:
                        wait(dve, mt_ready, t - 1)
                    nc.vector.tensor_reduce(negmax[u][:, m:m + 1], s1[:, m % 2, :], AX.X, ALU.max,
                                            negate=True).then_inc(max_done, 1)

            def probs_lo(t, b):
                if inside(t, TILES):
                    wait(dve, phi_done, 8 * t + 2 * b + 2)
                    nc.vector.tensor_tensor(plo[b][:, 2:4, :], prob[b][:, 2:4, :], phi[b][:, 2:4, :],
                                            ALU.subtract).then_inc(plo_done, 1)

            def values_lo(t, u):
                if inside(t, TILES):
                    wait(dve, v_ready, 2 * t + 2)
                    nc.vector.tensor_tensor(vlo[u][:, 1:NT, :, :], vT[:, 1:NT, :].rearrange("p j (b c) -> p j b c", b=B),
                                            vhi[u][:, 1:NT, :, 0:C], ALU.subtract).then_inc(vlo_done, 1)

            def maxima_parts(t):
                if inside(t, TILES):
                    wait(dve, mt_ready, t + 1)
                    wait(dve, mrow_in, 32 * t)
                    nc.vector.tensor_copy(mrow[:, 0, :], bankA[0:SLOTS, 0:P]).then_inc(mhi_done, 1)
                    wait(dve, mhi_done, t + 1)
                    nc.vector.tensor_tensor(mrow[:, 1, :], bankA[0:SLOTS, 0:P], mrow[:, 0, :],
                                            ALU.subtract).then_inc(mrow_done, 1)

            def inverse_sums(t, pair):
                if inside(t, TILES):
                    wait(dve, pv_done, 4 * t + 2 * pair + 2)
                    nc.vector.reciprocal(rden[:, pair, :, :], sums[pair][:, :, :, C]).then_inc(rden_done, 1)

            def normalise(t, u, pair):
                if inside(t, TILES):
                    wait(dve, rden_done, 2 * t + pair + 1)
                    if pair == 0:
                        wait(dve, htr_done, t - 1)
                    nc.vector.tensor_tensor(hT[u][:, :, 2 * pair:2 * pair + 2, :].rearrange("p i b c -> p b i c"),
                                            sums[pair][:, :, :, 0:C],
                                            rden[:, pair, :, :].unsqueeze(3).broadcast_to([P, 2, NT, C]),
                                            ALU.mult).then_inc(norm_done, 1)

            def step(k, u):
                n = 2 * k + u
                for g in range(SLOTS):
                    ahead, m = divmod(g + LEAD, SLOTS)
                    maxes(n + 1 + ahead, (u + 1 + ahead) % 2, m)
                    if g == 3:
                        probs_lo(n - 1, 3)
                    if g == LAG - SLOTS // 2:
                        inverse_sums(n - 1, 0)
                    if g == LAG - SLOTS // 2 + 1:
                        normalise(n - 1, 1 - u, 0)
                    if g == 7:
                        probs_lo(n, 0)
                    if g == VALUES_AT + 2:
                        values_lo(n, u)
                    if g == MAXIMA_AT + 1:
                        maxima_parts(n + 1)
                    if g == LAG:
                        inverse_sums(n - 1, 1)
                        probs_lo(n, 1)
                    if g == LAG + 1:
                        normalise(n - 1, 1 - u, 1)
                    if g == 15:
                        probs_lo(n, 2)
            loop_pairs(dve, step, FIRST, FROM, TO, LAST)

        @block.tensor
        def _(pe):
            pe.wait_ge(ident_in, 16)
            pe.wait_ge(ones_set, 6)

            def values_transposed(t, u, half):
                if inside(t, TILES):
                    wait(pe, v_in[u], 16 * (half + 1))
                    wait(pe, norm_done, 2 * t - 1)
                    for j in range(NT):
                        last = nc.tensor.transpose(vT[:, j, :], xv[u][:, j * P:(j + 1) * P], ident[:, :])
                    last.then_inc(vt_ready, 1)

            def scores_for_max(t, u, half, m):
                if inside(t, TILES):
                    b, i = divmod(m, NT)
                    if i == 0:
                        wait(pe, stacked[u][b], 48 * (half + 1))
                    wait(pe, max_done, SLOTS * t + m - 1)
                    nc.tensor.matmul(s1[:, m % 2, :], qk[u][0:KS, 0, b, i * P:(i + 1) * P],
                                     qk[u][0:KS, 1, b, :], start=True, stop=True).then_inc(s1_ready, 1)

            def scores(t, u, g):
                if inside(t, TILES):
                    b, j = divmod(g, NT)
                    if g == 0:
                        wait(pe, mrow_in, 32 * (t + 1))
                    if j % 2 == 0:
                        wait(pe, exp_done, 8 * t + 2 * b + j // 2 - 1)
                    last = nc.tensor.matmul(s2[:, j // 2, j % 2, :], qk[u][0:KM, 1, b, j * P:(j + 1) * P],
                                            qk[u][0:KM, 0, b, :], start=True, stop=True)
                    if j % 2 == 1:
                        last.then_inc(s2_ready, 1)

            def sum_values(t, u, q):
                if inside(t, TILES):
                    b, i = divmod(q, NT)
                    if i == 0:
                        wait(pe, plo_pool, 4 * t + b + 1)
                        wait(pe, plo_done, 4 * t + b + 1)
                        if b == 0:
                            wait(pe, vlo_done, t + 1)
                            wait(pe, mrow_done, min(t + 2, TILES) if isinstance(t, int) else t + 2)
                        elif b == 2:
                            wait(pe, htok_ready, t)
                    out = sums[b // 2][:, b % 2, i, :]
                    rows = slice(i * P, (i + 1) * P)
                    nc.tensor.matmul(out, prob[b][:, 0, rows], v[u][:, b, :], start=True, stop=False)
                    for j in range(1, NT):
                        hi, lo = phi[b][:, j, rows], plo[b][:, j, rows]
                        nc.tensor.matmul(out, hi, vhi[u][:, j, b, :], start=False, stop=False)
                        nc.tensor.matmul(out[:, 0:C], hi, vlo[u][:, j, b, :], start=False, stop=False)
                        last = nc.tensor.matmul(out, lo, vhi[u][:, j, b, :], start=False, stop=j == NT - 1)
                    if i == NT - 1:
                        last.then_inc(pv_done, 1)

            def tokens(t, u):
                if inside(t, TILES):
                    wait(pe, norm_done, 2 * t + 2)
                    for i in range(NT):
                        last = nc.tensor.transpose(tokT[:, i, :], hT[u][:, i, :, :].rearrange("p b c -> p (b c)"),
                                                   ident[:, :])
                    last.then_inc(htr_done, 1)

            def maxima(t, u):
                if inside(t, TILES):
                    wait(pe, max_done, SLOTS * (t + 1))
                    wait(pe, vlo_done, t)
                    nc.tensor.transpose(bankA[0:SLOTS, 0:P], negmax[u][:, :], ident[:, :]).then_inc(mt_ready, 1)

            def step(k, u):
                n = 2 * k + u
                for g in range(SLOTS):
                    ahead, m = divmod(g + LEAD, SLOTS)
                    scores_for_max(n + 1 + ahead, (u + 1 + ahead) % 2, k + (u + 1 + ahead) // 2, m)
                    scores(n, u, g)
                    if g < LAG:
                        sum_values(n - 1, 1 - u, SLOTS + g - LAG)
                    else:
                        sum_values(n, u, g - LAG)
                    if g == TOKENS_AT:
                        tokens(n - 1, 1 - u)
                    if g == MAXIMA_AT:
                        maxima(n + 1, 1 - u)
                    if g == VALUES_AT:
                        values_transposed(n, u, k)
            loop_pairs(pe, step, FIRST, FROM, TO, LAST)
def attention(nc, pre, h_dram, out_dram, wqkv_dram, wo_dram, const, HKV, D, rope, TILES=32):
    P, L, DM = 128, 32, 512
    R = 4
    B = P // L
    KT = DM // P
    G = HKV // 2
    DQ, DKV = R * HKV * D, HKV * D
    DALL = DQ + 2 * DKV
    NB = HKV * B * L
    SB = max(1, NB // 512)
    W = D + 1
    SCALE, EPS = float(D) ** -0.5, 1e-5
    with ExitStack() as ctx:
        sb = lambda name, shape, dt: ctx.enter_context(nc.sbuf_tensor(pre + name, shape, dt))
        sem = semaphores(nc, ctx, pre)
        ps = lambda name, shape, dt: ctx.enter_context(nc.psum_tensor(pre + name, shape, dt))
        pair = lambda name, shape, dt: [sb(f"{name}{i}", shape, dt) for i in range(2)]
        ident = sb("ident", [P, P], F32)
        ident16 = sb("ident16", [P, P], F16)
        select = sb("select", [96, P], BF16)
        bias = sb("bias", [96, NB], BF16)
        own = sb("own", [P, B], F32)
        minus_half = sb("minus_half", [P, 1], F32)
        wstage = sb("wstage", [P, KT * DALL], F32)
        wqkv = [sb(f"wqkv{i}", [P, KT, DALL], F16) for i in range(2)]
        wo = [sb(f"wo{i}", [P, R, DM], F16) for i in range(2)]
        if rope:
            cos = sb("cos", [P, 16], F32)
            sin = sb("sin", [P, 2, 8], F32)
            turned = sb("turned", [P, DQ + DKV], F32)
            crossed = sb("crossed", [P, DQ + DKV], F32)
            rot = sb("rot", [P, DQ + DKV], F32)
        hin, hres, hout = pair("hin", [P, DM], F32), pair("hres", [P, DM], F32), pair("hout", [P, DM], F32)
        stats, mv, rstd = pair("stats", [P, 6], F32), pair("mv", [P, 2], F32), pair("rstd", [P, 1], F32)
        veps = pair("veps", [P, 1], F32)
        xn = pair("xn", [P, DM], F32)
        xhi, xlo = pair("xhi", [P, KT, P], F16), pair("xlo", [P, KT, P], F16)
        qkv = pair("qkv", [P, DALL], F32)
        qs = sb("qs", [P, R, HKV, 2, D], F16)
        kp = sb("kp", [P, 2, HKV, 2, D], F16)
        v16, vrest = sb("v16", [P, DKV], F16), sb("vrest", [P, DKV], F32)
        vhi, vlo = pair("vhi", [P, HKV, B, W], F16), pair("vlo", [P, HKV, B, W], F16)
        qT = sb("qT", [P, 2, B, R, L], F16)
        kT = sb("kT", [P, 2, 2, B, G, L], F16)
        mx = sb("mx", [P, HKV * B], F32)
        shifted = sb("shifted", [P, NB], F32)
        prob = sb("prob", [P, HKV, B, L], F32)
        pThi, pTlo = sb("pThi", [P, HKV, P], F16), sb("pTlo", [P, HKV, P], F16)
        rden = sb("rden", [P, 2, G, B], F32)
        y = sb("y", [P, B, HKV, D], F32)
        yThi, yTlo = sb("yThi", [P, R, B, L], F16), sb("yTlo", [P, R, B, L], F16)

        bankA = ps("bankA", [P, 512], F32)
        bankB = ps("bankB", [P, 512], F32)
        bankC = ps("bankC", [P, 512], F32)
        bankD = ps("bankD", [P, 1024], F16)
        bankS = ps("bankS", [P, 1024], F32)
        bankO = ps("bankO", [P, 2, 512], F32)
        S = bankS[:, 0:NB]
        kTp = bankC[:, :].bitcast(F16)[:, 0:4 * P]
        O = bankO[:, :, 0:G * B * W].rearrange("p f (g b w) -> p f g b w", g=G, b=B)

        c_in, w_in, w_hi, w_ready = sem("c_in"), sem("w_in"), sem("w_hi"), sem("w_ready")
        set_up = sem("set_up")
        h_in = [sem(f"h_in{i}") for i in range(2)]
        res_in = [sem(f"res_in{i}") for i in range(2)]
        stored = [sem(f"stored{i}") for i in range(2)]
        names = ("stats_done mv_done veps_done rstd_done xn_done xT_ready xhi_done xlo_done q_ready kv_ready "
                 "q_copied kv_copied turned_done crossed_done rot_done qhi_done qlo_done khi_done klo_done "
                 "v16_done vrest_done v_done qT_ready kT_ready qT_copied kT_act kT_dve s_ready max_done "
                 "shift_done exp_done pT_ready pThi_done pTlo_done o_ready rden_done y_done yT_ready "
                 "yThi_done yTlo_done z_ready out_done sp_passed pool_passed dve_passed").split()
        s = {n: sem(n) for n in names}

        FIRST, FROM, TO, LAST = -5, 4, (TILES - 5) // 2 * 2, TILES + 2
        block = ctx.enter_context(nc.Block())

        @block.sync
        def _(sp):
            consts = [(ident, "ident"), (ident16, "ident16"), (select, "select"), (bias, pre + "bias"),
                      (own, "own")]
            if rope:
                consts += [(cos, "cos"), (sin, "sin")]
            for dst, name in consts:
                sp.dma_start(dst[:], const[name]).then_inc(c_in, 16)
            sp.dma_start(wstage[:, :].rearrange("p (j n) -> p j n", j=KT),
                         wqkv_dram.rearrange("(j p) n -> p j n", p=P)).then_inc(w_in, 16)
            sp.wait_ge(w_ready, 1)
            sp.dma_start(wstage[:, 0:R * DM].rearrange("p (r n) -> p r n", r=R),
                         wo_dram.rearrange("(r p) n -> p r n", p=P)).then_inc(w_in, 16)

            def load(t, u):
                if inside(t, TILES):
                    wait_alone(sp, s["sp_passed"], s["xn_done"], t - 1)
                    sp.dma_start(hin[u][:, :], h_dram[bass.ds(t * P, P), :]).then_inc(h_in[u], 16)

            def load_residual(t, u):
                if inside(t, TILES):
                    wait_alone(sp, s["sp_passed"], s["out_done"], t - 1)
                    sp.dma_start(hres[u][:, :], h_dram[bass.ds(t * P, P), :]).then_inc(res_in[u], 16)

            def store(t, u):
                if inside(t, TILES):
                    wait_alone(sp, s["sp_passed"], s["out_done"], t + 1)
                    sp.dma_start(out_dram[bass.ds(t * P, P), :], hout[u][:, :]).then_inc(stored[u], 16)

            def step(k, u):
                n = 2 * k + u
                load(n + 5, 1 - u)
                store(n - 2, u)
                load_residual(n, u)
            loop_pairs(sp, step, FIRST, FROM, TO, LAST)
            for u in range(2):
                sp.wait_ge(stored[u], 16 * (TILES // 2))

        @block.gpsimd
        def _(pool):
            pool.wait_ge(c_in, 16 * (7 if rope else 5))
            pool.wait_ge(set_up, 8)

            def inverse_deviation(t, u):
                if inside(t, TILES):
                    wait(pool, s["veps_done"], t + 1)
                    pool.tensor_tensor(rstd[u][:, :], veps[u][:, :], minus_half[:, :], ALU.pow)\
                        .then_inc(s["rstd_done"], 1)

            def cross(t, u, part):
                if inside(t, TILES) and rope:
                    wait_alone(pool, s["pool_passed"], s[("q_copied", "kv_copied")[part]], t + 1)
                    if part == 0:
                        wait_alone(pool, s["pool_passed"], s["rot_done"], t)
                    cols = (slice(0, DQ), slice(DQ, DQ + DKV))[part]
                    n = (DQ, DKV)[part] // 16
                    src = qkv[u][:, cols].rearrange("p (h i e) -> p h i e", e=2, i=8)
                    dst = crossed[:, cols].rearrange("p (h i e) -> p h i e", e=2, i=8)
                    for e in range(2):
                        pool.tensor_tensor(dst[:, :, :, e], src[:, :, :, 1 - e],
                                           sin[:, e, :].unsqueeze(1).broadcast_to([P, n, 8]),
                                           ALU.mult).then_inc(s["crossed_done"], 1)

            def values(t, u):
                if inside(t, TILES):
                    wait_alone(pool, s["pool_passed"], s["kv_copied"], t + 1)
                    wait_alone(pool, s["pool_passed"], s["o_ready"], t - 1)
                    v = qkv[u][:, DQ + DKV:DALL]
                    spread = lambda a: a.rearrange("p (h d) -> p h d", h=HKV).unsqueeze(2)\
                        .broadcast_to([P, HKV, B, D])
                    mask = own[:, :].unsqueeze(1).unsqueeze(3).broadcast_to([P, HKV, B, D])
                    pool.tensor_copy(v16[:, :], v).then_inc(s["v16_done"], 1)
                    pool.tensor_tensor(vhi[u][:, :, :, 0:D], spread(v), mask, ALU.mult).then_inc(s["v_done"], 1)
                    wait_alone(pool, s["pool_passed"], s["v16_done"], t + 1)
                    pool.tensor_tensor(vrest[:, :], v, v16[:, :], ALU.subtract).then_inc(s["vrest_done"], 1)
                    wait_alone(pool, s["pool_passed"], s["vrest_done"], t + 1)
                    pool.tensor_tensor(vlo[u][:, :, :, 0:D], spread(vrest[:, :]), mask, ALU.mult)\
                        .then_inc(s["v_done"], 1)

            def step(k, u):
                n = 2 * k + u
                values(n + 1, 1 - u)
                inverse_deviation(n + 4, u)
                cross(n + 2, u, 0)
                cross(n + 2, u, 1)
            loop_pairs(pool, step, FIRST, FROM, TO, LAST)

        @block.scalar
        def _(act):
            act.wait_ge(w_in, 16)
            nc.scalar.copy(wqkv[0][:, :, :], wstage[:, :].rearrange("p (j n) -> p j n", j=KT)).then_inc(w_hi, 1)
            act.wait_ge(w_in, 32)
            nc.scalar.copy(wo[0][:, :, :], wstage[:, 0:R * DM].rearrange("p (r n) -> p r n", r=R)).then_inc(w_hi, 1)
            act.wait_ge(set_up, 8)

            def copy_qT(t):
                if inside(t, TILES):
                    wait(act, s["qT_ready"], t + 1)
                    wait(act, s["s_ready"], t)
                    for f in range(2):
                        last = nc.scalar.copy(qT[:, f, :, :, :].rearrange("p b r q -> p r b q"),
                                              bankD[:, f * R * P:(f + 1) * R * P]
                                              .rearrange("p (r b q) -> p r b q", r=R, b=B))
                    last.then_inc(s["qT_copied"], 1)

            def copy_kT(t):
                if inside(t, TILES):
                    wait(act, s["kT_dve"], t + 1)
                    for j in range(G // 2, G):
                        rows = slice(j * P // G, (j + 1) * P // G)
                        last = nc.scalar.copy(kT[rows, :, :, :, j, :].rearrange("p a f b k -> p (a f b) k"),
                                              kTp[rows, :].rearrange("p (n k) -> p n k", k=L))
                    last.then_inc(s["kT_act"], 1)

            def x_hi(t, u):
                if inside(t, TILES):
                    wait(act, s["xT_ready"], t + 1)
                    wait(act, s["kv_ready"], t - 1)
                    nc.scalar.copy(xhi[u][:, :, :], bankA[:, :].rearrange("p (j n) -> p j n", j=KT))\
                        .then_inc(s["xhi_done"], 1)

            def exps(t):
                if inside(t, TILES):
                    wait(act, s["shift_done"], t + 1)
                    wait(act, s["pT_ready"], t)
                    for f in range(2):
                        half = slice(f * NB // 2, (f + 1) * NB // 2)
                        last = nc.scalar.activation(
                            prob[:, f * G:(f + 1) * G, :, :].rearrange("p g b k -> p b g k"),
                            shifted[:, half].rearrange("p (b g k) -> p b g k", b=B, g=G), ACT.Exp, scale=SCALE)
                    last.then_inc(s["exp_done"], 1)

            def copy_q(t, u):
                if inside(t, TILES):
                    wait(act, s["q_ready"], t + 1)
                    wait(act, s["klo_done"], t - 1)
                    wait(act, s["v_done"], 2 * (t - 1))
                    nc.scalar.copy(qkv[u][:, 0:DQ], bankB[:, 0:DQ]).then_inc(s["q_copied"], 1)

            def copy_kv(t, u):
                if inside(t, TILES):
                    wait(act, s["kv_ready"], t + 1)
                    nc.scalar.copy(qkv[u][:, DQ:DALL], bankC[:, 0:2 * DKV]).then_inc(s["kv_copied"], 1)

            def probs_hi(t):
                if inside(t, TILES):
                    wait(act, s["pT_ready"], t + 1)
                    wait(act, s["o_ready"], t)
                    nc.scalar.copy(pThi[:, :, :], bankS[:, 0:HKV * P].rearrange("p (h n) -> p h n", h=HKV))\
                        .then_inc(s["pThi_done"], 1)

            def y_hi(t):
                if inside(t, TILES):
                    wait(act, s["yT_ready"], t + 1)
                    wait(act, s["z_ready"], t)
                    nc.scalar.copy(yThi[:, :, :, :].rearrange("p r b q -> p b r q"),
                                   bankA[:, :].rearrange("p (b r q) -> p b r q", b=B, r=R))\
                        .then_inc(s["yThi_done"], 1)

            def qk_hi(t, u):
                if inside(t, TILES):
                    if rope:
                        wait(act, s["rot_done"], t + 1)
                    else:
                        wait(act, s["q_copied"], t + 1)
                        wait(act, s["kv_copied"], t + 1)
                    wait(act, s["kT_ready"], t)
                    src = rot if rope else qkv[u]
                    nc.scalar.copy(qs[:, :, :, 0, :], src[:, 0:DQ].rearrange("p (h r d) -> p r h d", h=HKV, r=R))\
                        .then_inc(s["qhi_done"], 1)
                    nc.scalar.copy(kp[:, 0, :, :, :], src[:, DQ:DQ + DKV].rearrange("p (h d) -> p h d", h=HKV)
                                   .unsqueeze(2).broadcast_to([P, HKV, 2, D])).then_inc(s["khi_done"], 1)

            def step(k, u):
                n = 2 * k + u
                copy_qT(n + 1)
                copy_kT(n + 1)
                if rope:
                    copy_q(n + 2, u)
                exps(n)
                y_hi(n - 1)
                if not rope:
                    copy_q(n + 2, u)
                copy_kv(n + 2, u)
                probs_hi(n)
                qk_hi(n + 2, u)
                x_hi(n + 3, 1 - u)
            loop_pairs(act, step, FIRST, FROM, TO, LAST)

        @block.vector
        def _(dve):
            dve.memset(minus_half[:, :], -0.5).then_inc(set_up, 1)
            for i in range(4):
                dve.memset(kT[:, i // 2, i % 2, :, :, :], 0.0).then_inc(set_up, 1)
            dve.wait_ge(c_in, 16 * (7 if rope else 5))
            for u in range(2):
                nc.vector.tensor_copy(vhi[u][:, :, :, D], own[:, :].unsqueeze(1).broadcast_to([P, HKV, B]))\
                    .then_inc(set_up, 1)
            dve.memset(vlo[0][:, :, :, D], 0.0)
            dve.memset(vlo[1][:, :, :, D], 0.0).then_inc(set_up, 1)
            dve.wait_ge(w_hi, 1)
            nc.vector.tensor_tensor(wqkv[1][:, :, :], wstage[:, :].rearrange("p (j n) -> p j n", j=KT),
                                    wqkv[0][:, :, :], ALU.subtract).then_inc(w_ready, 1)
            dve.wait_ge(w_hi, 2)
            nc.vector.tensor_tensor(wo[1][:, :, :], wstage[:, 0:R * DM].rearrange("p (r n) -> p r n", r=R),
                                    wo[0][:, :, :], ALU.subtract).then_inc(w_ready, 1)

            def row_stats(t, u):
                if inside(t, TILES):
                    nc.vector.bn_stats(stats[u][:, :], hin[u][:, :]).then_inc(s["stats_done"], 1)

            def mean_variance(t, u):
                if inside(t, TILES):
                    wait_alone(dve, s["dve_passed"], s["stats_done"], t + 1)
                    nc.vector.bn_aggr(mv[u][:, :], stats[u][:, :]).then_inc(s["mv_done"], 1)

            def variance_eps(t, u):
                if inside(t, TILES):
                    wait(dve, s["mv_done"], t + 1)
                    nc.vector.tensor_scalar(veps[u][:, :], mv[u][:, 1:2], EPS, None, ALU.add)\
                        .then_inc(s["veps_done"], 1)

            def x_normalised(t, u):
                if inside(t, TILES):
                    wait(dve, s["rstd_done"], t + 1)
                    wait(dve, s["xT_ready"], t - 1)
                    nc.vector.tensor_scalar(xn[u][:, :], hin[u][:, :], mv[u][:, 0:1], rstd[u][:, :],
                                            ALU.subtract, ALU.mult).then_inc(s["xn_done"], 1)

            def copy_kT(t):
                if inside(t, TILES):
                    wait(dve, s["kT_ready"], t + 1)
                    wait(dve, s["s_ready"], t)
                    for j in range(G // 2):
                        rows = slice(j * P // G, (j + 1) * P // G)
                        last = nc.vector.tensor_copy(kT[rows, :, :, :, j, :].rearrange("p a f b k -> p (a f b) k"),
                                                     kTp[rows, :].rearrange("p (n k) -> p n k", k=L))
                    last.then_inc(s["kT_dve"], 1)

            def residual(t, u, half):
                if inside(t, TILES):
                    wait(dve, s["z_ready"], t + 1)
                    wait(dve, res_in[u], 16 * (half + 1))
                    wait(dve, stored[u], 16 * half)
                    nc.vector.tensor_tensor(hout[u][:, :], bankB[:, :], hres[u][:, :], ALU.add)\
                        .then_inc(s["out_done"], 1)

            def maxes(t):
                if inside(t, TILES):
                    wait(dve, s["s_ready"], t + 1)
                    nc.vector.tensor_reduce(mx[:, :], S.rearrange("p (n k) -> p n k", k=L), AX.X, ALU.max)\
                        .then_inc(s["max_done"], 1)

            def shift(t):
                if inside(t, TILES):
                    wait(dve, s["max_done"], t + 1)
                    wait(dve, s["exp_done"], t)
                    nc.vector.tensor_tensor(shifted[:, :].rearrange("p (n k) -> p n k", k=L),
                                            S.rearrange("p (n k) -> p n k", k=L),
                                            mx[:, :].unsqueeze(2).broadcast_to([P, HKV * B, L]), ALU.subtract)\
                        .then_inc(s["shift_done"], 1)

            def x_lo(t, u):
                if inside(t, TILES):
                    wait(dve, s["xhi_done"], t + 1)
                    nc.vector.tensor_tensor(xlo[u][:, :, :], bankA[:, :].rearrange("p (j n) -> p j n", j=KT),
                                            xhi[u][:, :, :], ALU.subtract).then_inc(s["xlo_done"], 1)

            def probs_lo(t):
                if inside(t, TILES):
                    wait(dve, s["pThi_done"], t + 1)
                    nc.vector.tensor_tensor(pTlo[:, :, :], bankS[:, 0:HKV * P].rearrange("p (h n) -> p h n", h=HKV),
                                            pThi[:, :, :], ALU.subtract).then_inc(s["pTlo_done"], 1)

            def turn(t, u, part):
                if inside(t, TILES) and rope:
                    wait(dve, s[("q_copied", "kv_copied")[part]], t + 1)
                    cols = (slice(0, DQ), slice(DQ, DQ + DKV))[part]
                    n = (DQ, DKV)[part] // 16
                    nc.vector.tensor_tensor(turned[:, cols].rearrange("p (n d) -> p n d", d=16),
                                            qkv[u][:, cols].rearrange("p (n d) -> p n d", d=16),
                                            cos[:, :].unsqueeze(1).broadcast_to([P, n, 16]), ALU.mult)\
                        .then_inc(s["turned_done"], 1)

            def rotate(t):
                if inside(t, TILES) and rope:
                    wait(dve, s["turned_done"], 2 * t + 2)
                    wait(dve, s["crossed_done"], 4 * t + 4)
                    wait(dve, s["khi_done"], t)
                    nc.vector.tensor_tensor(rot[:, :], turned[:, :], crossed[:, :], ALU.add)\
                        .then_inc(s["rot_done"], 1)

            def inverse_sums(t):
                if inside(t, TILES):
                    wait(dve, s["o_ready"], t + 1)
                    nc.vector.reciprocal(rden[:, :, :, :].rearrange("p f g b -> p f (g b)"),
                                         bankO[:, :, 0:G * B * W].rearrange("p f (n w) -> p f n w", w=W)[:, :, :, D])\
                        .then_inc(s["rden_done"], 1)

            def normalise(t):
                if inside(t, TILES):
                    wait(dve, s["rden_done"], t + 1)
                    wait(dve, s["yT_ready"], t)
                    for f in range(2):
                        last = nc.vector.tensor_tensor(
                            y[:, :, f * G:(f + 1) * G, :].rearrange("p b g d -> p g b d"), O[:, f, :, :, 0:D],
                            rden[:, f, :, :].unsqueeze(3).broadcast_to([P, G, B, D]), ALU.mult)
                    last.then_inc(s["y_done"], 1)

            def y_lo(t):
                if inside(t, TILES):
                    wait(dve, s["yThi_done"], t + 1)
                    nc.vector.tensor_tensor(yTlo[:, :, :, :].rearrange("p r b q -> p b r q"),
                                            bankA[:, :].rearrange("p (b r q) -> p b r q", b=B, r=R),
                                            yThi[:, :, :, :].rearrange("p r b q -> p b r q"), ALU.subtract)\
                        .then_inc(s["yTlo_done"], 1)

            def qk_lo(t, u):
                if inside(t, TILES):
                    wait(dve, s["qhi_done"], t + 1)
                    src = rot if rope else qkv[u]
                    nc.vector.tensor_tensor(qs[:, :, :, 1, :], src[:, 0:DQ].rearrange("p (h r d) -> p r h d", h=HKV, r=R),
                                            qs[:, :, :, 0, :], ALU.subtract).then_inc(s["qlo_done"], 1)
                    wait(dve, s["khi_done"], t + 1)
                    nc.vector.tensor_tensor(kp[:, 1, :, :, :], src[:, DQ:DQ + DKV].rearrange("p (h d) -> p h d", h=HKV)
                                            .unsqueeze(2).broadcast_to([P, HKV, 2, D]),
                                            kp[:, 0, :, :, :], ALU.subtract).then_inc(s["klo_done"], 1)

            def step(k, u):
                n = 2 * k + u
                residual(n - 2, u, k - 1)
                maxes(n)
                copy_kT(n + 1)
                inverse_sums(n - 1)
                normalise(n - 1)
                shift(n)
                if inside(n + 4, TILES):
                    wait(dve, h_in[u], 16 * (k + 3))
                row_stats(n + 4, u)
                mean_variance(n + 4, u)
                variance_eps(n + 4, u)
                turn(n + 2, u, 0)
                x_normalised(n + 4, u)
                y_lo(n - 1)
                turn(n + 2, u, 1)
                rotate(n + 2)
                probs_lo(n)
                qk_lo(n + 2, u)
                x_lo(n + 3, 1 - u)
            loop_pairs(dve, step, FIRST, FROM, TO, LAST)

        @block.tensor
        def _(pe):
            pe.wait_ge(c_in, 16 * (7 if rope else 5))
            pe.wait_ge(set_up, 8)
            pe.wait_ge(w_ready, 2)

            def transpose_qk(t):
                if inside(t, TILES):
                    wait(pe, s["qlo_done"], t + 1)
                    wait(pe, s["qT_copied"], t)
                    for f in range(2):
                        for r in range(R):
                            at = (f * R + r) * P
                            last = nc.tensor.transpose(bankD[:, at:at + P],
                                                       qs[:, r, f * G:(f + 1) * G, :, :]
                                                       .rearrange("p g a d -> p (g a d)"), ident16[:, :])
                    last.then_inc(s["qT_ready"], 1)
                    wait(pe, s["klo_done"], t + 1)
                    wait(pe, s["kv_copied"], t + 1)
                    for a in range(2):
                        for f in range(2):
                            at = (a * 2 + f) * P
                            last = nc.tensor.transpose(kTp[:, at:at + P],
                                                       kp[:, a, f * G:(f + 1) * G, :, :]
                                                       .rearrange("p g e d -> p (g e d)"), ident16[:, :])
                    last.then_inc(s["kT_ready"], 1)

            def project_out(t):
                if inside(t, TILES):
                    wait(pe, s["yTlo_done"], t + 1)
                    wait(pe, s["q_copied"], t + 4 if not isinstance(t, int) else min(t + 4, TILES))
                    n = 0
                    for r in range(R):
                        hi, lo = (a[:, r, :, :].rearrange("p b q -> p (b q)") for a in (yThi, yTlo))
                        for a, w in ((hi, wo[0]), (hi, wo[1]), (lo, wo[0])):
                            last = nc.tensor.matmul(bankB[:, :], a, w[:, r, :], start=n == 0, stop=n == 3 * R - 1)
                            n += 1
                    last.then_inc(s["z_ready"], 1)

            def scores(t):
                if inside(t, TILES):
                    wait(pe, s["qT_copied"], t + 1)
                    wait(pe, s["kT_act"], t + 1)
                    wait(pe, s["pTlo_done"], t)
                    cols = NB // 2 // B
                    for i in range(SB):
                        span = slice(i * NB // SB, (i + 1) * NB // SB)
                        nc.tensor.matmul(S[:, span], select[:, :], bias[:, span], start=True, stop=False)
                        blocks = [(f, b) for f in range(2) for b in range(B)]
                        mine = blocks[i * len(blocks) // SB:(i + 1) * len(blocks) // SB]
                        for f, b in mine:
                            at = (f * B + b) * cols
                            for a in range(2):
                                last = nc.tensor.matmul(S[:, at:at + cols], qT[:, f, b, :, :].rearrange("p r q -> p (r q)"),
                                                        kT[:, a, f, b, :, :].rearrange("p g k -> p (g k)"),
                                                        start=False, stop=(f, b) == mine[-1] and a == 1)
                    last.then_inc(s["s_ready"], 1)

            def transpose_x(t, u):
                if inside(t, TILES):
                    wait(pe, s["xn_done"], t + 1)
                    wait(pe, s["yTlo_done"], t - 3)
                    for j in range(KT):
                        last = nc.tensor.transpose(bankA[:, j * P:(j + 1) * P], xn[u][:, j * P:(j + 1) * P], ident[:, :])
                    last.then_inc(s["xT_ready"], 1)

            def project(t, u, out, cols, done, free, used):
                if inside(t, TILES):
                    wait(pe, s["xlo_done"], t + 1)
                    wait(pe, s[free], used)
                    n = 0
                    for j in range(KT):
                        for a, w in ((xhi, wqkv[0]), (xhi, wqkv[1]), (xlo, wqkv[0])):
                            last = nc.tensor.matmul(out, a[u][:, j, :], w[:, j, cols], start=n == 0,
                                                    stop=n == 3 * KT - 1)
                            n += 1
                    last.then_inc(s[done], 1)

            def transpose_probs(t):
                if inside(t, TILES):
                    wait(pe, s["exp_done"], t + 1)
                    for h in range(HKV):
                        last = nc.tensor.transpose(bankS[:, h * P:(h + 1) * P],
                                                   prob[:, h, :, :].rearrange("p b k -> p (b k)"), ident[:, :])
                    last.then_inc(s["pT_ready"], 1)

            def weigh_values(t, u):
                if inside(t, TILES):
                    wait(pe, s["pTlo_done"], t + 1)
                    wait(pe, s["v_done"], 2 * t + 2)
                    wait(pe, s["y_done"], t)
                    for h in range(HKV):
                        out = bankO[:, h // G, (h % G) * B * W:(h % G + 1) * B * W]
                        for n, (p, v) in enumerate(((pThi, vhi), (pThi, vlo), (pTlo, vhi))):
                            last = nc.tensor.matmul(out, p[:, h, :], v[u][:, h, :, :].rearrange("p b w -> p (b w)"),
                                                    start=n == 0, stop=n == 2)
                    last.then_inc(s["o_ready"], 1)

            def transpose_y(t):
                if inside(t, TILES):
                    wait(pe, s["y_done"], t + 1)
                    wait(pe, s["xlo_done"], t + 4 if not isinstance(t, int) else min(t + 4, TILES))
                    for b in range(B):
                        last = nc.tensor.transpose(bankA[:, b * P:(b + 1) * P],
                                                   y[:, b, :, :].rearrange("p h d -> p (h d)"), ident[:, :])
                    last.then_inc(s["yT_ready"], 1)

            def step(k, u):
                n = 2 * k + u
                scores(n)
                transpose_qk(n + 1)
                weigh_values(n - 1, 1 - u)
                project(n + 2, u, bankB[:, 0:DQ], slice(0, DQ), "q_ready", "out_done", n - 1)
                transpose_y(n - 1)
                project(n + 2, u, bankC[:, 0:2 * DKV], slice(DQ, DALL), "kv_ready", "kT_act", n + 2)
                transpose_probs(n)
                transpose_x(n + 3, 1 - u)
                project_out(n - 1)
            loop_pairs(pe, step, FIRST, FROM, TO, LAST)
def ternary_weights(nc, sources, targets, scales, counts):
    P = 128
    with ExitStack() as ctx:
        sb = lambda name, shape, dt: ctx.enter_context(nc.sbuf_tensor("tw_" + name, shape, dt))
        sem = semaphores(nc, ctx, "tw_")
        N = max(t.shape[1] * t.shape[2] for t in targets)
        w = [sb(f"w{i}", [P, N], F32) for i in range(3)]
        below = sb("below", [P, N], F16)
        ones = sb("ones", [P, P], F32)
        rows = sb("rows", [P, 3], F32)
        bounds = sb("bounds", [P, 2, 3], F32)
        total = ctx.enter_context(nc.psum_tensor("tw_total", [P, 512], F32))
        cleared, arrived = sem("cleared"), [sem(f"arrived{i}") for i in range(3)]
        summed, totalled, bounded, below_done, done = (sem(n) for n in
                                                       ("summed", "totalled", "bounded", "below_done", "done"))
        block = ctx.enter_context(nc.Block())
        sizes = [t.shape[1] * t.shape[2] for t in targets]
        counts_in = []

        @block.sync
        def _(sp):
            for i, (src, target) in enumerate(zip(sources, targets)):
                K, M = src.shape
                full = K // P
                v = w[i][:, 0:sizes[i]].rearrange("p (j n) -> p j n", n=M)
                if K % P:
                    sp.wait_ge(cleared, 1)
                    sp.dma_start(v[0:K % P, full, :], src[full * P:K, :]).then_inc(arrived[i], 16)
                sp.dma_start(v[:, 0:full, :], src[0:full * P, :].rearrange("(j p) n -> p j n", p=P))\
                    .then_inc(arrived[i], 16)

        @block.tensor
        def _(pe):
            pe.wait_ge(summed, 3)
            pe.wait_ge(cleared, 2)
            nc.tensor.matmul(total[:, 0:3], ones[:, :], rows[:, :], start=True, stop=True).then_inc(totalled, 1)

        @block.vector
        def _(dve):
            K, M = sources[2].shape
            dve.memset(w[2][:, (K // P) * M:sizes[2]], 0.0).then_inc(cleared, 1)
            dve.memset(ones[:, :], 1.0).then_inc(cleared, 1)
            for i in range(3):
                dve.wait_ge(arrived[i], 32 if sources[i].shape[0] % P else 16)
                nc.vector.tensor_reduce(rows[:, i:i + 1], w[i][:, 0:sizes[i]], AX.X, ALU.add,
                                        apply_absolute_value=True).then_inc(summed, 1)
            dve.wait_ge(totalled, 1)
            for i in range(3):
                for sign, to in ((0.5, bounds[:, 0, i:i + 1]), (-0.5, bounds[:, 1, i:i + 1]),
                                 (1.0, scales[:, i:i + 1])):
                    nc.vector.tensor_scalar(to, total[:, i:i + 1], 1.0 / counts[i], sign, ALU.mult, ALU.mult)\
                        .then_inc(bounded, 1)
            dve.wait_ge(bounded, 9)
            for i in range(3):
                if i:
                    dve.wait_ge(done, i)
                nc.vector.tensor_scalar(below[:, 0:sizes[i]], w[i][:, 0:sizes[i]], bounds[:, 1, i:i + 1], None,
                                        ALU.is_lt).then_inc(below_done, 1)
                dve.wait_ge(below_done, i + 1)
                nc.vector.scalar_tensor_tensor(targets[i][:, :, :].rearrange("p j n -> p (j n)"),
                                               w[i][:, 0:sizes[i]], bounds[:, 0, i:i + 1], below[:, 0:sizes[i]],
                                               ALU.is_gt, ALU.subtract).then_inc(done, 1)


def fp4_weights(nc, packed, scales, targets, const):
    P, WORDS = 128, 16
    CH = 1408
    chunks = []
    for which, (words, _) in enumerate(zip(packed, scales)):
        K, M = words.shape[0] // WORDS, words.shape[1]
        if M > CH:
            chunks += [(which, j, 1, c) for j in range(K) for c in range(0, M, CH)]
        else:
            chunks += [(which, j, min(2, K - j), 0) for j in range(0, K, 2)]
    with ExitStack() as ctx:
        sb = lambda name, shape, dt: ctx.enter_context(nc.sbuf_tensor("fw_" + name, shape, dt))
        sem = semaphores(nc, ctx, "fw_")
        pair = lambda name, dt: [sb(f"{name}{i}", [P, CH], dt) for i in range(2)]
        shifts = sb("shifts", [P, 1], I32)
        words, scale = pair("words", I32), pair("scale", F16)
        nibble, code, sign = pair("nibble", I32), pair("code", I32), pair("sign", I32)
        half, double, signed, value = pair("half", F32), pair("double", F32), pair("signed", F32), pair("value", F32)
        c_in, in0, in1 = sem("c_in"), sem("in0"), sem("in1")
        arrived = (in0, in1)
        nib, codes, halves, doubles, signs, sscale, v1, v2, v3, hi, lo = (
            sem(n) for n in "nib codes halves doubles signs sscale v1 v2 v3 hi lo".split())
        block = ctx.enter_context(nc.Block())

        def views(n):
            which, j, rows, c = chunks[n]
            M = packed[which].shape[1]
            cols = min(CH, M)
            t = [x[:, j:j + rows, c:c + cols] for x in targets[which]]
            v = lambda x: x[n % 2][:, 0:rows * cols]
            return t, v, lambda a: a.rearrange("p (j n) -> p j n", j=rows)

        @block.sync
        def _(sp):
            sp.dma_start(shifts[:, :], const["shifts"]).then_inc(c_in, 16)
            for n, (which, j, rows, c) in enumerate(chunks):
                M = packed[which].shape[1]
                cols = min(CH, M)
                if n >= 2:
                    sp.wait_ge(nib, n - 1)
                    sp.wait_ge(sscale, n - 1)
                for r in range(rows):
                    at = (j + r) * WORDS
                    src = packed[which][at:at + WORDS, c:c + cols]
                    for w in range(WORDS):
                        sp.dma_start(words[n % 2][8 * w:8 * w + 8, r * cols:(r + 1) * cols],
                                     src[w:w + 1, :].broadcast_to([8, cols])).then_inc(arrived[n % 2], 16)
                    sp.dma_start(scale[n % 2][:, r * cols:(r + 1) * cols],
                                 scales[which][j + r:j + r + 1, c:c + cols].broadcast_to([P, cols]))\
                        .then_inc(arrived[n % 2], 16)

        arrivals = []
        total = [0, 0]
        for n, (_, _, rows, _) in enumerate(chunks):
            total[n % 2] += 16 * (WORDS + 1) * rows
            arrivals.append(total[n % 2])

        @block.vector
        def _(dve):
            dve.wait_ge(c_in, 16)

            def unpack(n):
                _, v, _ = views(n)
                dve.wait_ge(arrived[n % 2], arrivals[n])
                size = v(words).shape[1]
                nc.vector.tensor_tensor(v(nibble), v(words), shifts[:, :].broadcast_to([P, size]),
                                        ALU.logical_shift_right).then_inc(nib, 1)
                dve.wait_ge(nib, n + 1)
                if n >= 2:
                    dve.wait_ge(doubles, n - 1)
                    dve.wait_ge(halves, n - 1)
                    dve.wait_ge(signs, n - 1)
                nc.vector.tensor_scalar(v(code), v(nibble), 7, None, ALU.bitwise_and).then_inc(codes, 1)
                nc.vector.tensor_scalar(v(sign), v(nibble), 8, None, ALU.bitwise_and).then_inc(codes, 1)

            def combine(n):
                t, v, r = views(n)
                dve.wait_ge(halves, n + 1)
                nc.vector.scalar_tensor_tensor(v(value), v(code), -2.0, v(half), ALU.add, ALU.max).then_inc(v1, 1)
                dve.wait_ge(v1, n + 1)
                dve.wait_ge(doubles, n + 1)
                nc.vector.tensor_tensor(v(value), v(value), v(double), ALU.max).then_inc(v2, 1)
                dve.wait_ge(v2, n + 1)
                dve.wait_ge(sscale, n + 1)
                nc.vector.tensor_tensor(v(value), v(value), v(signed), ALU.mult).then_inc(v3, 1)
                dve.wait_ge(hi, n + 1)
                nc.vector.tensor_tensor(t[1], r(v(value)), t[0], ALU.subtract).then_inc(lo, 1)

            for n in range(len(chunks) + 1):
                if n < len(chunks):
                    unpack(n)
                if n:
                    combine(n - 1)

        @block.scalar
        def _(act):
            def prepare(n):
                _, v, _ = views(n)
                act.wait_ge(codes, 2 * n + 2)
                if n >= 2:
                    act.wait_ge(v2, n - 1)
                    act.wait_ge(v3, n - 1)
                nc.scalar.activation(v(half), v(code), ACT.Copy, scale=0.5).then_inc(halves, 1)
                nc.scalar.activation(v(double), v(code), ACT.Copy, scale=2.0, bias=-8.0).then_inc(doubles, 1)
                nc.scalar.activation(v(signed), v(sign), ACT.Copy, scale=-0.25, bias=1.0).then_inc(signs, 1)

            def high(n):
                t, v, r = views(n)
                act.wait_ge(v3, n + 1)
                nc.scalar.copy(t[0], r(v(value))).then_inc(hi, 1)

            for n in range(len(chunks) + 1):
                if n < len(chunks):
                    prepare(n)
                if n:
                    high(n - 1)

        @block.gpsimd
        def _(pool):
            for n in range(len(chunks)):
                _, v, _ = views(n)
                pool.wait_ge(signs, n + 1)
                pool.wait_ge(arrived[n % 2], arrivals[n])
                pool.tensor_tensor(v(signed), v(signed), v(scale), ALU.mult).then_inc(sscale, 1)


def feed_forward(nc, pre, h_dram, out_dram, gate, up, down, scales, const, HID, rms_out, GROUPS=8):
    P, DM, GT = 128, 512, 512
    KT, NT = DM // P, GT // P
    MT = (HID + P - 1) // P
    rows = [min(P, HID - m * P) for m in range(MT)]
    EPS, RMS_EPS = 1e-5, 1e-6
    TILES = GROUPS * NT
    assert MT % 2
    with ExitStack() as ctx:
        sb = lambda name, shape, dt: ctx.enter_context(nc.sbuf_tensor(pre + name, shape, dt))
        sem = semaphores(nc, ctx, pre)
        pair = lambda name, shape, dt: [sb(f"{name}{i}", shape, dt) for i in range(2)]
        ident, minus_half = sb("ident", [P, P], F32), sb("minus_half", [P, 1], F32)
        hin, hres, hout = pair("hin", [P, DM], F32), pair("hres", [P, DM], F32), pair("hout", [P, DM], F32)
        stats, mv, veps, rstd = (pair(n, [P, w], F32) for n, w in (("stats", 6), ("mv", 2), ("veps", 1), ("rstd", 1)))
        xn = sb("xn", [P, DM], F32)
        xhi, xlo = pair("xhi", [P, KT, GT], F16), pair("xlo", [P, KT, GT], F16)
        act_out, prod = pair("act_out", [P, GT], F32), pair("prod", [P, GT], F32)
        ghi, glo = pair("ghi", [P, MT, GT], F16), pair("glo", [P, MT, GT], F16)
        if rms_out:
            square, ssum, ms, rinv = pair("square", [P, DM], F32), pair("ssum", [P, 1], F32), pair("ms", [P, 1], F32), pair("rinv", [P, 1], F32)
        gu = [[ctx.enter_context(nc.psum_tensor(f"{pre}gu{i}{w}", [P, GT], F32)) for w in "gu"] for i in range(2)]
        px = ctx.enter_context(nc.psum_tensor(pre + "px", [P, KT * P], F32))
        pz = [ctx.enter_context(nc.psum_tensor(f"{pre}pz{i}", [P, DM], F32)) for i in range(2)]

        c_in, set_up = sem("c_in"), sem("set_up")
        h_in, res_in, stored = ([sem(f"{n}{i}") for i in range(2)] for n in ("h_in", "res_in", "stored"))
        names = ("stats_done mv_done veps_done rstd_done xn_done xT_ready xhi_done xlo_done gu_ready act_done "
                 "prod_done ghi_done glo_done z_ready out_done sp_passed dve_passed sq_done ms_done "
                 "rinv_done").split()
        s = {n: sem(n) for n in names}
        FIRST, FROM, TO, LAST = -1, 2, (GROUPS - 1) // 2 * 2, GROUPS + 1
        parts_x = [(x, w) for x in (0, 1) for w in range(len(gate)) if x + w < 2]
        xparts, gparts = (xhi, xlo), (ghi, glo)
        block = ctx.enter_context(nc.Block())

        norm_at = [2, 4, 6, 8]
        down_at = [0, 1, 2, 3]

        @block.sync
        def _(sp):
            sp.dma_start(ident[:, :], const["ident"]).then_inc(c_in, 16)

            def load(g, i):
                if inside(g, GROUPS):
                    t = NT * g + i
                    wait_alone(sp, s["sp_passed"], s["xn_done"], t - 1)
                    sp.dma_start(hin[i % 2][:, :], h_dram[bass.ds(t * P, P), :]).then_inc(h_in[i % 2], 16)

            def residual(g, i):
                if inside(g, GROUPS):
                    t = NT * g + i
                    wait_alone(sp, s["sp_passed"], s["out_done"], t - 1)
                    sp.dma_start(hres[i % 2][:, :], h_dram[bass.ds(t * P, P), :]).then_inc(res_in[i % 2], 16)

            def store(g, i):
                if inside(g, GROUPS):
                    t = NT * g + i
                    wait_alone(sp, s["sp_passed"], s["out_done"], t + 1)
                    sp.dma_start(out_dram[bass.ds(t * P, P), :], hout[i % 2][:, :]).then_inc(stored[i % 2], 16)

            def step(k, u):
                n = 2 * k + u
                residual(n - 1, 0)
                residual(n - 1, 1)
                load(n + 1, 0)
                load(n + 1, 1)
                store(n - 1, 0)
                residual(n - 1, 2)
                store(n - 1, 1)
                residual(n - 1, 3)
                store(n - 1, 2)
                store(n - 1, 3)
                load(n + 1, 2)
                load(n + 1, 3)
            loop_pairs(sp, step, FIRST, FROM, TO, LAST)
            for u in range(2):
                sp.wait_ge(stored[u], 16 * (TILES // 2))

        @block.gpsimd
        def _(pool):
            pool.wait_ge(set_up, 1)

            def inverse_deviation(g, i):
                if inside(g, GROUPS):
                    wait(pool, s["veps_done"], NT * g + i + 1)
                    pool.tensor_tensor(rstd[i % 2][:, :], veps[i % 2][:, :], minus_half[:, :], ALU.pow)\
                        .then_inc(s["rstd_done"], 1)

            def inverse_rms(g, i):
                if inside(g, GROUPS) and rms_out:
                    wait(pool, s["ms_done"], NT * g + i + 1)
                    pool.tensor_tensor(rinv[i % 2][:, :], ms[i % 2][:, :], minus_half[:, :], ALU.pow)\
                        .then_inc(s["rinv_done"], 1)

            def step(k, u):
                n = 2 * k + u
                for m in range(MT):
                    if m in down_at:
                        inverse_rms(n - 1, down_at.index(m))
                    if m + 2 in norm_at:
                        inverse_deviation(n + 1, norm_at.index(m + 2))
            loop_pairs(pool, step, FIRST, FROM, TO, LAST)

        @block.scalar
        def _(act):
            def gate_act(g, m, u):
                if inside(g, GROUPS):
                    n = MT * g + m
                    wait(act, s["gu_ready"], n + 1)
                    wait(act, s["prod_done"], n - 1)
                    nc.scalar.activation(act_out[(m + u) % 2][0:rows[m], :], gu[(m + u) % 2][0][0:rows[m], :], ACT.Silu,
                                         scale=scales[0:rows[m], 0:1] if scales is not None else 1.0)\
                        .then_inc(s["act_done"], 1)

            def hidden_hi(g, m, u):
                if inside(g, GROUPS):
                    wait(act, s["prod_done"], MT * g + m + 1)
                    if m == 0:
                        wait(act, s["z_ready"], NT * (g - 1))
                    nc.scalar.copy(ghi[u][0:rows[m], m, :], prod[(m + u) % 2][0:rows[m], :])\
                        .then_inc(s["ghi_done"], 1)

            def x_hi(g, i, u):
                if inside(g, GROUPS):
                    wait(act, s["xT_ready"], NT * g + i + 1)
                    if i == 0:
                        wait(act, s["gu_ready"], MT * (g - 1))
                    nc.scalar.copy(xhi[u][:, :, i * P:(i + 1) * P], px[:, :].rearrange("p (j n) -> p j n", j=KT))\
                        .then_inc(s["xhi_done"], 1)

            def squares(g, i):
                if inside(g, GROUPS) and rms_out:
                    t = NT * g + i
                    wait(act, s["z_ready"], t + 1)
                    wait(act, s["sq_done"], t - 1)
                    nc.scalar.activation(square[i % 2][:, :], pz[i % 2][:, :], ACT.Square, accum_out=ssum[i % 2][:, :])\
                        .then_inc(s["sq_done"], 1)

            def step(k, u):
                n = 2 * k + u
                for m in range(MT):
                    gate_act(n, m, u)
                    if m:
                        hidden_hi(n, m - 1, u)
                    if m in down_at:
                        squares(n - 1, down_at.index(m))
                    if m in norm_at:
                        x_hi(n + 1, norm_at.index(m), 1 - u)
                hidden_hi(n, MT - 1, u)
            loop_pairs(act, step, FIRST, FROM, TO, LAST)

        @block.vector
        def _(dve):
            dve.memset(minus_half[:, :], -0.5).then_inc(set_up, 1)

            def hidden(g, m, u):
                if inside(g, GROUPS):
                    n = MT * g + m
                    r = slice(0, rows[m])
                    wait(dve, s["act_done"], n + 1)
                    wait(dve, s["glo_done"], n - 1)
                    if scales is not None:
                        nc.vector.scalar_tensor_tensor(prod[(m + u) % 2][r, :], gu[(m + u) % 2][1][r, :], scales[r, 1:2],
                                                       act_out[(m + u) % 2][r, :], ALU.mult, ALU.mult)\
                            .then_inc(s["prod_done"], 1)
                    else:
                        nc.vector.tensor_tensor(prod[(m + u) % 2][r, :], gu[(m + u) % 2][1][r, :], act_out[(m + u) % 2][r, :],
                                                ALU.mult).then_inc(s["prod_done"], 1)

            def hidden_lo(g, m, u):
                if inside(g, GROUPS):
                    wait(dve, s["ghi_done"], MT * g + m + 1)
                    r = slice(0, rows[m])
                    nc.vector.tensor_tensor(glo[u][r, m, :], prod[(m + u) % 2][r, :], ghi[u][r, m, :], ALU.subtract)\
                        .then_inc(s["glo_done"], 1)

            def row_stats(g, i, half):
                if inside(g, GROUPS):
                    t, u = NT * g + i, i % 2
                    wait_alone(dve, s["dve_passed"], h_in[u], 16 * (half + 1))
                    nc.vector.bn_stats(stats[u][:, :], hin[u][:, :]).then_inc(s["stats_done"], 1)
                    wait_alone(dve, s["dve_passed"], s["stats_done"], t + 1)
                    nc.vector.bn_aggr(mv[u][:, :], stats[u][:, :]).then_inc(s["mv_done"], 1)
                    wait(dve, s["mv_done"], t + 1)
                    nc.vector.tensor_scalar(veps[u][:, :], mv[u][:, 1:2], EPS, None, ALU.add)\
                        .then_inc(s["veps_done"], 1)

            def x_normalised(g, i):
                if inside(g, GROUPS):
                    t, u = NT * g + i, i % 2
                    wait(dve, s["rstd_done"], t + 1)
                    wait(dve, s["xT_ready"], t)
                    nc.vector.tensor_scalar(xn[:, :], hin[u][:, :], mv[u][:, 0:1], rstd[u][:, :],
                                            ALU.subtract, ALU.mult).then_inc(s["xn_done"], 1)

            def x_lo(g, i, u):
                if inside(g, GROUPS):
                    wait(dve, s["xhi_done"], NT * g + i + 1)
                    nc.vector.tensor_tensor(xlo[u][:, :, i * P:(i + 1) * P], px[:, :].rearrange("p (j n) -> p j n", j=KT),
                                            xhi[u][:, :, i * P:(i + 1) * P], ALU.subtract).then_inc(s["xlo_done"], 1)

            def mean_square(g, i):
                if inside(g, GROUPS) and rms_out:
                    wait(dve, s["sq_done"], NT * g + i + 1)
                    nc.vector.tensor_scalar(ms[i % 2][:, :], ssum[i % 2][:, :], 1.0 / DM, RMS_EPS, ALU.mult, ALU.add)\
                        .then_inc(s["ms_done"], 1)

            def output(g, i, half):
                if inside(g, GROUPS):
                    t, u = NT * g + i, i % 2
                    wait(dve, s["rinv_done" if rms_out else "z_ready"], t + 1)
                    wait(dve, res_in[u], 16 * (half + 1))
                    wait(dve, stored[u], 16 * half)
                    nc.vector.scalar_tensor_tensor(hout[u][:, :], pz[u][:, :],
                                                   rinv[u][:, :] if rms_out else scales[:, 2:3], hres[u][:, :],
                                                   ALU.mult, ALU.add).then_inc(s["out_done"], 1)

            def step(k, u):
                n = 2 * k + u
                for m in range(MT):
                    hidden(n, m, u)
                    if m + 1 in norm_at:
                        x_normalised(n + 1, norm_at.index(m + 1))
                    if m in down_at:
                        mean_square(n - 1, down_at.index(m))
                    if m:
                        hidden_lo(n, m - 1, u)
                    if m - 1 in down_at:
                        i = down_at.index(m - 1)
                        output(n - 1, i, 2 * (n - 1) + i // 2)
                    if m in norm_at:
                        x_lo(n + 1, norm_at.index(m), 1 - u)
                    if m + 2 in norm_at:
                        i = norm_at.index(m + 2)
                        row_stats(n + 1, i, 2 * (n + 1) + i // 2)
                hidden_lo(n, MT - 1, u)
            loop_pairs(dve, step, FIRST, FROM, TO, LAST)

        @block.tensor
        def _(pe):
            pe.wait_ge(c_in, 16)

            def gate_up(g, m, u):
                if inside(g, GROUPS):
                    n = MT * g + m
                    if m == 0:
                        wait(pe, s["xlo_done"], NT * (g + 1))
                    wait(pe, s["prod_done"], n - 1)
                    for which, weights in enumerate((gate, up)):
                        c = 0
                        for j in range(KT):
                            for x, w in parts_x:
                                last = nc.tensor.matmul(gu[(m + u) % 2][which][0:rows[m], :],
                                                        weights[w][:, j, m * P:m * P + rows[m]],
                                                        xparts[x][u][:, j, :], start=c == 0,
                                                        stop=c == KT * len(parts_x) - 1)
                                c += 1
                    last.then_inc(s["gu_ready"], 1)

            def transpose_x(g, i):
                if inside(g, GROUPS):
                    t = NT * g + i
                    wait(pe, s["xn_done"], t + 1)
                    wait(pe, s["xlo_done"], t)
                    for j in range(KT):
                        last = nc.tensor.transpose(px[:, j * P:(j + 1) * P], xn[:, j * P:(j + 1) * P], ident[:, :])
                    last.then_inc(s["xT_ready"], 1)

            def project(g, i, u):
                if inside(g, GROUPS):
                    t = NT * g + i
                    if i == 0:
                        wait(pe, s["glo_done"], MT * (g + 1))
                    wait(pe, s["out_done"], t - 1)
                    c = 0
                    for m in range(MT):
                        for x, w in parts_x:
                            last = nc.tensor.matmul(pz[i % 2][:, :], gparts[x][u][0:rows[m], m, i * P:(i + 1) * P],
                                                    down[w][0:rows[m], m, :], start=c == 0,
                                                    stop=c == MT * len(parts_x) - 1)
                            c += 1
                    last.then_inc(s["z_ready"], 1)

            def step(k, u):
                n = 2 * k + u
                for m in range(MT):
                    gate_up(n, m, u)
                    if m in down_at:
                        project(n - 1, down_at.index(m), 1 - u)
                    if m in norm_at:
                        transpose_x(n + 1, norm_at.index(m))
            loop_pairs(pe, step, FIRST, FROM, TO, LAST)
def three_bf16(a):
    parts, rest = [], np.asarray(a, np.float64)
    for _ in range(3):
        part = rest.astype(np.float32).astype(np.dtype("bfloat16"))
        parts.append(part)
        rest = rest - part.astype(np.float64)
    return parts


def constants():
    P, L, B = 128, 32, 4
    q, k = np.arange(L)[:, None], np.arange(L)[None, :]
    out = {"ident": np.eye(P, dtype=np.float32), "ident16": np.eye(P, dtype=np.float16)}
    row = np.arange(96)[:, None] % L
    out["select"] = (row == np.arange(P)[None, :] % L).astype(np.dtype("bfloat16"))
    out["own"] = (np.arange(P)[:, None] // L == np.arange(B)[None, :]).astype(np.float32)
    for pre, kv, d, slope in (("a0_", 8, 16, lambda h: 0.0), ("a1_", 4, 32, lambda h: np.float32(2 ** -0.5 * (2 ** -0.5) ** h))):
        table = np.zeros((96, 2, B, kv // 2, L), np.dtype("bfloat16"))
        for h in range(kv):
            full = np.where(k <= q, float(slope(h)) * (k - q) * float(d) ** 0.5, 0.0)
            for n, part in enumerate(three_bf16(full)):
                part = part.copy()
                if n == 0:
                    part[k + 0 * q > q] = -1e30
                table[n * L:(n + 1) * L, h // (kv // 2), :, h % (kv // 2), :] = part[:, None, :]
        out[pre + "bias"] = table.reshape(96, -1)
    out["shifts"] = np.ascontiguousarray((np.arange(P, dtype=np.int32)[:, None] % 8) * 4).astype(np.int32)
    inv = (np.float32(1.0) / np.power(np.float32(10000.0), np.arange(0, 16, 2, dtype=np.float32) / np.float32(16))).astype(np.float32)
    angle = np.outer(np.arange(L, dtype=np.float32), inv).astype(np.float32)
    angle = np.tile(angle, (B, 1))
    out["cos"] = np.repeat(np.cos(angle), 2, axis=1).astype(np.float32)
    out["sin"] = np.stack([-np.sin(angle), np.sin(angle)], axis=1).astype(np.float32)
    return out


_X = "x"
_OUT = (128, 32, 512)


def audio_tower(nc, x, weights, const, out):
    P, TOKENS, DM = 128, 4096, 512
    h = [nc.dram_tensor(f"h{i}", (TOKENS, DM), F32, kind="Internal").ap() for i in range(4)]
    y = out.rearrange("b s d -> (b s) d")
    token_mixer(nc, x, const["ident"], h[0])
    attention(nc, "a0_", h[0], h[1], weights["qkv0"], weights["o0"], const, 8, 16, True)
    with ExitStack() as ctx:
        sources = [weights[n] for n in ("w1", "w3", "w2")]
        tern = [ctx.enter_context(nc.sbuf_tensor(f"tern{i}", [P, (w.shape[0] + P - 1) // P, w.shape[1]], F16))
                for i, w in enumerate(sources)]
        scales = ctx.enter_context(nc.sbuf_tensor("tern_scales", [P, 3], F32))
        ternary_weights(nc, sources, tern, scales, [w.shape[0] * w.shape[1] for w in sources])
        feed_forward(nc, "f0_", h[1], h[2], [tern[0]], [tern[1]], [tern[2]], scales, const, sources[0].shape[1], False)
    attention(nc, "a1_", h[2], h[3], weights["qkv1"], weights["o1"], const, 4, 32, False)
    with ExitStack() as ctx:
        HID = weights["gu"].shape[1] // 2
        gu = [ctx.enter_context(nc.sbuf_tensor(f"gu{i}", [P, DM // P, 2 * HID], F16)) for i in range(2)]
        dn = [ctx.enter_context(nc.sbuf_tensor(f"dn{i}", [P, HID // P, DM], F16)) for i in range(2)]
        fp4_weights(nc, (weights["gu"], weights["dn"]), (weights["gu_scales"], weights["dn_scales"]), (gu, dn), const)
        feed_forward(nc, "f1_", h[3], y, [w[:, :, 0:HID] for w in gu], [w[:, :, HID:] for w in gu], dn, None,
                     const, HID, True)


def kernel(**inputs):
    import concourse.bacc as bacc
    from concourse.bass_utils import run_bass_kernel_spmd

    a = {k: np.asarray(v) for k, v in inputs.items()}

    def rows_by_repeat(w, heads, d):
        return w.reshape(heads, 4, d, 512).transpose(1, 0, 2, 3).reshape(512, 512)

    layouts = {
        "qkv0": np.concatenate([a["L0_attn_wq"], a["L0_attn_wk"], a["L0_attn_wv"]], axis=0).T,
        "o0": rows_by_repeat(a["L0_attn_wo"].T, 8, 16),
        "w1": a["L0_ffn_w1"].T, "w3": a["L0_ffn_w3"].T, "w2": a["L0_ffn_w2"].T,
        "qkv1": np.concatenate([a["L1_attn_Wq"], a["L1_attn_Wk"], a["L1_attn_Wv"]], axis=1),
        "o1": rows_by_repeat(a["L1_attn_Wo"], 4, 32),
        "gu": a["L1_ffn_gate_up_packed"].T, "gu_scales": a["L1_ffn_gate_up_scales"],
        "dn": a["L1_ffn_down_packed"].T, "dn_scales": a["L1_ffn_down_scales"],
    }
    tables = constants()
    nc = bacc.Bacc("TRN2", target_bir_lowering=False, num_devices=1)
    arrays = {"in_x": np.ascontiguousarray(a["x"])}
    arrays.update({f"in_{k}": np.ascontiguousarray(v) for k, v in layouts.items()})
    arrays.update({f"const_{k}": np.ascontiguousarray(v) for k, v in tables.items()})
    aps = {k: nc.dram_tensor(k, v.shape, mybir.dt.from_np(v.dtype), kind="ExternalInput").ap()
           for k, v in arrays.items()}
    out = nc.dram_tensor("out", _OUT, F32, kind="ExternalOutput").ap()
    audio_tower(nc, aps["in_x"], {k: aps[f"in_{k}"] for k in layouts}, {k: aps[f"const_{k}"] for k in tables}, out)
    r = run_bass_kernel_spmd(nc, [arrays], core_ids=[0])
    return r.results[0]["out"]
```

```python
import numpy as np
import concourse.bass as bass
from concourse import mybir
from contextlib import ExitStack

F32 = mybir.dt.float32
F16 = mybir.dt.float16
BF16 = mybir.dt.bfloat16
I32 = mybir.dt.int32
ALU = mybir.AluOpType
ACT = mybir.ActivationFunctionType
AX = mybir.AxisListType


def loop_pairs(eng, step, first, loop_from, loop_to, last):
    for n in range(first, loop_from):
        step(n // 2, n % 2)
    with eng.Fori(loop_from // 2, loop_to // 2) as k:
        step(k, 0)
        step(k, 1)
    for n in range(loop_to, last):
        step(n // 2, n % 2)


def wait(eng, sem, count):
    if not isinstance(count, int) or count > 0:
        eng.wait_ge(sem, count)


def wait_alone(eng, passed, sem, count):
    if not isinstance(count, int) or count > 0:
        eng.wait_ge(sem, count)
        if not isinstance(count, int):
            eng.sem_inc(passed, 1)


def semaphores(nc, ctx, prefix):
    made = []

    def make(name):
        made.append(nc.alloc_semaphore(prefix + name))
        return made[-1]

    def end():
        nc.clear_and_free_semaphores(made)
        nc.all_engine_barrier()
    ctx.callback(end)
    return make


def inside(t, tiles):
    return not isinstance(t, int) or 0 <= t < tiles


def token_mixer(nc, x, ident_dram, h_dram, SEQS=128):
    C, T = x.shape[1] // 3, x.shape[2]
    P = 128
    B = P // C
    NT = T // P
    TILES = SEQS // B
    SCALE = float(C) ** -0.5
    PARTS = 3
    KS = PARTS * C
    KM = KS + 2
    W = C + 1
    SLOTS = B * NT
    LEAD, LAG = 7, 12
    with ExitStack() as ctx:
        sb = lambda name, shape, dt: ctx.enter_context(nc.sbuf_tensor(name, shape, dt))
        sem = semaphores(nc, ctx, "")
        ident = sb("tm_ident", [P, P], F32)
        xqk = [sb(f"tm_xqk{i}", [P, 2, T], F32) for i in range(2)]
        xv = [sb(f"tm_xv{i}", [P, T], F32) for i in range(2)]
        xs = [sb(f"tm_xs{i}", [P, 4, T], F16) for i in range(2)]
        qk = [sb(f"tm_qk{i}", [P, 2, B, T], F16) for i in range(2)]
        v = [sb(f"tm_v{i}", [P, B, W], F32) for i in range(2)]
        vhi = [sb(f"tm_vhi{i}", [P, NT, B, W], F16) for i in range(2)]
        vlo = [sb(f"tm_vlo{i}", [P, NT, B, C], F16) for i in range(2)]
        negmax = [sb(f"tm_negmax{i}", [P, SLOTS], F32) for i in range(2)]
        mrow = sb("tm_mrow", [SLOTS, 2, P], F16)
        prob = [sb(f"tm_prob{i}", [P, NT, T], F32) for i in range(B)]
        phi = [sb(f"tm_phi{i}", [P, NT, T], F16) for i in range(B)]
        plo = [sb(f"tm_plo{i}", [P, NT, T], F16) for i in range(B)]
        rden = sb("tm_rden", [P, 2, 2, NT], F32)
        hT = [sb(f"tm_hT{i}", [P, NT, B, C], F32) for i in range(2)]
        htok = [sb(f"tm_htok{i}", [P, T], F32) for i in range(2)]
        s1 = ctx.enter_context(nc.psum_tensor("tm_s1", [P, 2, T], F32))
        s2 = ctx.enter_context(nc.psum_tensor("tm_s2", [P, 2, 2, T], F32))
        bankA = ctx.enter_context(nc.psum_tensor("tm_bankA", [P, 512], F32))
        bankB = ctx.enter_context(nc.psum_tensor("tm_bankB", [P, 512], F32))
        sums = [bank[:, 0:2 * NT * W].rearrange("p (b i w) -> p b i w", b=2, i=NT) for bank in (bankA, bankB)]
        vT = bankA[:, :].rearrange("p (j n) -> p j n", j=NT)
        tokT = bankB[:, :].rearrange("p (j n) -> p j n", j=NT)

        ident_in = sem("tm_ident_in")
        ones_set = sem("tm_ones_set")
        qk_in = [sem(f"tm_qk_in{i}") for i in range(2)]
        v_in = [sem(f"tm_v_in{i}") for i in range(2)]
        xhi_done, xlo_done = sem("tm_xhi_done"), sem("tm_xlo_done")
        phi_done = sem("tm_phi_done")
        plo_done, plo_pool = sem("tm_plo_done"), sem("tm_plo_pool")
        vlo_done = sem("tm_vlo_done")
        sp_passed = sem("tm_sp_passed")
        stacked = [[sem(f"tm_stacked{u}{b}") for b in range(B)] for u in range(2)]
        vt_ready = sem("tm_vt_ready")
        v_ready = sem("tm_v_ready")
        s1_ready = sem("tm_s1_ready")
        max_done = sem("tm_max_done")
        mt_ready = sem("tm_mt_ready")
        mhi_done = sem("tm_mhi_done")
        mrow_done = sem("tm_mrow_done")
        mrow_in = sem("tm_mrow_in")
        s2_ready = sem("tm_s2_ready")
        exp_done = sem("tm_exp_done")
        pv_done = sem("tm_pv_done")
        rden_done = sem("tm_rden_done")
        norm_done = sem("tm_norm_done")
        htr_done = sem("tm_htr_done")
        htok_ready = sem("tm_htok_ready")
        stored = [sem(f"tm_stored{i}") for i in range(2)]

        FIRST, FROM, TO, LAST = -4, 4, (TILES - 3) // 2 * 2, TILES + 2
        VALUES_AT, TOKENS_AT, MAXIMA_AT = 6, 14, 10
        block = ctx.enter_context(nc.Block())

        @block.sync
        def _(sp):
            sp.dma_start(ident[:, :], ident_dram).then_inc(ident_in, 16)

            def load(t, u):
                if inside(t, TILES):
                    wait_alone(sp, sp_passed, xlo_done, t - 1)
                    for part in range(2):
                        sp.dma_start(xqk[u][:, part, :], x[bass.ds(t * B, B)][:, part * C:(part + 1) * C, :])\
                            .then_inc(qk_in[u], 16)

            def load_values(t, u):
                if inside(t, TILES):
                    wait_alone(sp, sp_passed, vt_ready, t - 1)
                    sp.dma_start(xv[u][:, :], x[bass.ds(t * B, B)][:, 2 * C:3 * C, :]).then_inc(v_in[u], 16)

            def store(t, u):
                if inside(t, TILES):
                    wait_alone(sp, sp_passed, htok_ready, t + 1)
                    sp.dma_start(h_dram[bass.ds(t * P, P), :], htok[u][:, :]).then_inc(stored[u], 16)

            def stack(t, u, b):
                if inside(t, TILES):
                    wait_alone(sp, sp_passed, xlo_done, t + 1)
                    wait_alone(sp, sp_passed, s2_ready, 8 * (t - 2) + 2 * b + 2)
                    c = slice(b * C, (b + 1) * C)
                    for g, (lo, hi) in enumerate(((0, 2), (0, 3), (1, 2))):
                        sp.dma_start(qk[u][g * C:(g + 1) * C, :, b, :],
                                     xs[u][c, lo:hi + 1:hi - lo, :]).then_inc(stacked[u][b], 16)

            def maxima(t, u):
                if inside(t, TILES):
                    wait_alone(sp, sp_passed, mrow_done, t + 1)
                    for part in range(2):
                        sp.dma_start(qk[u][KS + part:KS + part + 1, 0, :, :]
                                     .rearrange("o b (i t) -> o (b i) t", i=NT),
                                     mrow[:, part, :]).then_inc(mrow_in, 16)

            def step(k, u):
                n = 2 * k + u
                load(n + 4, u)
                load_values(n + 1, 1 - u)
                store(n - 2, u)
                stack(n + 2, u, 0)
                stack(n + 2, u, 1)
                stack(n + 2, u, 2)
                maxima(n + 1, 1 - u)
                stack(n + 2, u, 3)
            loop_pairs(sp, step, FIRST, FROM, TO, LAST)
            for u in range(2):
                sp.wait_ge(stored[u], 16 * (TILES // 2))

        @block.gpsimd
        def _(pool):
            def x_lo(t, u):
                if inside(t, TILES):
                    wait(pool, xhi_done, t + 1)
                    pool.tensor_tensor(xs[u][:, 1:4:2, :], xqk[u][:, :, :], xs[u][:, 0:4:2, :],
                                       ALU.subtract).then_inc(xlo_done, 1)

            def probs_lo(t, b):
                if inside(t, TILES):
                    for j in range(1, 3):
                        wait(pool, phi_done, 8 * t + 2 * b + j)
                        pool.tensor_tensor(plo[b][:, j, :], prob[b][:, j, :], phi[b][:, j, :],
                                           ALU.subtract).then_inc(plo_pool, 1)

            def step(k, u):
                n = 2 * k + u
                for b in range(B):
                    if b == 1:
                        x_lo(n + 3, 1 - u)
                    probs_lo(n, b)
            loop_pairs(pool, step, FIRST, FROM, TO, LAST)

        @block.scalar
        def _(act):
            def x_hi(t, u, half):
                if inside(t, TILES):
                    wait(act, qk_in[u], 32 * (half + 1))
                    for b in range(B):
                        wait(act, stacked[u][b], 48 * half)
                    nc.scalar.copy(xs[u][:, 0:4:2, :], xqk[u][:, :, :]).then_inc(xhi_done, 1)

            def values_in(t, u):
                if inside(t, TILES):
                    wait(act, vt_ready, t + 1)
                    wait(act, pv_done, 4 * (t - 1))
                    if isinstance(t, int) and t < 2:
                        wait(act, ones_set, 6)
                    nc.scalar.copy(vhi[u][:, 1:NT, :, 0:C], vT[:, 1:NT, :].rearrange("p j (b c) -> p j b c", b=B))\
                        .then_inc(v_ready, 1)
                    nc.scalar.copy(v[u][:, :, 0:C], vT[:, 0, :].rearrange("p (b c) -> p b c", b=B))\
                        .then_inc(v_ready, 1)

            def exps(t, b, h):
                if inside(t, TILES):
                    wait(act, s2_ready, 8 * t + 2 * b + h + 1)
                    if h == 0:
                        wait(act, pv_done, 4 * (t - 1) + b + 1)
                    nc.scalar.activation(prob[b][:, 2 * h:2 * h + 2, :], s2[:, h, :, :], ACT.Exp,
                                         scale=SCALE).then_inc(exp_done, 1)

            def probs_hi(t, b, h):
                if inside(t, TILES):
                    tiles = slice(2, 4) if h else slice(1, 2)
                    wait(act, exp_done, 8 * t + 2 * b + h + 1)
                    nc.scalar.copy(phi[b][:, tiles, :], prob[b][:, tiles, :]).then_inc(phi_done, 1)

            def tokens_out(t, u, half):
                if inside(t, TILES):
                    wait(act, htr_done, t + 1)
                    wait(act, stored[u], 16 * half)
                    nc.scalar.copy(htok[u][:, :], bankB[:, :]).then_inc(htok_ready, 1)

            def step(k, u):
                n = 2 * k + u
                exps(n, 0, 0)
                probs_hi(n - 1, 3, 1)
                exps(n, 0, 1)
                probs_hi(n, 0, 0)
                x_hi(n + 3, 1 - u, k + 1 + u)
                exps(n, 1, 0)
                probs_hi(n, 0, 1)
                values_in(n, u)
                exps(n, 1, 1)
                probs_hi(n, 1, 0)
                exps(n, 2, 0)
                probs_hi(n, 1, 1)
                exps(n, 2, 1)
                probs_hi(n, 2, 0)
                exps(n, 3, 0)
                probs_hi(n, 2, 1)
                exps(n, 3, 1)
                probs_hi(n, 3, 0)
                tokens_out(n - 1, 1 - u, k + (u - 1) // 2)
            loop_pairs(act, step, FIRST, FROM, TO, LAST)

        @block.vector
        def _(dve):
            for u in range(2):
                dve.memset(qk[u][KS:KM, 1, :, :], 1.0).then_inc(ones_set, 1)
                dve.memset(v[u][:, :, C:W], 1.0).then_inc(ones_set, 1)
                dve.memset(vhi[u][:, :, :, C:W], 1.0).then_inc(ones_set, 1)

            def maxes(t, u, m):
                if inside(t, TILES):
                    wait(dve, s1_ready, SLOTS * t + m + 1)
                    if m == 0:
                        wait(dve, mt_ready, t - 1)
                    nc.vector.tensor_reduce(negmax[u][:, m:m + 1], s1[:, m % 2, :], AX.X, ALU.max,
                                            negate=True).then_inc(max_done, 1)

            def probs_lo(t, b):
                if inside(t, TILES):
                    wait(dve, phi_done, 8 * t + 2 * b + 2)
                    nc.vector.tensor_tensor(plo[b][:, 3, :], prob[b][:, 3, :], phi[b][:, 3, :],
                                            ALU.subtract).then_inc(plo_done, 1)

            def values_lo(t, u):
                if inside(t, TILES):
                    wait(dve, v_ready, 2 * t + 2)
                    nc.vector.tensor_tensor(vlo[u][:, 1:NT, :, :], vT[:, 1:NT, :].rearrange("p j (b c) -> p j b c", b=B),
                                            vhi[u][:, 1:NT, :, 0:C], ALU.subtract).then_inc(vlo_done, 1)

            def maxima_parts(t):
                if inside(t, TILES):
                    wait(dve, mt_ready, t + 1)
                    wait(dve, mrow_in, 32 * t)
                    nc.vector.tensor_copy(mrow[:, 0, :], bankA[0:SLOTS, 0:P]).then_inc(mhi_done, 1)
                    wait(dve, mhi_done, t + 1)
                    nc.vector.tensor_tensor(mrow[:, 1, :], bankA[0:SLOTS, 0:P], mrow[:, 0, :],
                                            ALU.subtract).then_inc(mrow_done, 1)

            def inverse_sums(t, pair):
                if inside(t, TILES):
                    wait(dve, pv_done, 4 * t + 2 * pair + 2)
                    nc.vector.reciprocal(rden[:, pair, :, :], sums[pair][:, :, :, C]).then_inc(rden_done, 1)

            def normalise(t, u, pair):
                if inside(t, TILES):
                    wait(dve, rden_done, 2 * t + pair + 1)
                    if pair == 0:
                        wait(dve, htr_done, t - 1)
                    nc.vector.tensor_tensor(hT[u][:, :, 2 * pair:2 * pair + 2, :].rearrange("p i b c -> p b i c"),
                                            sums[pair][:, :, :, 0:C],
                                            rden[:, pair, :, :].unsqueeze(3).broadcast_to([P, 2, NT, C]),
                                            ALU.mult).then_inc(norm_done, 1)

            def step(k, u):
                n = 2 * k + u
                for g in range(SLOTS):
                    ahead, m = divmod(g + LEAD, SLOTS)
                    maxes(n + 1 + ahead, (u + 1 + ahead) % 2, m)
                    if g == 3:
                        probs_lo(n - 1, 3)
                    if g == LAG - SLOTS // 2:
                        inverse_sums(n - 1, 0)
                    if g == LAG - SLOTS // 2 + 1:
                        normalise(n - 1, 1 - u, 0)
                    if g == 7:
                        probs_lo(n, 0)
                    if g == VALUES_AT + 2:
                        values_lo(n, u)
                    if g == MAXIMA_AT + 1:
                        maxima_parts(n + 1)
                    if g == LAG:
                        inverse_sums(n - 1, 1)
                        probs_lo(n, 1)
                    if g == LAG + 1:
                        normalise(n - 1, 1 - u, 1)
                    if g == 15:
                        probs_lo(n, 2)
            loop_pairs(dve, step, FIRST, FROM, TO, LAST)

        @block.tensor
        def _(pe):
            pe.wait_ge(ident_in, 16)
            pe.wait_ge(ones_set, 6)

            def values_transposed(t, u, half):
                if inside(t, TILES):
                    wait(pe, v_in[u], 16 * (half + 1))
                    wait(pe, norm_done, 2 * t - 1)
                    for j in range(NT):
                        last = nc.tensor.transpose(vT[:, j, :], xv[u][:, j * P:(j + 1) * P], ident[:, :])
                    last.then_inc(vt_ready, 1)

            def scores_for_max(t, u, half, m):
                if inside(t, TILES):
                    b, i = divmod(m, NT)
                    if i == 0:
                        wait(pe, stacked[u][b], 48 * (half + 1))
                    wait(pe, max_done, SLOTS * t + m - 1)
                    nc.tensor.matmul(s1[:, m % 2, :], qk[u][0:KS, 0, b, i * P:(i + 1) * P],
                                     qk[u][0:KS, 1, b, :], start=True, stop=True).then_inc(s1_ready, 1)

            def scores(t, u, g):
                if inside(t, TILES):
                    b, j = divmod(g, NT)
                    if g == 0:
                        wait(pe, mrow_in, 32 * (t + 1))
                    if j % 2 == 0:
                        wait(pe, exp_done, 8 * t + 2 * b + j // 2 - 1)
                    last = nc.tensor.matmul(s2[:, j // 2, j % 2, :], qk[u][0:KM, 1, b, j * P:(j + 1) * P],
                                            qk[u][0:KM, 0, b, :], start=True, stop=True)
                    if j % 2 == 1:
                        last.then_inc(s2_ready, 1)

            def sum_values(t, u, q):
                if inside(t, TILES):
                    b, i = divmod(q, NT)
                    if i == 0:
                        wait(pe, plo_pool, 8 * t + 2 * b + 2)
                        wait(pe, plo_done, 4 * t + b + 1)
                        if b == 0:
                            wait(pe, vlo_done, t + 1)
                            wait(pe, mrow_done, min(t + 2, TILES) if isinstance(t, int) else t + 2)
                        elif b == 2:
                            wait(pe, htok_ready, t)
                    out = sums[b // 2][:, b % 2, i, :]
                    rows = slice(i * P, (i + 1) * P)
                    nc.tensor.matmul(out, prob[b][:, 0, rows], v[u][:, b, :], start=True, stop=False)
                    for j in range(1, NT):
                        hi, lo = phi[b][:, j, rows], plo[b][:, j, rows]
                        nc.tensor.matmul(out, hi, vhi[u][:, j, b, :], start=False, stop=False)
                        nc.tensor.matmul(out[:, 0:C], hi, vlo[u][:, j, b, :], start=False, stop=False)
                        last = nc.tensor.matmul(out, lo, vhi[u][:, j, b, :], start=False, stop=j == NT - 1)
                    if i == NT - 1:
                        last.then_inc(pv_done, 1)

            def tokens(t, u):
                if inside(t, TILES):
                    wait(pe, norm_done, 2 * t + 2)
                    for i in range(NT):
                        last = nc.tensor.transpose(tokT[:, i, :], hT[u][:, i, :, :].rearrange("p b c -> p (b c)"),
                                                   ident[:, :])
                    last.then_inc(htr_done, 1)

            def maxima(t, u):
                if inside(t, TILES):
                    wait(pe, max_done, SLOTS * (t + 1))
                    wait(pe, vlo_done, t)
                    nc.tensor.transpose(bankA[0:SLOTS, 0:P], negmax[u][:, :], ident[:, :]).then_inc(mt_ready, 1)

            def step(k, u):
                n = 2 * k + u
                for g in range(SLOTS):
                    ahead, m = divmod(g + LEAD, SLOTS)
                    scores_for_max(n + 1 + ahead, (u + 1 + ahead) % 2, k + (u + 1 + ahead) // 2, m)
                    scores(n, u, g)
                    if g < LAG:
                        sum_values(n - 1, 1 - u, SLOTS + g - LAG)
                    else:
                        sum_values(n, u, g - LAG)
                    if g == TOKENS_AT:
                        tokens(n - 1, 1 - u)
                    if g == MAXIMA_AT:
                        maxima(n + 1, 1 - u)
                    if g == VALUES_AT:
                        values_transposed(n, u, k)
            loop_pairs(pe, step, FIRST, FROM, TO, LAST)
def attention(nc, pre, h_dram, out_dram, wqkv_dram, wo_dram, const, HKV, D, rope, TILES=32, prefetch=None):
    P, L, DM = 128, 32, 512
    R = 4
    B = P // L
    KT = DM // P
    G = HKV // 2
    DQ, DKV = R * HKV * D, HKV * D
    DALL = DQ + 2 * DKV
    NB = HKV * B * L
    SB = max(1, NB // 512)
    W = D + 1
    SCALE, EPS = float(D) ** -0.5, 1e-5
    with ExitStack() as ctx:
        sb = lambda name, shape, dt: ctx.enter_context(nc.sbuf_tensor(pre + name, shape, dt))
        sem = semaphores(nc, ctx, pre)
        ps = lambda name, shape, dt: ctx.enter_context(nc.psum_tensor(pre + name, shape, dt))
        pair = lambda name, shape, dt: [sb(f"{name}{i}", shape, dt) for i in range(2)]
        ident = sb("ident", [P, P], F32)
        ident16 = sb("ident16", [P, P], F16)
        select = sb("select", [96, P], BF16)
        bias = sb("bias", [96, NB], BF16)
        own = sb("own", [P, B], F32)
        minus_half = sb("minus_half", [P, 1], F32)
        wstage = sb("wstage", [P, KT, DALL], F32)
        wostage = sb("wostage", [P, R * DM], F32)
        wqkv = [sb(f"wqkv{i}", [P, KT, DALL], F16) for i in range(2)]
        wo = [sb(f"wo{i}", [P, R, DM], F16) for i in range(2)]
        if rope:
            cos = sb("cos", [P, 16], F32)
            sin = sb("sin", [P, 2, 8], F32)
            turned = sb("turned", [P, DQ + DKV], F32)
            crossed = sb("crossed", [P, DQ + DKV], F32)
            rot = sb("rot", [P, DQ + DKV], F32)
        hin, hres, hout = pair("hin", [P, DM], F32), pair("hres", [P, DM], F32), pair("hout", [P, DM], F32)
        stats, mv, rstd = pair("stats", [P, 6], F32), pair("mv", [P, 2], F32), pair("rstd", [P, 1], F32)
        veps = pair("veps", [P, 1], F32)
        xn = pair("xn", [P, DM], F32)
        xhi, xlo = pair("xhi", [P, KT, P], F16), pair("xlo", [P, KT, P], F16)
        qkv = pair("qkv", [P, DALL], F32)
        qs = sb("qs", [P, R, HKV, 2, D], F16)
        kp = sb("kp", [P, 2, HKV, 2, D], F16)
        v16, vrest = sb("v16", [P, DKV], F16), sb("vrest", [P, DKV], F32)
        vhi, vlo = pair("vhi", [P, HKV, B, W], F16), pair("vlo", [P, HKV, B, W], F16)
        qT = sb("qT", [P, 2, B, R, L], F16)
        kT = sb("kT", [P, 2, 2, B, G, L], F16)
        mx = sb("mx", [P, HKV * B], F32)
        shifted = sb("shifted", [P, NB], F32)
        prob = sb("prob", [P, HKV, B, L], F32)
        pThi, pTlo = sb("pThi", [P, HKV, P], F16), sb("pTlo", [P, HKV, P], F16)
        rden = sb("rden", [P, 2, G, B], F32)
        y = sb("y", [P, B, HKV, D], F32)
        yThi, yTlo = sb("yThi", [P, R, B, L], F16), sb("yTlo", [P, R, B, L], F16)

        bankA = ps("bankA", [P, 512], F32)
        bankB = ps("bankB", [P, 512], F32)
        bankC = ps("bankC", [P, 512], F32)
        bankD = ps("bankD", [P, 1024], F16)
        bankS = ps("bankS", [P, 1024], F32)
        bankO = ps("bankO", [P, 2, 512], F32)
        S = bankS[:, 0:NB]
        kTp = bankC[:, :].bitcast(F16)[:, 0:4 * P]
        O = bankO[:, :, 0:G * B * W].rearrange("p f (g b w) -> p f g b w", g=G, b=B)

        c_in, wo_in = sem("c_in"), sem("wo_in")
        w_in = [sem(f"w_in{j}") for j in range(KT)]
        w_hi, w_ready = sem("w_hi"), sem("w_ready")
        set_up = sem("set_up")
        h_in = [sem(f"h_in{i}") for i in range(2)]
        res_in = [sem(f"res_in{i}") for i in range(2)]
        stored = [sem(f"stored{i}") for i in range(2)]
        names = ("stats_done mv_done veps_done rstd_done xn_done xT_ready xhi_done xlo_done q_ready kv_ready "
                 "q_copied kv_copied turned_done crossed_done rot_done qhi_done qlo_done khi_done klo_done "
                 "v16_done vrest_done v_done qT_ready kT_ready qT_copied kT_act kT_dve s_ready max_done "
                 "shift_done exp_done pT_ready pThi_done pTlo_done o_ready rden_done y_done yT_ready "
                 "yThi_done yTlo_done z_ready out_done sp_passed pool_passed dve_passed").split()
        s = {n: sem(n) for n in names}

        FIRST, FROM, TO, LAST = -5, 4, (TILES - 5) // 2 * 2, TILES + 2
        block = ctx.enter_context(nc.Block())

        @block.sync
        def _(sp):
            consts = [(ident, "ident"), (ident16, "ident16"), (select, "select"), (bias, pre + "bias"),
                      (own, "own")]
            if rope:
                consts += [(cos, "cos"), (sin, "sin")]
            for j in range(KT):
                sp.dma_start(wstage[:, j, :], wqkv_dram[j * P:(j + 1) * P, :]).then_inc(w_in[j], 16)
            for dst, name in consts:
                sp.dma_start(dst[:], const[name]).then_inc(c_in, 16)
            sp.dma_start(wostage[:, :].rearrange("p (r n) -> p r n", r=R),
                         wo_dram.rearrange("(r p) n -> p r n", p=P)).then_inc(wo_in, 16)

            def load(t, u):
                if inside(t, TILES):
                    wait_alone(sp, s["sp_passed"], s["xn_done"], t - 1)
                    sp.dma_start(hin[u][:, :], h_dram[bass.ds(t * P, P), :]).then_inc(h_in[u], 16)

            def load_residual(t, u):
                if inside(t, TILES):
                    wait_alone(sp, s["sp_passed"], s["out_done"], t - 1)
                    sp.dma_start(hres[u][:, :], h_dram[bass.ds(t * P, P), :]).then_inc(res_in[u], 16)

            def store(t, u):
                if inside(t, TILES):
                    wait_alone(sp, s["sp_passed"], s["out_done"], t + 1)
                    sp.dma_start(out_dram[bass.ds(t * P, P), :], hout[u][:, :]).then_inc(stored[u], 16)

            def step(k, u):
                n = 2 * k + u
                load(n + 5, 1 - u)
                store(n - 2, u)
                load_residual(n, u)
                if prefetch is not None and isinstance(n, int) and 1 <= n < FROM:
                    prefetch(sp, n - 1)
            loop_pairs(sp, step, FIRST, FROM, TO, LAST)
            for u in range(2):
                sp.wait_ge(stored[u], 16 * (TILES // 2))

        @block.gpsimd
        def _(pool):
            pool.wait_ge(c_in, 16 * (7 if rope else 5))
            pool.wait_ge(set_up, 8)

            def inverse_deviation(t, u):
                if inside(t, TILES):
                    wait(pool, s["veps_done"], t + 1)
                    pool.tensor_tensor(rstd[u][:, :], veps[u][:, :], minus_half[:, :], ALU.pow)\
                        .then_inc(s["rstd_done"], 1)

            def cross(t, u, part):
                if inside(t, TILES) and rope:
                    wait_alone(pool, s["pool_passed"], s[("q_copied", "kv_copied")[part]], t + 1)
                    if part == 0:
                        wait_alone(pool, s["pool_passed"], s["rot_done"], t)
                    cols = (slice(0, DQ), slice(DQ, DQ + DKV))[part]
                    n = (DQ, DKV)[part] // 16
                    src = qkv[u][:, cols].rearrange("p (h i e) -> p h i e", e=2, i=8)
                    dst = crossed[:, cols].rearrange("p (h i e) -> p h i e", e=2, i=8)
                    for e in range(2):
                        pool.tensor_tensor(dst[:, :, :, e], src[:, :, :, 1 - e],
                                           sin[:, e, :].unsqueeze(1).broadcast_to([P, n, 8]),
                                           ALU.mult).then_inc(s["crossed_done"], 1)

            def values(t, u):
                if inside(t, TILES):
                    wait_alone(pool, s["pool_passed"], s["kv_copied"], t + 1)
                    wait_alone(pool, s["pool_passed"], s["o_ready"], t - 1)
                    v = qkv[u][:, DQ + DKV:DALL]
                    spread = lambda a: a.rearrange("p (h d) -> p h d", h=HKV).unsqueeze(2)\
                        .broadcast_to([P, HKV, B, D])
                    mask = own[:, :].unsqueeze(1).unsqueeze(3).broadcast_to([P, HKV, B, D])
                    pool.tensor_copy(v16[:, :], v).then_inc(s["v16_done"], 1)
                    pool.tensor_tensor(vhi[u][:, :, :, 0:D], spread(v), mask, ALU.mult).then_inc(s["v_done"], 1)
                    wait_alone(pool, s["pool_passed"], s["v16_done"], t + 1)
                    pool.tensor_tensor(vrest[:, :], v, v16[:, :], ALU.subtract).then_inc(s["vrest_done"], 1)
                    wait_alone(pool, s["pool_passed"], s["vrest_done"], t + 1)
                    pool.tensor_tensor(vlo[u][:, :, :, 0:D], spread(vrest[:, :]), mask, ALU.mult)\
                        .then_inc(s["v_done"], 1)

            def step(k, u):
                n = 2 * k + u
                values(n + 1, 1 - u)
                inverse_deviation(n + 4, u)
                cross(n + 2, u, 0)
                cross(n + 2, u, 1)
            loop_pairs(pool, step, FIRST, FROM, TO, LAST)

        @block.scalar
        def _(act):
            for j in range(KT):
                act.wait_ge(w_in[j], 16)
                nc.scalar.copy(wqkv[0][:, j, :], wstage[:, j, :]).then_inc(w_hi, 1)
            act.wait_ge(wo_in, 16)
            nc.scalar.copy(wo[0][:, :, :], wostage[:, :].rearrange("p (r n) -> p r n", r=R)).then_inc(w_hi, 1)
            act.wait_ge(set_up, 8)

            def copy_qT(t):
                if inside(t, TILES):
                    wait(act, s["qT_ready"], t + 1)
                    wait(act, s["s_ready"], t)
                    for f in range(2):
                        last = nc.scalar.copy(qT[:, f, :, :, :].rearrange("p b r q -> p r b q"),
                                              bankD[:, f * R * P:(f + 1) * R * P]
                                              .rearrange("p (r b q) -> p r b q", r=R, b=B))
                    last.then_inc(s["qT_copied"], 1)

            def copy_kT(t):
                if inside(t, TILES):
                    wait(act, s["kT_dve"], t + 1)
                    for j in range(G // 2, G):
                        rows = slice(j * P // G, (j + 1) * P // G)
                        last = nc.scalar.copy(kT[rows, :, :, :, j, :].rearrange("p a f b k -> p (a f b) k"),
                                              kTp[rows, :].rearrange("p (n k) -> p n k", k=L))
                    last.then_inc(s["kT_act"], 1)

            def x_hi(t, u):
                if inside(t, TILES):
                    wait(act, s["xT_ready"], t + 1)
                    wait(act, s["kv_ready"], t - 1)
                    nc.scalar.copy(xhi[u][:, :, :], bankA[:, :].rearrange("p (j n) -> p j n", j=KT))\
                        .then_inc(s["xhi_done"], 1)

            def exps(t):
                if inside(t, TILES):
                    wait(act, s["shift_done"], t + 1)
                    wait(act, s["pT_ready"], t)
                    for f in range(2):
                        half = slice(f * NB // 2, (f + 1) * NB // 2)
                        last = nc.scalar.activation(
                            prob[:, f * G:(f + 1) * G, :, :].rearrange("p g b k -> p b g k"),
                            shifted[:, half].rearrange("p (b g k) -> p b g k", b=B, g=G), ACT.Exp, scale=SCALE)
                    last.then_inc(s["exp_done"], 1)

            def copy_q(t, u):
                if inside(t, TILES):
                    wait(act, s["q_ready"], t + 1)
                    wait(act, s["klo_done"], t - 1)
                    wait(act, s["v_done"], 2 * (t - 1))
                    nc.scalar.copy(qkv[u][:, 0:DQ], bankB[:, 0:DQ]).then_inc(s["q_copied"], 1)

            def copy_kv(t, u):
                if inside(t, TILES):
                    wait(act, s["kv_ready"], t + 1)
                    nc.scalar.copy(qkv[u][:, DQ:DALL], bankC[:, 0:2 * DKV]).then_inc(s["kv_copied"], 1)

            def probs_hi(t):
                if inside(t, TILES):
                    wait(act, s["pT_ready"], t + 1)
                    wait(act, s["o_ready"], t)
                    nc.scalar.copy(pThi[:, :, :], bankS[:, 0:HKV * P].rearrange("p (h n) -> p h n", h=HKV))\
                        .then_inc(s["pThi_done"], 1)

            def y_hi(t):
                if inside(t, TILES):
                    wait(act, s["yT_ready"], t + 1)
                    wait(act, s["z_ready"], t)
                    nc.scalar.copy(yThi[:, :, :, :].rearrange("p r b q -> p b r q"),
                                   bankA[:, :].rearrange("p (b r q) -> p b r q", b=B, r=R))\
                        .then_inc(s["yThi_done"], 1)

            def qk_hi(t, u):
                if inside(t, TILES):
                    if rope:
                        wait(act, s["rot_done"], t + 1)
                    else:
                        wait(act, s["q_copied"], t + 1)
                        wait(act, s["kv_copied"], t + 1)
                    wait(act, s["kT_ready"], t)
                    src = rot if rope else qkv[u]
                    nc.scalar.copy(qs[:, :, :, 0, :], src[:, 0:DQ].rearrange("p (h r d) -> p r h d", h=HKV, r=R))\
                        .then_inc(s["qhi_done"], 1)
                    nc.scalar.copy(kp[:, 0, :, :, :], src[:, DQ:DQ + DKV].rearrange("p (h d) -> p h d", h=HKV)
                                   .unsqueeze(2).broadcast_to([P, HKV, 2, D])).then_inc(s["khi_done"], 1)

            def step(k, u):
                n = 2 * k + u
                copy_qT(n + 1)
                copy_kT(n + 1)
                if rope:
                    copy_q(n + 2, u)
                exps(n)
                y_hi(n - 1)
                if not rope:
                    copy_q(n + 2, u)
                copy_kv(n + 2, u)
                probs_hi(n)
                qk_hi(n + 2, u)
                x_hi(n + 3, 1 - u)
            loop_pairs(act, step, FIRST, FROM, TO, LAST)

        @block.vector
        def _(dve):
            dve.memset(minus_half[:, :], -0.5).then_inc(set_up, 1)
            for i in range(4):
                dve.memset(kT[:, i // 2, i % 2, :, :, :], 0.0).then_inc(set_up, 1)
            dve.wait_ge(c_in, 16 * (7 if rope else 5))
            for u in range(2):
                nc.vector.tensor_copy(vhi[u][:, :, :, D], own[:, :].unsqueeze(1).broadcast_to([P, HKV, B]))\
                    .then_inc(set_up, 1)
            dve.memset(vlo[0][:, :, :, D], 0.0)
            dve.memset(vlo[1][:, :, :, D], 0.0).then_inc(set_up, 1)
            for j in range(KT):
                dve.wait_ge(w_hi, j + 1)
                nc.vector.tensor_tensor(wqkv[1][:, j, :], wstage[:, j, :], wqkv[0][:, j, :], ALU.subtract)\
                    .then_inc(w_ready, 1)
            dve.wait_ge(w_hi, KT + 1)
            nc.vector.tensor_tensor(wo[1][:, :, :], wostage[:, :].rearrange("p (r n) -> p r n", r=R),
                                    wo[0][:, :, :], ALU.subtract).then_inc(w_ready, 1)

            def row_stats(t, u):
                if inside(t, TILES):
                    nc.vector.bn_stats(stats[u][:, :], hin[u][:, :]).then_inc(s["stats_done"], 1)

            def mean_variance(t, u):
                if inside(t, TILES):
                    wait_alone(dve, s["dve_passed"], s["stats_done"], t + 1)
                    nc.vector.bn_aggr(mv[u][:, :], stats[u][:, :]).then_inc(s["mv_done"], 1)

            def variance_eps(t, u):
                if inside(t, TILES):
                    wait(dve, s["mv_done"], t + 1)
                    nc.vector.tensor_scalar(veps[u][:, :], mv[u][:, 1:2], EPS, None, ALU.add)\
                        .then_inc(s["veps_done"], 1)

            def x_normalised(t, u):
                if inside(t, TILES):
                    wait(dve, s["rstd_done"], t + 1)
                    wait(dve, s["xT_ready"], t - 1)
                    nc.vector.tensor_scalar(xn[u][:, :], hin[u][:, :], mv[u][:, 0:1], rstd[u][:, :],
                                            ALU.subtract, ALU.mult).then_inc(s["xn_done"], 1)

            def copy_kT(t):
                if inside(t, TILES):
                    wait(dve, s["kT_ready"], t + 1)
                    wait(dve, s["s_ready"], t)
                    for j in range(G // 2):
                        rows = slice(j * P // G, (j + 1) * P // G)
                        last = nc.vector.tensor_copy(kT[rows, :, :, :, j, :].rearrange("p a f b k -> p (a f b) k"),
                                                     kTp[rows, :].rearrange("p (n k) -> p n k", k=L))
                    last.then_inc(s["kT_dve"], 1)

            def residual(t, u, half):
                if inside(t, TILES):
                    wait(dve, s["z_ready"], t + 1)
                    wait(dve, res_in[u], 16 * (half + 1))
                    wait(dve, stored[u], 16 * half)
                    nc.vector.tensor_tensor(hout[u][:, :], bankB[:, :], hres[u][:, :], ALU.add)\
                        .then_inc(s["out_done"], 1)

            def maxes(t):
                if inside(t, TILES):
                    wait(dve, s["s_ready"], t + 1)
                    nc.vector.tensor_reduce(mx[:, :], S.rearrange("p (n k) -> p n k", k=L), AX.X, ALU.max)\
                        .then_inc(s["max_done"], 1)

            def shift(t):
                if inside(t, TILES):
                    wait(dve, s["max_done"], t + 1)
                    wait(dve, s["exp_done"], t)
                    nc.vector.tensor_tensor(shifted[:, :].rearrange("p (n k) -> p n k", k=L),
                                            S.rearrange("p (n k) -> p n k", k=L),
                                            mx[:, :].unsqueeze(2).broadcast_to([P, HKV * B, L]), ALU.subtract)\
                        .then_inc(s["shift_done"], 1)

            def x_lo(t, u):
                if inside(t, TILES):
                    wait(dve, s["xhi_done"], t + 1)
                    nc.vector.tensor_tensor(xlo[u][:, :, :], bankA[:, :].rearrange("p (j n) -> p j n", j=KT),
                                            xhi[u][:, :, :], ALU.subtract).then_inc(s["xlo_done"], 1)

            def probs_lo(t):
                if inside(t, TILES):
                    wait(dve, s["pThi_done"], t + 1)
                    nc.vector.tensor_tensor(pTlo[:, :, :], bankS[:, 0:HKV * P].rearrange("p (h n) -> p h n", h=HKV),
                                            pThi[:, :, :], ALU.subtract).then_inc(s["pTlo_done"], 1)

            def turn(t, u, part):
                if inside(t, TILES) and rope:
                    wait(dve, s[("q_copied", "kv_copied")[part]], t + 1)
                    cols = (slice(0, DQ), slice(DQ, DQ + DKV))[part]
                    n = (DQ, DKV)[part] // 16
                    nc.vector.tensor_tensor(turned[:, cols].rearrange("p (n d) -> p n d", d=16),
                                            qkv[u][:, cols].rearrange("p (n d) -> p n d", d=16),
                                            cos[:, :].unsqueeze(1).broadcast_to([P, n, 16]), ALU.mult)\
                        .then_inc(s["turned_done"], 1)

            def rotate(t):
                if inside(t, TILES) and rope:
                    wait(dve, s["turned_done"], 2 * t + 2)
                    wait(dve, s["crossed_done"], 4 * t + 4)
                    wait(dve, s["khi_done"], t)
                    nc.vector.tensor_tensor(rot[:, :], turned[:, :], crossed[:, :], ALU.add)\
                        .then_inc(s["rot_done"], 1)

            def inverse_sums(t):
                if inside(t, TILES):
                    wait(dve, s["o_ready"], t + 1)
                    nc.vector.reciprocal(rden[:, :, :, :].rearrange("p f g b -> p f (g b)"),
                                         bankO[:, :, 0:G * B * W].rearrange("p f (n w) -> p f n w", w=W)[:, :, :, D])\
                        .then_inc(s["rden_done"], 1)

            def normalise(t):
                if inside(t, TILES):
                    wait(dve, s["rden_done"], t + 1)
                    wait(dve, s["yT_ready"], t)
                    for f in range(2):
                        last = nc.vector.tensor_tensor(
                            y[:, :, f * G:(f + 1) * G, :].rearrange("p b g d -> p g b d"), O[:, f, :, :, 0:D],
                            rden[:, f, :, :].unsqueeze(3).broadcast_to([P, G, B, D]), ALU.mult)
                    last.then_inc(s["y_done"], 1)

            def y_lo(t):
                if inside(t, TILES):
                    wait(dve, s["yThi_done"], t + 1)
                    nc.vector.tensor_tensor(yTlo[:, :, :, :].rearrange("p r b q -> p b r q"),
                                            bankA[:, :].rearrange("p (b r q) -> p b r q", b=B, r=R),
                                            yThi[:, :, :, :].rearrange("p r b q -> p b r q"), ALU.subtract)\
                        .then_inc(s["yTlo_done"], 1)

            def qk_lo(t, u):
                if inside(t, TILES):
                    wait(dve, s["qhi_done"], t + 1)
                    src = rot if rope else qkv[u]
                    nc.vector.tensor_tensor(qs[:, :, :, 1, :], src[:, 0:DQ].rearrange("p (h r d) -> p r h d", h=HKV, r=R),
                                            qs[:, :, :, 0, :], ALU.subtract).then_inc(s["qlo_done"], 1)
                    wait(dve, s["khi_done"], t + 1)
                    nc.vector.tensor_tensor(kp[:, 1, :, :, :], src[:, DQ:DQ + DKV].rearrange("p (h d) -> p h d", h=HKV)
                                            .unsqueeze(2).broadcast_to([P, HKV, 2, D]),
                                            kp[:, 0, :, :, :], ALU.subtract).then_inc(s["klo_done"], 1)

            def step(k, u):
                n = 2 * k + u
                residual(n - 2, u, k - 1)
                maxes(n)
                copy_kT(n + 1)
                inverse_sums(n - 1)
                normalise(n - 1)
                shift(n)
                if inside(n + 4, TILES):
                    wait(dve, h_in[u], 16 * (k + 3))
                row_stats(n + 4, u)
                mean_variance(n + 4, u)
                variance_eps(n + 4, u)
                turn(n + 2, u, 0)
                x_normalised(n + 4, u)
                y_lo(n - 1)
                turn(n + 2, u, 1)
                rotate(n + 2)
                probs_lo(n)
                qk_lo(n + 2, u)
                x_lo(n + 3, 1 - u)
            loop_pairs(dve, step, FIRST, FROM, TO, LAST)

        @block.tensor
        def _(pe):
            pe.wait_ge(c_in, 16 * (7 if rope else 5))
            pe.wait_ge(set_up, 8)
            pe.wait_ge(w_ready, KT)

            def transpose_qk(t):
                if inside(t, TILES):
                    wait(pe, s["qlo_done"], t + 1)
                    wait(pe, s["qT_copied"], t)
                    for f in range(2):
                        for r in range(R):
                            at = (f * R + r) * P
                            last = nc.tensor.transpose(bankD[:, at:at + P],
                                                       qs[:, r, f * G:(f + 1) * G, :, :]
                                                       .rearrange("p g a d -> p (g a d)"), ident16[:, :])
                    last.then_inc(s["qT_ready"], 1)
                    wait(pe, s["klo_done"], t + 1)
                    wait(pe, s["kv_copied"], t + 1)
                    for a in range(2):
                        for f in range(2):
                            at = (a * 2 + f) * P
                            last = nc.tensor.transpose(kTp[:, at:at + P],
                                                       kp[:, a, f * G:(f + 1) * G, :, :]
                                                       .rearrange("p g e d -> p (g e d)"), ident16[:, :])
                    last.then_inc(s["kT_ready"], 1)

            def project_out(t):
                if inside(t, TILES):
                    if isinstance(t, int) and t == 0:
                        wait(pe, w_ready, KT + 1)
                    wait(pe, s["yTlo_done"], t + 1)
                    wait(pe, s["q_copied"], t + 4 if not isinstance(t, int) else min(t + 4, TILES))
                    n = 0
                    for r in range(R):
                        hi, lo = (a[:, r, :, :].rearrange("p b q -> p (b q)") for a in (yThi, yTlo))
                        for a, w in ((hi, wo[0]), (hi, wo[1]), (lo, wo[0])):
                            last = nc.tensor.matmul(bankB[:, :], a, w[:, r, :], start=n == 0, stop=n == 3 * R - 1)
                            n += 1
                    last.then_inc(s["z_ready"], 1)

            def scores(t):
                if inside(t, TILES):
                    wait(pe, s["qT_copied"], t + 1)
                    wait(pe, s["kT_act"], t + 1)
                    wait(pe, s["pTlo_done"], t)
                    cols = NB // 2 // B
                    for i in range(SB):
                        span = slice(i * NB // SB, (i + 1) * NB // SB)
                        nc.tensor.matmul(S[:, span], select[:, :], bias[:, span], start=True, stop=False)
                        blocks = [(f, b) for f in range(2) for b in range(B)]
                        mine = blocks[i * len(blocks) // SB:(i + 1) * len(blocks) // SB]
                        for f, b in mine:
                            at = (f * B + b) * cols
                            for a in range(2):
                                last = nc.tensor.matmul(S[:, at:at + cols], qT[:, f, b, :, :].rearrange("p r q -> p (r q)"),
                                                        kT[:, a, f, b, :, :].rearrange("p g k -> p (g k)"),
                                                        start=False, stop=(f, b) == mine[-1] and a == 1)
                    last.then_inc(s["s_ready"], 1)

            def transpose_x(t, u):
                if inside(t, TILES):
                    wait(pe, s["xn_done"], t + 1)
                    wait(pe, s["yTlo_done"], t - 3)
                    for j in range(KT):
                        last = nc.tensor.transpose(bankA[:, j * P:(j + 1) * P], xn[u][:, j * P:(j + 1) * P], ident[:, :])
                    last.then_inc(s["xT_ready"], 1)

            def project(t, u, out, cols, done, free, used):
                if inside(t, TILES):
                    wait(pe, s["xlo_done"], t + 1)
                    wait(pe, s[free], used)
                    n = 0
                    for j in range(KT):
                        for a, w in ((xhi, wqkv[0]), (xhi, wqkv[1]), (xlo, wqkv[0])):
                            last = nc.tensor.matmul(out, a[u][:, j, :], w[:, j, cols], start=n == 0,
                                                    stop=n == 3 * KT - 1)
                            n += 1
                    last.then_inc(s[done], 1)

            def transpose_probs(t):
                if inside(t, TILES):
                    wait(pe, s["exp_done"], t + 1)
                    for h in range(HKV):
                        last = nc.tensor.transpose(bankS[:, h * P:(h + 1) * P],
                                                   prob[:, h, :, :].rearrange("p b k -> p (b k)"), ident[:, :])
                    last.then_inc(s["pT_ready"], 1)

            def weigh_values(t, u):
                if inside(t, TILES):
                    wait(pe, s["pTlo_done"], t + 1)
                    wait(pe, s["v_done"], 2 * t + 2)
                    wait(pe, s["y_done"], t)
                    for h in range(HKV):
                        out = bankO[:, h // G, (h % G) * B * W:(h % G + 1) * B * W]
                        for n, (p, v) in enumerate(((pThi, vhi), (pThi, vlo), (pTlo, vhi))):
                            last = nc.tensor.matmul(out, p[:, h, :], v[u][:, h, :, :].rearrange("p b w -> p (b w)"),
                                                    start=n == 0, stop=n == 2)
                    last.then_inc(s["o_ready"], 1)

            def transpose_y(t):
                if inside(t, TILES):
                    wait(pe, s["y_done"], t + 1)
                    wait(pe, s["xlo_done"], t + 4 if not isinstance(t, int) else min(t + 4, TILES))
                    for b in range(B):
                        last = nc.tensor.transpose(bankA[:, b * P:(b + 1) * P],
                                                   y[:, b, :, :].rearrange("p h d -> p (h d)"), ident[:, :])
                    last.then_inc(s["yT_ready"], 1)

            def step(k, u):
                n = 2 * k + u
                scores(n)
                transpose_qk(n + 1)
                weigh_values(n - 1, 1 - u)
                project(n + 2, u, bankB[:, 0:DQ], slice(0, DQ), "q_ready", "out_done", n - 1)
                transpose_y(n - 1)
                project(n + 2, u, bankC[:, 0:2 * DKV], slice(DQ, DALL), "kv_ready", "kT_act", n + 2)
                transpose_probs(n)
                transpose_x(n + 3, 1 - u)
                project_out(n - 1)
            loop_pairs(pe, step, FIRST, FROM, TO, LAST)
def load_ternary(sp, src, stage, arrived):
    P = 128
    K, M = src.shape
    full = K // P
    v = stage[:, :].rearrange("p (j n) -> p j n", n=M)
    if K % P:
        sp.dma_start(v[0:K % P, full, :], src[full * P:K, :]).then_inc(arrived, 16)
    sp.dma_start(v[:, 0:full, :], src[0:full * P, :].rearrange("(j p) n -> p j n", p=P)).then_inc(arrived, 16)


def ternary_weights(nc, sources, stage, arrived, targets, scales, counts):
    P = 128
    with ExitStack() as ctx:
        sb = lambda name, shape, dt: ctx.enter_context(nc.sbuf_tensor("tw_" + name, shape, dt))
        sem = semaphores(nc, ctx, "tw_")
        sizes = [t.shape[1] * t.shape[2] for t in targets]
        below = [sb(f"below{i}", [P, sizes[i]], F16) for i in range(3)]
        signs = sb("signs", [P, max(sizes)], F16)
        ones = sb("ones", [P, P], F32)
        rows = sb("rows", [P, 3], F32)
        last_rows = sb("last_rows", [P, 1], F32)
        bounds = sb("bounds", [P, 2, 3], F32)
        total = ctx.enter_context(nc.psum_tensor("tw_total", [P, 512], F32))
        cleared, summed, summed2, totalled, bounded, signed, below_done, below2_done, done = (
            sem(n) for n in "cleared summed summed2 totalled bounded signed below_done below2_done done".split())
        K, M = sources[2].shape
        full, rest = K // P * M, K % P
        flat = lambda t: t[:, :, :].rearrange("p j n -> p (j n)")
        block = ctx.enter_context(nc.Block())

        @block.tensor
        def _(pe):
            pe.wait_ge(summed, 2)
            pe.wait_ge(summed2, 2)
            pe.wait_ge(cleared, 1)
            nc.tensor.matmul(total[:, 0:3], ones[:, :], rows[:, :], start=True, stop=False)
            nc.tensor.matmul(total[:, 2:3], ones[0:rest, :], last_rows[0:rest, :], start=False, stop=True)\
                .then_inc(totalled, 1)

        @block.scalar
        def _(act):
            for i in range(2):
                act.wait_ge(arrived[i], 16)
                if i:
                    act.wait_ge(summed, 1)
                nc.scalar.activation(signs[:, 0:sizes[i]], stage[i][:, :], ACT.Abs, accum_out=rows[:, i:i + 1])\
                    .then_inc(summed, 1)
            act.wait_ge(bounded, 9)
            for i in range(2):
                if i == 0:
                    act.wait_ge(summed, 2)
                if i:
                    act.wait_ge(below_done, i)
                nc.scalar.activation(signs[:, 0:sizes[i]], stage[i][:, :], ACT.Sign, bias=bounds[:, 0, i:i + 1])\
                    .then_inc(signed, 1)
                act.wait_ge(signed, i + 1)
                nc.scalar.activation(below[i][:, :], signs[:, 0:sizes[i]], ACT.Relu, scale=-1.0)\
                    .then_inc(below_done, 1)

        @block.vector
        def _(dve):
            dve.memset(ones[:, :], 1.0).then_inc(cleared, 1)
            dve.wait_ge(arrived[2], 32)
            nc.vector.tensor_reduce(rows[:, 2:3], stage[2][:, 0:full], AX.X, ALU.add,
                                    apply_absolute_value=True).then_inc(summed2, 1)
            nc.vector.tensor_reduce(last_rows[0:rest, :], stage[2][0:rest, full:full + M], AX.X, ALU.add,
                                    apply_absolute_value=True).then_inc(summed2, 1)
            dve.wait_ge(totalled, 1)
            for i in range(3):
                for sign, to in ((0.5, bounds[:, 0, i:i + 1]), (-0.5, bounds[:, 1, i:i + 1]),
                                 (1.0, scales[:, i:i + 1])):
                    nc.vector.tensor_scalar(to, total[:, i:i + 1], 1.0 / counts[i], sign, ALU.mult, ALU.mult)\
                        .then_inc(bounded, 1)
            dve.wait_ge(bounded, 9)
            parts = ((slice(0, P), slice(0, full)), (slice(0, rest), slice(full, full + M)))
            for n, (p, c) in enumerate(parts):
                nc.vector.tensor_scalar(below[2][p, c], stage[2][p, c], bounds[p, 1, 2:3], None, ALU.is_lt)\
                    .then_inc(below2_done, 1)
            for i in (2, 0, 1):
                if i == 2:
                    dve.wait_ge(below2_done, 2)
                else:
                    dve.wait_ge(below_done, i + 1)
                for p, c in parts if i == 2 else ((slice(0, P), slice(0, sizes[i])),):
                    nc.vector.scalar_tensor_tensor(flat(targets[i])[p, c], stage[i][p, c], bounds[p, 0, i:i + 1],
                                                   below[i][p, c], ALU.is_gt, ALU.subtract).then_inc(done, 1)


class Fp4Weights:

    def __init__(self, nc, ctx, packed, scales, targets, const, plain=()):
        P, self.WORDS, CH = 128, 16, 512
        self.nc, self.packed, self.scales, self.targets = nc, packed, scales, targets
        self.chunks = [(which, j, c, min(CH, words.shape[1] - c)) for which, words in enumerate(packed)
                       for j in range(words.shape[0] // self.WORDS) for c in range(0, words.shape[1], CH)]
        self.is_scaled = [not (which == 0 and j in plain) for which, j, _, _ in self.chunks]
        self.arrivals = [16 * sum(1 + self.is_scaled[i] for i in range(n % 3, n + 1, 3))
                         for n in range(len(self.chunks))]
        sb = lambda name, shape, dt: ctx.enter_context(nc.sbuf_tensor("fw_" + name, shape, dt))
        sem = semaphores(nc, ctx, "fw_")
        self.const = const
        self.masks = sb("masks", [P, 2], I32)
        self.factors = sb("factors", [P, 3], F32)
        self.biases = sb("biases", [P, 2], F32)
        self.words = [sb(f"words{i}", [P, CH], I32) for i in range(3)]
        self.scale = [sb(f"scale{i}", [P, CH], F16) for i in range(3)]
        self.code = [sb(f"code{i}", [P, CH], I32) for i in range(2)]
        self.bend = [sb(f"bend{i}", [P, CH], F32) for i in range(2)]
        self.value = [sb(f"value{i}", [P, CH], F32) for i in range(4)]
        self.tables_in = sem("tables_in")
        self.arrived = [sem(f"arrived{i}") for i in range(3)]
        self.masked, self.prepared, self.joined, self.scaled, self.summed, self.valued, self.high, self.low = (
            sem(n) for n in "masked prepared joined scaled summed valued high low".split())

    def views(self, n):
        which, j, c, cols = self.chunks[n]
        return ([t[:, j, c:c + cols] for t in self.targets[which]],
                lambda bufs: bufs[n % len(bufs)][:, 0:cols])

    def load_tables(self, sp):
        for table, name in ((self.masks, "fp4_masks"), (self.factors, "fp4_factors"), (self.biases, "fp4_biases")):
            sp.dma_start(table[:, :], self.const[name]).then_inc(self.tables_in, 16)

    def load(self, eng, n):
        if 0 <= n < len(self.chunks):
            which, j, c, cols = self.chunks[n]
            _, v = self.views(n)
            if n >= 3:
                eng.wait_ge(self.valued, n - 2)
            eng.dma_start(v(self.words), self.packed[which][j * self.WORDS:(j + 1) * self.WORDS, c:c + cols]
                          .unsqueeze(1).broadcast_to([self.WORDS, 8, cols])).then_inc(self.arrived[n % 3], 16)
            if self.is_scaled[n]:
                eng.dma_start(v(self.scale), self.scales[which][j:j + 1, c:c + cols].broadcast_to([128, cols]))\
                    .then_inc(self.arrived[n % 3], 16)

    def vector_code(self, dve, n):
        if 0 <= n < len(self.chunks):
            _, v = self.views(n)
            cols = v(self.words).shape[1]
            if n == 0:
                dve.wait_ge(self.tables_in, 48)
            dve.wait_ge(self.arrived[n % 3], self.arrivals[n])
            if n >= 2:
                dve.wait_ge(self.summed, n - 1)
            self.nc.vector.tensor_tensor(v(self.code), v(self.words), self.masks[:, 0:1].broadcast_to([128, cols]),
                                         ALU.bitwise_and).then_inc(self.masked, 1)

    def vector_sign(self, dve, n):
        if 0 <= n < len(self.chunks):
            _, v = self.views(n)
            cols = v(self.words).shape[1]
            dve.wait_ge(self.masked, 2 * n + 1)
            self.nc.vector.tensor_tensor(v(self.words), v(self.words), self.masks[:, 1:2].broadcast_to([128, cols]),
                                         ALU.bitwise_and).then_inc(self.masked, 1)

    def vector_join(self, dve, n):
        if 0 <= n < len(self.chunks):
            _, v = self.views(n)
            dve.wait_ge(self.prepared, 4 * n + 2)
            self.nc.vector.tensor_tensor(v(self.value), v(self.value), v(self.bend), ALU.add)\
                .then_inc(self.joined, 1)

    def vector_low(self, dve, n):
        if 0 <= n < len(self.chunks) and self.is_scaled[n]:
            (hi, lo), v = self.views(n)
            dve.wait_ge(self.high, n + 1)
            self.nc.vector.tensor_tensor(lo, v(self.value), hi, ALU.subtract).then_inc(self.low, 1)

    def scalar_prepare(self, act, n):
        if 0 <= n < len(self.chunks):
            _, v = self.views(n)
            code, signs = v(self.code), v(self.words)
            act.wait_ge(self.masked, 2 * n + 2)
            if n == 0:
                act.wait_ge(self.tables_in, 48)
            if n >= 4:
                act.wait_ge(self.high, n - 3)
                if sum(self.is_scaled[:n - 3]):
                    act.wait_ge(self.low, sum(self.is_scaled[:n - 3]))
            if n >= 2:
                act.wait_ge(self.joined, n - 1)
            activation = self.nc.scalar.activation
            activation(v(self.value), code, ACT.Copy, scale=self.factors[:, 0:1]).then_inc(self.prepared, 1)
            activation(v(self.bend), code, ACT.Relu, scale=self.factors[:, 0:1], bias=self.biases[:, 0:1])\
                .then_inc(self.prepared, 1)
            activation(signs.bitcast(F32), signs, ACT.Copy, scale=self.factors[:, 2:3], bias=1.0)\
                .then_inc(self.prepared, 1)
            act.wait_ge(self.prepared, 4 * n + 2)
            activation(code.bitcast(F32), code, ACT.Relu, scale=self.factors[:, 1:2], bias=self.biases[:, 1:2])\
                .then_inc(self.prepared, 1)

    def scalar_high(self, act, n):
        if 0 <= n < len(self.chunks):
            (hi, _), v = self.views(n)
            act.wait_ge(self.valued, n + 1)
            self.nc.scalar.copy(hi, v(self.value)).then_inc(self.high, 1)

    def pool_value(self, pool, n):
        if 0 <= n < len(self.chunks):
            _, v = self.views(n)
            signs = v(self.words).bitcast(F32)
            pool.wait_ge(self.prepared, 4 * n + 4)
            if self.is_scaled[n]:
                pool.wait_ge(self.arrived[n % 3], self.arrivals[n])
                pool.tensor_tensor(signs, signs, v(self.scale), ALU.mult).then_inc(self.scaled, 1)
            pool.wait_ge(self.joined, n + 1)
            pool.tensor_tensor(v(self.value), v(self.value), v(self.code).bitcast(F32), ALU.add)\
                .then_inc(self.summed, 1)
            if self.is_scaled[n]:
                pool.wait_ge(self.scaled, sum(self.is_scaled[:n + 1]))
            pool.wait_ge(self.summed, n + 1)
            pool.tensor_tensor(v(self.value), v(self.value), signs, ALU.mult).then_inc(self.valued, 1)


def feed_forward(nc, pre, h_dram, out_dram, gate, up, down, scales, const, HID, rms_out, GROUPS=8,
                 beside=None, plain=(), plain_scales=None, plain_in=None):
    P, DM, GT = 128, 512, 512
    KT, NT = DM // P, GT // P
    MT = (HID + P - 1) // P
    rows = [min(P, HID - m * P) for m in range(MT)]
    EPS, RMS_EPS = 1e-5, 1e-6
    TILES = GROUPS * NT
    assert MT % 2

    def slot(n, m):
        full = [g for g in range(GROUPS) if not FROM <= g < TO]
        if beside is None or not isinstance(n, int) or n not in full:
            return None
        at = full.index(n) * MT + m
        return None if at % 7 == 6 else at - at // 7

    with ExitStack() as ctx:
        sb = lambda name, shape, dt: ctx.enter_context(nc.sbuf_tensor(pre + name, shape, dt))
        sem = semaphores(nc, ctx, pre)
        pair = lambda name, shape, dt: [sb(f"{name}{i}", shape, dt) for i in range(2)]
        ident, minus_half = sb("ident", [P, P], F32), sb("minus_half", [P, 1], F32)
        hin, hres, hout = pair("hin", [P, DM], F32), pair("hres", [P, DM], F32), pair("hout", [P, DM], F32)
        stats, mv, veps, rstd = (pair(n, [P, w], F32) for n, w in (("stats", 6), ("mv", 2), ("veps", 1), ("rstd", 1)))
        xn = sb("xn", [P, DM], F32)
        xhi, xlo = pair("xhi", [P, KT, GT], F16), pair("xlo", [P, KT, GT], F16)
        act_out, prod = pair("act_out", [P, GT], F32), pair("prod", [P, GT], F32)
        ghi, glo = pair("ghi", [P, MT, GT], F16), pair("glo", [P, MT, GT], F16)
        if rms_out:
            square, ssum, ms, rinv = pair("square", [P, DM], F32), pair("ssum", [P, 1], F32), pair("ms", [P, 1], F32), pair("rinv", [P, 1], F32)
        gu = [[ctx.enter_context(nc.psum_tensor(f"{pre}gu{i}{w}", [P, GT], F32)) for w in "gu"] for i in range(2)]
        px = ctx.enter_context(nc.psum_tensor(pre + "px", [P, KT * P], F32))
        if plain:
            assert len(plain) == 2 and HID % P == 0
            part = [ctx.enter_context(nc.psum_tensor(f"{pre}part{w}", [P, GT], F32)) for w in "gu"]
            joined = [pair(f"joined{w}", [P, GT], F32) for w in "gu"]
            factor = sb("factor", [P, 2 * MT, KT], F32)
        PZ = 1 if plain else 2
        pz = [ctx.enter_context(nc.psum_tensor(f"{pre}pz{i}", [P, DM], F32)) for i in range(PZ)] * (2 // PZ)

        c_in, set_up, half_set = sem("c_in"), sem("set_up"), sem("half_set")
        h_in, res_in, stored = ([sem(f"{n}{i}") for i in range(2)] for n in ("h_in", "res_in", "stored"))
        names = ("stats_done mv_done veps_done rstd_done xn_done xT_ready xhi_done xlo_done gu_ready act_done "
                 "prod_done ghi_done glo_done z_ready out_done sp_passed dve_passed sq_done ms_done "
                 "rinv_done part_ready scale_done join_done add_done").split()
        s = {n: sem(n) for n in names}
        FIRST, FROM, TO, LAST = -1, 2, (GROUPS - 1) // 2 * 2, GROUPS + 1
        parts_x = [(x, w) for x in (0, 1) for w in range(len(gate)) if x + w < 2]
        xparts, gparts = (xhi, xlo), (ghi, glo)
        block = ctx.enter_context(nc.Block())

        norm_at = [3, 5, 7, 9]
        down_at = [2, 4, 6, 8]

        @block.sync
        def _(sp):
            sp.dma_start(ident[:, :], const["ident"]).then_inc(c_in, 16)
            if beside is not None:
                beside.load_tables(sp)

            def load(g, i):
                if inside(g, GROUPS):
                    t = NT * g + i
                    wait_alone(sp, s["sp_passed"], s["xn_done"], t - 1)
                    sp.dma_start(hin[i % 2][:, :], h_dram[bass.ds(t * P, P), :]).then_inc(h_in[i % 2], 16)

            def residual(g, i):
                if inside(g, GROUPS):
                    t = NT * g + i
                    wait_alone(sp, s["sp_passed"], s["out_done"], t - 1)
                    sp.dma_start(hres[i % 2][:, :], h_dram[bass.ds(t * P, P), :]).then_inc(res_in[i % 2], 16)

            def store(g, i):
                if inside(g, GROUPS):
                    t = NT * g + i
                    wait_alone(sp, s["sp_passed"], s["out_done"], t + 1)
                    sp.dma_start(out_dram[bass.ds(t * P, P), :], hout[i % 2][:, :]).then_inc(stored[i % 2], 16)

            def step(k, u):
                n = 2 * k + u
                for m in range(MT):
                    q = slot(n, m)
                    if q is not None:
                        if q == 0:
                            beside.load(sp, 0)
                        beside.load(sp, q + 1)
                    if m == 0:
                        residual(n - 1, 0)
                        residual(n - 1, 1)
                        load(n + 1, 0)
                        load(n + 1, 1)
                    if m == 3:
                        load(n + 1, 2)
                    if m == 5:
                        load(n + 1, 3)
                    if m - 2 in down_at:
                        i = down_at.index(m - 2)
                        store(n - 1, i)
                        if i < 2:
                            residual(n - 1, i + 2)
            loop_pairs(sp, step, FIRST, FROM, TO, LAST)
            for u in range(2):
                sp.wait_ge(stored[u], 16 * (TILES // 2))

        @block.gpsimd
        def _(pool):
            pool.wait_ge(half_set, 1)

            def inverse_deviation(g, i):
                if inside(g, GROUPS):
                    wait(pool, s["veps_done"], NT * g + i + 1)
                    pool.tensor_tensor(rstd[i % 2][:, :], veps[i % 2][:, :], minus_half[:, :], ALU.pow)\
                        .then_inc(s["rstd_done"], 1)

            def inverse_rms(g, i):
                if inside(g, GROUPS) and rms_out:
                    wait(pool, s["ms_done"], NT * g + i + 1)
                    pool.tensor_tensor(rinv[i % 2][:, :], ms[i % 2][:, :], minus_half[:, :], ALU.pow)\
                        .then_inc(s["rinv_done"], 1)

            def step(k, u):
                n = 2 * k + u
                for m in range(MT):
                    if m in down_at:
                        inverse_rms(n - 1, down_at.index(m))
                    q = slot(n, m)
                    if q is not None:
                        beside.pool_value(pool, q - 1)
                    if m + 3 in norm_at:
                        inverse_deviation(n + 1, norm_at.index(m + 3))
            loop_pairs(pool, step, FIRST, FROM, TO, LAST)

        @block.scalar
        def _(act):
            if plain:
                act.wait_ge(plain_in, 16)
                nc.scalar.copy(factor[:, :, :], plain_scales[:, :, :]).then_inc(set_up, 1)

            def scale_part(g, m, u, which):
                if inside(g, GROUPS) and plain:
                    n = MT * g + m
                    wait(act, s["part_ready"], 4 * n + which + 1)
                    wait(act, s[("act_done", "prod_done")[which]], n - 1)
                    nc.scalar.activation(joined[which][(m + u) % 2][:, :], part[which][:, :], ACT.Copy,
                                         scale=factor[:, which * MT + m, plain[0]:plain[0] + 1])\
                        .then_inc(s["scale_done"], 1)

            def gate_act(g, m, u):
                if inside(g, GROUPS):
                    n = MT * g + m
                    if plain:
                        wait(act, s["add_done"], 2 * n + 1)
                    else:
                        wait(act, s["gu_ready"], n + 1)
                    wait(act, s["prod_done"], n - 1)
                    src = joined[0][(m + u) % 2] if plain else gu[(m + u) % 2][0]
                    nc.scalar.activation(act_out[(m + u) % 2][0:rows[m], :], src[0:rows[m], :], ACT.Silu,
                                         scale=scales[0:rows[m], 0:1] if scales is not None else 1.0)\
                        .then_inc(s["act_done"], 1)

            def hidden_hi(g, m, u):
                if inside(g, GROUPS):
                    wait(act, s["prod_done"], MT * g + m + 1)
                    if m == 0:
                        wait(act, s["z_ready"], NT * (g - 1))
                    nc.scalar.copy(ghi[u][0:rows[m], m, :], prod[(m + u) % 2][0:rows[m], :])\
                        .then_inc(s["ghi_done"], 1)

            def x_hi(g, i, u):
                if inside(g, GROUPS):
                    wait(act, s["xT_ready"], NT * g + i + 1)
                    if i == 0:
                        if plain:
                            wait(act, s["gu_ready"], 2 * MT * (g - 1))
                        else:
                            wait(act, s["gu_ready"], MT * (g - 1))
                    nc.scalar.copy(xhi[u][:, :, i * P:(i + 1) * P], px[:, :].rearrange("p (j n) -> p j n", j=KT))\
                        .then_inc(s["xhi_done"], 1)

            def squares(g, i):
                if inside(g, GROUPS) and rms_out:
                    t = NT * g + i
                    wait(act, s["z_ready"], t + 1)
                    wait(act, s["sq_done"], t - 1)
                    nc.scalar.activation(square[i % 2][:, :], pz[i % 2][:, :], ACT.Square, accum_out=ssum[i % 2][:, :])\
                        .then_inc(s["sq_done"], 1)

            def step(k, u):
                n = 2 * k + u
                for m in range(MT):
                    q = slot(n, m)
                    for which in range(2):
                        scale_part(n, m, u, which)
                    if not plain:
                        gate_act(n, m, u)
                    elif m:
                        gate_act(n, m - 1, u)
                    if m:
                        hidden_hi(n, m - 1, u)
                    if q is not None:
                        beside.scalar_high(act, q - 3)
                    if m in down_at:
                        squares(n - 1, down_at.index(m))
                    if m in norm_at:
                        x_hi(n + 1, norm_at.index(m), 1 - u)
                    if q is not None:
                        beside.scalar_prepare(act, q)
                if plain:
                    gate_act(n, MT - 1, u)
                hidden_hi(n, MT - 1, u)
            loop_pairs(act, step, FIRST, FROM, TO, LAST)

        @block.vector
        def _(dve):
            dve.memset(minus_half[:, :], -0.5).then_inc(half_set, 1)
            if plain:
                dve.wait_ge(set_up, 1)

            def join_part(g, m, u, which):
                if inside(g, GROUPS) and plain:
                    n = MT * g + m
                    to = joined[which][(m + u) % 2]
                    wait(dve, s["part_ready"], 4 * n + which + 3)
                    wait(dve, s["scale_done"], 2 * n + which + 1)
                    nc.vector.scalar_tensor_tensor(to[:, :], part[which][:, :],
                                                   factor[:, which * MT + m, plain[1]:plain[1] + 1], to[:, :],
                                                   ALU.mult, ALU.add).then_inc(s["join_done"], 1)

            def add_scaled(g, m, u, which):
                if inside(g, GROUPS) and plain:
                    n = MT * g + m
                    to = joined[which][(m + u) % 2]
                    wait(dve, s["gu_ready"], 2 * n + which + 1)
                    wait(dve, s["join_done"], 2 * n + which + 1)
                    nc.vector.tensor_tensor(to[:, :], gu[(m + u) % 2][which][:, :], to[:, :], ALU.add)\
                        .then_inc(s["add_done"], 1)

            def hidden(g, m, u):
                if inside(g, GROUPS):
                    n = MT * g + m
                    r = slice(0, rows[m])
                    wait(dve, s["act_done"], n + 1)
                    wait(dve, s["glo_done"], n - 1)
                    if scales is not None:
                        nc.vector.scalar_tensor_tensor(prod[(m + u) % 2][r, :], gu[(m + u) % 2][1][r, :], scales[r, 1:2],
                                                       act_out[(m + u) % 2][r, :], ALU.mult, ALU.mult)\
                            .then_inc(s["prod_done"], 1)
                    else:
                        if plain:
                            wait(dve, s["add_done"], 2 * n + 2)
                        src = joined[1][(m + u) % 2] if plain else gu[(m + u) % 2][1]
                        nc.vector.tensor_tensor(prod[(m + u) % 2][r, :], src[r, :], act_out[(m + u) % 2][r, :],
                                                ALU.mult).then_inc(s["prod_done"], 1)

            def hidden_lo(g, m, u):
                if inside(g, GROUPS):
                    wait(dve, s["ghi_done"], MT * g + m + 1)
                    r = slice(0, rows[m])
                    nc.vector.tensor_tensor(glo[u][r, m, :], prod[(m + u) % 2][r, :], ghi[u][r, m, :], ALU.subtract)\
                        .then_inc(s["glo_done"], 1)

            def row_stats(g, i, half):
                if inside(g, GROUPS):
                    t, u = NT * g + i, i % 2
                    wait_alone(dve, s["dve_passed"], h_in[u], 16 * (half + 1))
                    nc.vector.bn_stats(stats[u][:, :], hin[u][:, :]).then_inc(s["stats_done"], 1)
                    wait_alone(dve, s["dve_passed"], s["stats_done"], t + 1)
                    nc.vector.bn_aggr(mv[u][:, :], stats[u][:, :]).then_inc(s["mv_done"], 1)
                    wait(dve, s["mv_done"], t + 1)
                    nc.vector.tensor_scalar(veps[u][:, :], mv[u][:, 1:2], EPS, None, ALU.add)\
                        .then_inc(s["veps_done"], 1)

            def x_normalised(g, i):
                if inside(g, GROUPS):
                    t, u = NT * g + i, i % 2
                    wait(dve, s["rstd_done"], t + 1)
                    wait(dve, s["xT_ready"], t)
                    nc.vector.tensor_scalar(xn[:, :], hin[u][:, :], mv[u][:, 0:1], rstd[u][:, :],
                                            ALU.subtract, ALU.mult).then_inc(s["xn_done"], 1)

            def x_lo(g, i, u):
                if inside(g, GROUPS):
                    wait(dve, s["xhi_done"], NT * g + i + 1)
                    nc.vector.tensor_tensor(xlo[u][:, :, i * P:(i + 1) * P], px[:, :].rearrange("p (j n) -> p j n", j=KT),
                                            xhi[u][:, :, i * P:(i + 1) * P], ALU.subtract).then_inc(s["xlo_done"], 1)

            def mean_square(g, i):
                if inside(g, GROUPS) and rms_out:
                    wait(dve, s["sq_done"], NT * g + i + 1)
                    nc.vector.tensor_scalar(ms[i % 2][:, :], ssum[i % 2][:, :], 1.0 / DM, RMS_EPS, ALU.mult, ALU.add)\
                        .then_inc(s["ms_done"], 1)

            def output(g, i, half):
                if inside(g, GROUPS):
                    t, u = NT * g + i, i % 2
                    wait(dve, s["rinv_done" if rms_out else "z_ready"], t + 1)
                    wait(dve, res_in[u], 16 * (half + 1))
                    wait(dve, stored[u], 16 * half)
                    nc.vector.scalar_tensor_tensor(hout[u][:, :], pz[u][:, :],
                                                   rinv[u][:, :] if rms_out else scales[:, 2:3], hres[u][:, :],
                                                   ALU.mult, ALU.add).then_inc(s["out_done"], 1)

            def step(k, u):
                n = 2 * k + u
                for m in range(MT):
                    q = slot(n, m)
                    if m + 1 in norm_at:
                        x_normalised(n + 1, norm_at.index(m + 1))
                    if not plain:
                        hidden(n, m, u)
                    elif m:
                        hidden(n, m - 1, u)
                    for which in range(2):
                        join_part(n, m, u, which)
                    for which in range(2):
                        add_scaled(n, m, u, which)
                    if q is not None:
                        beside.vector_code(dve, q)
                        beside.vector_sign(dve, q)
                    if m in down_at:
                        mean_square(n - 1, down_at.index(m))
                    if m:
                        hidden_lo(n, m - 1, u)
                    if q is not None:
                        beside.vector_join(dve, q - 1)
                    if m - 1 in down_at:
                        i = down_at.index(m - 1)
                        output(n - 1, i, 2 * (n - 1) + i // 2)
                    if m in norm_at:
                        x_lo(n + 1, norm_at.index(m), 1 - u)
                    if m + 3 in norm_at:
                        i = norm_at.index(m + 3)
                        row_stats(n + 1, i, 2 * (n + 1) + i // 2)
                    if q is not None:
                        beside.vector_low(dve, q - 3)
                if plain:
                    hidden(n, MT - 1, u)
                hidden_lo(n, MT - 1, u)
            loop_pairs(dve, step, FIRST, FROM, TO, LAST)

        @block.tensor
        def _(pe):
            pe.wait_ge(c_in, 16)

            def gate_up(g, m, u):
                if inside(g, GROUPS):
                    n = MT * g + m
                    if m == 0:
                        wait(pe, s["xlo_done"], NT * (g + 1))
                    if not plain:
                        wait(pe, s["prod_done"], n - 1)
                    scaled = [j for j in range(KT) if j not in plain]
                    for which, weights in enumerate((gate, up)):
                        if plain:
                            for w in range(2):
                                products_plain(n, m, u, w, which)
                            wait(pe, s["add_done"], 2 * (n - 2) + which + 1)
                        c = 0
                        for j in scaled:
                            for x, w in parts_x:
                                last = nc.tensor.matmul(gu[(m + u) % 2][which][0:rows[m], :],
                                                        weights[w][:, j, m * P:m * P + rows[m]],
                                                        xparts[x][u][:, j, :], start=c == 0,
                                                        stop=c == len(scaled) * len(parts_x) - 1)
                                c += 1
                        if plain or which == 1:
                            last.then_inc(s["gu_ready"], 1)

            def products_plain(n, m, u, which, i):
                if i == 0:
                    wait(pe, s["join_done"], 2 * (n - 1) + which + 1)
                else:
                    wait(pe, s["scale_done"], 2 * n + which + 1)
                for x in range(2):
                    last = nc.tensor.matmul(part[which][:, :], (gate, up)[which][0][:, plain[i], m * P:(m + 1) * P],
                                            xparts[x][u][:, plain[i], :], start=x == 0, stop=x == 1)
                last.then_inc(s["part_ready"], 1)

            def transpose_x(g, i):
                if inside(g, GROUPS):
                    t = NT * g + i
                    wait(pe, s["xn_done"], t + 1)
                    wait(pe, s["xlo_done"], t)
                    for j in range(KT):
                        last = nc.tensor.transpose(px[:, j * P:(j + 1) * P], xn[:, j * P:(j + 1) * P], ident[:, :])
                    last.then_inc(s["xT_ready"], 1)

            def project(g, i, u):
                if inside(g, GROUPS):
                    t = NT * g + i
                    if i == 0:
                        wait(pe, s["glo_done"], MT * (g + 1))
                    wait(pe, s["out_done"], t + 1 - PZ)
                    c = 0
                    for m in range(MT):
                        for x, w in parts_x:
                            last = nc.tensor.matmul(pz[i % 2][:, :], gparts[x][u][0:rows[m], m, i * P:(i + 1) * P],
                                                    down[w][0:rows[m], m, :], start=c == 0,
                                                    stop=c == MT * len(parts_x) - 1)
                            c += 1
                    last.then_inc(s["z_ready"], 1)

            def step(k, u):
                n = 2 * k + u
                for m in range(MT):
                    gate_up(n, m, u)
                    if m in down_at:
                        project(n - 1, down_at.index(m), 1 - u)
                    if m in norm_at:
                        transpose_x(n + 1, norm_at.index(m))
            loop_pairs(pe, step, FIRST, FROM, TO, LAST)
def three_bf16(a):
    parts, rest = [], np.asarray(a, np.float64)
    for _ in range(3):
        part = rest.astype(np.float32).astype(np.dtype("bfloat16"))
        parts.append(part)
        rest = rest - part.astype(np.float64)
    return parts


def constants():
    P, L, B = 128, 32, 4
    q, k = np.arange(L)[:, None], np.arange(L)[None, :]
    out = {"ident": np.eye(P, dtype=np.float32), "ident16": np.eye(P, dtype=np.float16)}
    row = np.arange(96)[:, None] % L
    out["select"] = (row == np.arange(P)[None, :] % L).astype(np.dtype("bfloat16"))
    out["own"] = (np.arange(P)[:, None] // L == np.arange(B)[None, :]).astype(np.float32)
    for pre, kv, d, slope in (("a0_", 8, 16, lambda h: 0.0), ("a1_", 4, 32, lambda h: np.float32(2 ** -0.5 * (2 ** -0.5) ** h))):
        table = np.zeros((96, 2, B, kv // 2, L), np.dtype("bfloat16"))
        for h in range(kv):
            full = np.where(k <= q, float(slope(h)) * (k - q) * float(d) ** 0.5, 0.0)
            for n, part in enumerate(three_bf16(full)):
                part = part.copy()
                if n == 0:
                    part[k + 0 * q > q] = -1e30
                table[n * L:(n + 1) * L, h // (kv // 2), :, h % (kv // 2), :] = part[:, None, :]
        out[pre + "bias"] = table.reshape(96, -1)
    shift = (np.arange(P) % 8 * 4)[:, None]
    out["fp4_masks"] = (np.array([[7, 8]], np.uint32) << shift.astype(np.uint32)).astype(np.uint32).view(np.int32)
    to_minus_two = np.where(shift == 28, 2.0, -2.0) / 8
    out["fp4_factors"] = (np.concatenate([0.5 + 0.0 * shift, 1.0 + 0.0 * shift, to_minus_two], axis=1)
                          * 2.0 ** -shift).astype(np.float32)
    out["fp4_biases"] = np.tile(np.array([[-2.0, -6.0]], np.float32), (P, 1))
    inv = (np.float32(1.0) / np.power(np.float32(10000.0), np.arange(0, 16, 2, dtype=np.float32) / np.float32(16))).astype(np.float32)
    angle = np.outer(np.arange(L, dtype=np.float32), inv).astype(np.float32)
    angle = np.tile(angle, (B, 1))
    out["cos"] = np.repeat(np.cos(angle), 2, axis=1).astype(np.float32)
    out["sin"] = np.stack([-np.sin(angle), np.sin(angle)], axis=1).astype(np.float32)
    return out


_X = "x"
_OUT = (128, 32, 512)
PLAIN = (2, 3)


def load_gate_scales(sp, scales, target, arrived, i):
    if i == 0:
        sp.dma_start(target[:, :, :], scales.rearrange("(t p) j -> p t j", p=128)).then_inc(arrived, 16)


def audio_tower(nc, x, weights, const, out):
    P, TOKENS, DM = 128, 4096, 512
    h = [nc.dram_tensor(f"h{i}", (TOKENS, DM), F32, kind="Internal").ap() for i in range(4)]
    y = out.rearrange("b s d -> (b s) d")
    token_mixer(nc, x, const["ident"], h[0])
    with ExitStack() as outer:
        sources = [weights[n] for n in ("w1", "w3", "w2")]
        tern = [outer.enter_context(nc.sbuf_tensor(f"tern{i}", [P, (w.shape[0] + P - 1) // P, w.shape[1]], F16))
                for i, w in enumerate(sources)]
        scales = outer.enter_context(nc.sbuf_tensor("tern_scales", [P, 3], F32))
        with ExitStack() as ctx:
            stage = [ctx.enter_context(nc.sbuf_tensor(f"tern_stage{i}", [P, t.shape[1] * t.shape[2]], F32))
                     for i, t in enumerate(tern)]
            sem = semaphores(nc, ctx, "tern_")
            arrived = [sem(f"arrived{i}") for i in range(3)]
            attention(nc, "a0_", h[0], h[1], weights["qkv0"], weights["o0"], const, 8, 16, True,
                      prefetch=lambda sp, i: load_ternary(sp, sources[i], stage[i], arrived[i]))
            ternary_weights(nc, sources, stage, arrived, tern, scales, [w.shape[0] * w.shape[1] for w in sources])
        HID = weights["gu"].shape[1] // 2
        gu = [outer.enter_context(nc.sbuf_tensor(f"gu{i}", [P, DM // P, 2 * HID], F16)) for i in range(2)]
        gate_scales = outer.enter_context(nc.sbuf_tensor("gate_scales", [P, 2 * HID // P, DM // P], F16))
        dn = [outer.enter_context(nc.sbuf_tensor(f"dn{i}", [P, HID // P, DM], F16)) for i in range(2)]
        with ExitStack() as ctx:
            fp4 = Fp4Weights(nc, ctx, (weights["gu"], weights["dn"]), (weights["gu_scales"], weights["dn_scales"]),
                             (gu, dn), const, PLAIN)
            feed_forward(nc, "f0_", h[1], h[2], [tern[0]], [tern[1]], [tern[2]], scales, const,
                         sources[0].shape[1], False, beside=fp4)
        sem = semaphores(nc, outer, "scales_")
        scales_in = sem("in")
        attention(nc, "a1_", h[2], h[3], weights["qkv1"], weights["o1"], const, 4, 32, False,
                  prefetch=lambda sp, i: load_gate_scales(sp, weights["gu_scales_t"], gate_scales, scales_in, i))
        feed_forward(nc, "f1_", h[3], y, [w[:, :, 0:HID] for w in gu], [w[:, :, HID:] for w in gu], dn, None,
                     const, HID, True, plain=PLAIN, plain_scales=gate_scales,
                     plain_in=scales_in)


def kernel(**inputs):
    import concourse.bacc as bacc
    from concourse.bass_utils import run_bass_kernel_spmd

    a = {k: np.asarray(v) for k, v in inputs.items()}

    def rows_by_repeat(w, heads, d):
        return w.reshape(heads, 4, d, 512).transpose(1, 0, 2, 3).reshape(512, 512)

    layouts = {
        "qkv0": np.concatenate([a["L0_attn_wq"], a["L0_attn_wk"], a["L0_attn_wv"]], axis=0).T,
        "o0": rows_by_repeat(a["L0_attn_wo"].T, 8, 16),
        "w1": a["L0_ffn_w1"].T, "w3": a["L0_ffn_w3"].T, "w2": a["L0_ffn_w2"].T,
        "qkv1": np.concatenate([a["L1_attn_Wq"], a["L1_attn_Wk"], a["L1_attn_Wv"]], axis=1),
        "o1": rows_by_repeat(a["L1_attn_Wo"], 4, 32),
        "gu": a["L1_ffn_gate_up_packed"].T, "gu_scales": a["L1_ffn_gate_up_scales"],
        "gu_scales_t": a["L1_ffn_gate_up_scales"].T,
        "dn": a["L1_ffn_down_packed"].T, "dn_scales": a["L1_ffn_down_scales"],
    }
    tables = constants()
    nc = bacc.Bacc("TRN2", target_bir_lowering=False, num_devices=1)
    arrays = {"in_x": np.ascontiguousarray(a["x"])}
    arrays.update({f"in_{k}": np.ascontiguousarray(v) for k, v in layouts.items()})
    arrays.update({f"const_{k}": np.ascontiguousarray(v) for k, v in tables.items()})
    aps = {k: nc.dram_tensor(k, v.shape, mybir.dt.from_np(v.dtype), kind="ExternalInput").ap()
           for k, v in arrays.items()}
    out = nc.dram_tensor("out", _OUT, F32, kind="ExternalOutput").ap()
    audio_tower(nc, aps["in_x"], {k: aps[f"in_{k}"] for k in layouts}, {k: aps[f"const_{k}"] for k in tables}, out)
    r = run_bass_kernel_spmd(nc, [arrays], core_ids=[0])
    return r.results[0]["out"]
```
